# Optimizing a Trainium2 kernel written in Bass

```python
import numpy as np
import jax
import jax.numpy as jnp

def _softmax(x, axis=-1):
    return jax.nn.softmax(x, axis=axis)

def _gelu(x):
    return jax.nn.gelu(x, approximate=True)

def _silu(x):
    return jax.nn.silu(x)

def _sigmoid(x):
    return jax.nn.sigmoid(x)

def _layernorm(x, axis=-1, eps=1e-05):
    m = jnp.mean(x, axis=axis, keepdims=True)
    v = jnp.var(x, axis=axis, keepdims=True)
    return (x - m) / jnp.sqrt(v + eps)

def _scatter_add(tgt, idx, src, axis=0):
    return tgt.at[idx].add(src)

def _segment_sum(src, seg, n):
    return jax.ops.segment_sum(src, seg, n)
kernel_name = 'mk_gnn_preln_d2_gnn_r8_749532'

def setup_inputs(seed: int=0):
    np.random.seed(seed)
    _w = jnp.asarray

    def _rec_inputs():
        import jax
        import jax.numpy as jnp
        _gk = jax.random.key(seed)
        x = -0.0006008 + 1.001 * jax.random.normal(jax.random.fold_in(_gk, 1), (6250, 128), jnp.float32)
        _s = jax.random.randint(jax.random.fold_in(_gk, 2), (100000,), 0, 6250, jnp.int32)
        _d = jax.random.randint(jax.random.fold_in(_gk, 3), (100000,), 0, 6250, jnp.int32)
        _loop = jnp.arange(6250, dtype=jnp.int32)
        src = jnp.concatenate([_s, _d, _loop])
        dst = jnp.concatenate([_d, _s, _loop])
        _o = jnp.argsort(dst, stable=True)
        src = src[_o]
        dst = dst[_o]
        edge_attr_128 = -0.000128692 + 0.999872 * jax.random.normal(jax.random.fold_in(_gk, 11), (206250, 128), jnp.float32)
        edge_type_4 = jax.random.randint(jax.random.fold_in(_gk, 13), (206250,), 0, 4, jnp.int32)
        return (x, src, dst, edge_attr_128, edge_type_4)
    x, src, dst, edge_attr_128, edge_type_4 = _rec_inputs()

    def _L0_gnn_setup():
        import jax, jax.numpy as jnp
        import numpy as np
        N = 2500
        DEG = 16
        E = N * DEG
        DIM = 128
        H = 8
        HD = DIM // H
        HE = 8
        SCALE = HD ** (-0.5)
        key = jax.random.key(seed)
        ks = jax.random.split(key, 10)
        s = 0.05
        x = jax.random.normal(ks[0], (N, DIM), jnp.float32)
        edges = jax.random.normal(ks[1], (E, DIM), jnp.float32)
        src = jnp.repeat(jnp.arange(N, dtype=jnp.int32), DEG)
        off = jnp.tile(jnp.arange(1, DEG + 1, dtype=jnp.int32), N)
        dst = (src + off) % N
        edge_index = jnp.stack([src, dst], axis=0)
        Wq = jax.random.normal(ks[2], (DIM, DIM), jnp.float32) * s
        Wk = jax.random.normal(ks[3], (DIM, DIM), jnp.float32) * s
        Wv = jax.random.normal(ks[4], (DIM, HE * HD), jnp.float32) * s
        Wek = jax.random.normal(ks[5], (DIM, DIM), jnp.float32) * s
        Wev = jax.random.normal(ks[6], (DIM, HE * HD), jnp.float32) * s
        Wexp = jax.random.normal(ks[7], (H, HE), jnp.float32) * s
        Wout = jax.random.normal(ks[8], (HE * HD, DIM), jnp.float32) * s
        bout = jnp.zeros((DIM,), jnp.float32)
        return {'x': x, 'edges': edges, 'edge_index': edge_index, 'Wq': Wq, 'Wk': Wk, 'Wv': Wv, 'Wek': Wek, 'Wev': Wev, 'Wexp': Wexp, 'Wout': Wout, 'bout': bout}
    _L0_gnn_all = _L0_gnn_setup()
    _L0_gnn_in = {k: v for k, v in _L0_gnn_all.items() if k in ('Wq', 'Wk', 'Wv', 'Wek', 'Wev', 'Wexp', 'Wout', 'bout')}
    del _L0_gnn_all

    def _L1_gnn_setup():
        import jax, jax.numpy as jnp
        import numpy as np
        N_NODES = 12500
        N_EDGES = 75000
        N_REL = 4
        N_HEADS = 4
        DIM = 128
        HEAD_DIM = DIM // N_HEADS
        NEG_SLOPE = 0.2
        key = jax.random.key(seed)
        k1, k2, k3, k4, k5 = jax.random.split(key, 5)
        x = jax.random.normal(k1, (N_NODES, DIM), dtype=jnp.float32)
        edge_index = jax.random.randint(k2, (2, N_EDGES), 0, N_NODES, dtype=jnp.int64)
        edge_types = jax.random.randint(k3, (N_EDGES,), 0, N_REL, dtype=jnp.int64)
        W = jax.random.normal(k4, (N_REL, DIM, DIM), dtype=jnp.float32) * (1.0 / np.sqrt(DIM))
        attn = jax.random.normal(k5, (N_REL, N_HEADS, 2 * HEAD_DIM), dtype=jnp.float32) * 0.1
        return {'x': x, 'edge_index': edge_index, 'edge_types': edge_types, 'W': W, 'attn': attn}
    _L1_gnn_all = _L1_gnn_setup()
    _L1_gnn_in = {k: v for k, v in _L1_gnn_all.items() if k in ('W', 'attn')}
    del _L1_gnn_all
    return {'x': x, 'src': src, 'dst': dst, 'edge_attr_128': edge_attr_128, 'edge_type_4': edge_type_4, 'L0_gnn_Wq': _L0_gnn_in['Wq'], 'L0_gnn_Wk': _L0_gnn_in['Wk'], 'L0_gnn_Wv': _L0_gnn_in['Wv'], 'L0_gnn_Wek': _L0_gnn_in['Wek'], 'L0_gnn_Wev': _L0_gnn_in['Wev'], 'L0_gnn_Wexp': _L0_gnn_in['Wexp'], 'L0_gnn_Wout': _L0_gnn_in['Wout'], 'L0_gnn_bout': _L0_gnn_in['bout'], 'L1_gnn_W': _L1_gnn_in['W'], 'L1_gnn_attn': _L1_gnn_in['attn']}

def reference(x, src, dst, edge_attr_128, edge_type_4, L0_gnn_Wq, L0_gnn_Wk, L0_gnn_Wv, L0_gnn_Wek, L0_gnn_Wev, L0_gnn_Wexp, L0_gnn_Wout, L0_gnn_bout, L1_gnn_W, L1_gnn_attn):
    import jax
    import jax.numpy as jnp

    def _L0_gnn_ref(x, edges, edge_index, Wq, Wk, Wv, Wek, Wev, Wexp, Wout, bout):
        import jax, jax.numpy as jnp
        import numpy as np
        N = 2500
        DEG = 16
        E = N * DEG
        DIM = 128
        H = 8
        HD = DIM // H
        HE = 8
        SCALE = HD ** (-0.5)
        n = x.shape[0]
        src, dst = (edge_index[0], edge_index[1])
        qg = (x @ Wq)[src].reshape(-1, H, HD)
        kg = ((x @ Wk)[dst] * SCALE + edges @ Wek * SCALE).reshape(-1, H, HD)
        scores = jnp.einsum('ehd,ehd->eh', qg, kg)
        scores = scores @ Wexp
        seg_max = jax.ops.segment_max(scores, src, num_segments=n)
        exps = jnp.exp(scores - seg_max[src])
        denom = jax.ops.segment_sum(exps, src, num_segments=n)
        a = exps / denom[src]
        v_e = ((x @ Wv)[dst] + edges @ Wev).reshape(-1, HE, HD)
        agg = jax.ops.segment_sum(a[:, :, None] * v_e, src, num_segments=n)
        self_m = (src == dst).astype(x.dtype)
        self_c = jax.ops.segment_sum(v_e * self_m[:, None, None], src, num_segments=n)
        out = (self_c - agg).reshape(n, HE * HD)
        return out @ Wout + bout

    def _L1_gnn_ref(x, edge_index, edge_types, W, attn):
        import jax, jax.numpy as jnp
        import numpy as np
        N_NODES = 12500
        N_EDGES = 75000
        N_REL = 4
        N_HEADS = 4
        DIM = 128
        HEAD_DIM = DIM // N_HEADS
        NEG_SLOPE = 0.2
        N = x.shape[0]
        R, H, twoD = attn.shape
        D = twoD // 2
        E = edge_types.shape[0]
        x_rel = jnp.einsum('ni,rio->rno', x, W).reshape(R, N, H, D)
        src, dst = (edge_index[0], edge_index[1])
        src_feat = x_rel[edge_types, src]
        dst_feat = x_rel[edge_types, dst]
        a = attn[edge_types]
        cat = jnp.concatenate([src_feat, dst_feat], axis=-1)
        alpha = jnp.sum(cat * a, axis=-1)
        alpha = jnp.where(alpha > 0, alpha, NEG_SLOPE * alpha)
        seg = edge_types * N + dst
        S = R * N
        m = jax.ops.segment_max(alpha, seg, num_segments=S)
        alpha_exp = jnp.exp(alpha - m[seg])
        denom = jax.ops.segment_sum(alpha_exp, seg, num_segments=S)
        w = alpha_exp / denom[seg]
        msg = (src_feat * w[..., None]).reshape(E, H * D)
        out = jax.ops.segment_sum(msg, dst, num_segments=N)
        return out
    edge_index = jnp.stack([src, dst])
    h = jnp.maximum(_layernorm(x, axis=-1), 0.0)
    x = x + _L0_gnn_ref(h, edge_attr_128, edge_index, L0_gnn_Wq, L0_gnn_Wk, L0_gnn_Wv, L0_gnn_Wek, L0_gnn_Wev, L0_gnn_Wexp, L0_gnn_Wout, L0_gnn_bout)
    h = jnp.maximum(_layernorm(x, axis=-1), 0.0)
    x = x + _L1_gnn_ref(h, edge_index, edge_type_4, L1_gnn_W, L1_gnn_attn)
    return x

_drawn_inputs = setup_inputs


def setup_inputs(seed=0):
    import zlib

    import numpy as np

    out = dict(_drawn_inputs(seed))
    spreads = {'L0_gnn_bout': (0.0, 0.1)}
    factors = {'L0_gnn_Wq': 8.0, 'L0_gnn_Wk': 8.0, 'L0_gnn_Wek': 8.0, 'L0_gnn_Wexp': 8.0}
    for name, (base, spread) in spreads.items():
        noise = np.random.default_rng([zlib.crc32(name.encode()), seed]).standard_normal(out[name].shape)
        drawn = base * np.exp(spread * noise) if base else spread * noise
        out[name] = jnp.asarray(drawn.astype(out[name].dtype))
    for name, factor in factors.items():
        out[name] = (out[name] * factor).astype(out[name].dtype)
    return out
```

```python
from contextlib import ExitStack

import concourse.bass as bass
from concourse import mybir

F32 = mybir.dt.float32
BF16 = mybir.dt.bfloat16
I32 = mybir.dt.int32
ALU = mybir.AluOpType
ACT = mybir.ActivationFunctionType
AX_X = mybir.AxisListType.X

P = 128
SLOTS = 3
TILES = 4
GROUP = TILES * P
LOW = -3.0e38
NOWHERE = 4.0e6

SRC1, LO1, DST, HI2, KEY1, DLO1, TYPE, SEG2 = range(8)
TAGS = 8


def pipelined(engine, count, stages):
    depth = len(stages) - 1
    first = SLOTS if depth == 0 else 2 * SLOTS
    rounds = (count - first - 1) // SLOTS

    def written_out(t):
        for s, stage in enumerate(stages):
            if 0 <= t - s < count:
                stage(t - s, (t - s) % SLOTS, (t - s) // SLOTS)

    for t in range(first):
        written_out(t)
    with engine.Fori(0, rounds) as k:
        for u in range(SLOTS):
            for s, stage in enumerate(stages):
                at = first + u - s
                stage(k * SLOTS + at, at % SLOTS, k + at // SLOTS)
    for t in range(first + rounds * SLOTS, count + depth):
        written_out(t)


def wait(engine, semaphore, value):
    if isinstance(value, int) and value <= 0:
        return
    engine.wait_ge(semaphore, value)


def gnn_kernel(nc, x, src, dst, edge_attr, edge_type, Wq, Wk, Wv, Wek, Wev, Wexp, Wout, bout, W_rel, attn, out):
    N, D = x.shape
    E = src.shape[0]
    H0, HE = Wexp.shape
    R, H1, two_hd = attn.shape
    HD1 = two_hd // 2
    SCALE = float(D // H0) ** -0.5
    EPS = 1e-5
    SLOPE = 0.2
    WINDOWS = -(-N // P)
    LAST = N - (WINDOWS - 1) * P
    COLS = -(-E // (P * TILES)) * TILES
    TAIL = E - (P - 1) * COLS
    IN_GROUPS = COLS // TILES
    FULL = TAIL // TILES
    GROUPS = (E + WINDOWS * (GROUP - 1)) // GROUP
    NPOS = GROUPS * GROUP
    RUN = NPOS // P
    KV = 2 * D
    PAY = D + TAGS
    SROW = HE + TAGS
    FEAT = D + H1
    YROW = FEAT + 4
    ZROW = H1 + 4
    KEYS2 = WINDOWS * R
    assert HE == 8 and R == 4 and H1 == 4 and D == P and YROW == PAY

    kv_table = nc.dram_tensor("kv_table", [WINDOWS * P, KV], F32).ap()
    by_src = nc.dram_tensor("by_src", [NPOS, PAY], F32).ap()
    values = nc.dram_tensor("values", [NPOS, D], F32).ap()
    scores = nc.dram_tensor("scores", [NPOS, SROW], F32).ap()
    by_dst = nc.dram_tensor("by_dst", [NPOS, YROW], F32).ap()
    alphas = nc.dram_tensor("alphas", [NPOS, ZROW], F32).ap()

    names = [0]

    def sb(stack, shape, dtype=F32):
        names[0] += 1
        return stack.enter_context(nc.sbuf_tensor(f"sb{names[0]}", list(shape), dtype))

    def ps(stack, shape, dtype=F32):
        names[0] += 1
        return stack.enter_context(nc.psum_tensor(f"ps{names[0]}", list(shape), dtype))

    spent = []

    def sem(name):
        names[0] += 1
        spent.append(nc.alloc_semaphore(f"{name}_{names[0]}"))
        return spent[-1]

    def fresh_semaphores():
        nc.clear_and_free_semaphores(list(spent))
        nc.all_engine_barrier()
        spent.clear()

    def gpsimd_dma_sem(name):
        names[0] += 1
        return nc.alloc_semaphore(f"{name}_{names[0]}")

    whole = ExitStack()
    x_sb = sb(whole, [P, WINDOWS, D])
    ident = sb(whole, [P, P])
    ident_bf = sb(whole, [P, P], BF16)
    ones = sb(whole, [P, P])
    before = sb(whole, [P, P])
    after = sb(whole, [P, P])
    count1 = sb(whole, [P, P])
    count1_bf = sb(whole, [P, KEYS2], BF16)
    count0 = sb(whole, [P, R])
    row1 = sb(whole, [P, R])
    base1 = sb(whole, [P, WINDOWS])
    base2 = sb(whole, [P, KEYS2])
    window1 = sb(whole, [1, GROUPS], I32)
    window2 = sb(whole, [1, GROUPS], I32)

    with ExitStack() as st:
        cleared = sem("cleared")
        loaded = sem("loaded")
        made = sem("made")
        with nc.Block() as block:

            @block.vector
            def _(dve):
                nc.vector.memset(x_sb[:, :, :], 0.0).then_inc(cleared, 1)
                nc.vector.memset(ones[:, :], 1.0)

            @block.sync
            def _(sp):
                sp.wait_ge(cleared, 1)
                sp.dma_start(x_sb[:, 0:WINDOWS - 1, :],
                             x[0:(WINDOWS - 1) * P, :].rearrange("(w p) d -> p w d", p=P)).then_inc(loaded, 16)
                sp.dma_start(x_sb[0:LAST, WINDOWS - 1, :], x[(WINDOWS - 1) * P:N, :]).then_inc(loaded, 16)
                sp.wait_ge(loaded, 32)

            @block.gpsimd
            def _(pool):
                for t in (ident, ident_bf, before, after):
                    pool.memset(t[:, :], 0.0).then_inc(made, 1)
                pool.wait_ge(made, 4)
                for t in (ident, ident_bf):
                    pool.affine_select(out=t[:, :], in_=t[:, :], compare_op=ALU.not_equal, fill=1.0, base=0,
                                       pattern=[[-1, P]], channel_multiplier=1)
                pool.affine_select(out=before[:, :], in_=before[:, :], compare_op=ALU.is_ge, fill=1.0, base=0,
                                   pattern=[[-1, P]], channel_multiplier=1)
                pool.affine_select(out=after[:, :], in_=after[:, :], compare_op=ALU.is_ge, fill=1.0, base=0,
                                   pattern=[[1, P]], channel_multiplier=-1)
                for t, pattern, base, step in ((count1, [[1, P]], 1, 0), (count1_bf, [[1, KEYS2]], 1, 0),
                                               (count0, [[1, R]], 0, 0), (row1, [[P, R]], 1, 1)):
                    pool.iota(t[:, :], pattern=pattern, base=base, channel_multiplier=step,
                              allow_small_or_imprecise_dtypes=True)

    tables0 = ExitStack()
    q_sb = sb(tables0, [P, WINDOWS, D])
    edges = ExitStack()
    tags = sb(edges, [P, COLS, TAGS])
    lo1 = sb(edges, [P, COLS], BF16)
    hi1 = sb(edges, [P, COLS], BF16)
    lo2 = sb(edges, [P, COLS], BF16)
    hi2 = sb(edges, [P, COLS], BF16)

    with ExitStack() as st:
        ids = [sb(st, [P, COLS], I32) for _ in range(3)]
        part = sb(st, [P, COLS], I32)
        scratch = sb(st, [P, COLS])
        cleared = sem("cleared")
        loaded = sem("loaded")
        step = sem("step")
        with nc.Block() as block:

            @block.gpsimd
            def _(pool):
                for t in ids:
                    pool.memset(t[:, :], -1).then_inc(cleared, 1)

            @block.sync
            def _(sp):
                sp.wait_ge(cleared, 3)
                for t, given in zip(ids, (src, dst, edge_type)):
                    sp.dma_start(t[0:P - 1, :],
                                 given[0:(P - 1) * COLS].rearrange("(p c) -> p c", p=P - 1)).then_inc(loaded, 16)
                    sp.dma_start(t[P - 1:P, 0:TAIL],
                                 given[(P - 1) * COLS:E].rearrange("(p c) -> p c", p=1)).then_inc(loaded, 16)

            @block.vector
            def _(dve):
                done = [0]

                def then(instruction):
                    done[0] += 1
                    instruction.then_inc(step, 1)
                    dve.wait_ge(step, done[0])

                s, d, t = (i[:, :] for i in ids)
                v = nc.vector

                def col(c):
                    return tags[:, :, c]

                dve.wait_ge(loaded, 6 * 16)
                v.tensor_scalar(col(SRC1), s, 1.0, None, ALU.add)
                v.tensor_copy(col(DST), d)
                v.tensor_copy(col(TYPE), t)
                then(v.tensor_scalar(part[:, :], s, P - 1, None, ALU.bitwise_and))
                v.tensor_scalar(lo1[:, :], part[:, :], 1.0, None, ALU.add)
                then(v.tensor_scalar(col(LO1), part[:, :], 1.0, None, ALU.add))
                then(v.tensor_scalar(part[:, :], s, 7, None, ALU.arith_shift_right))
                then(v.tensor_scalar(hi1[:, :], part[:, :], 1.0, None, ALU.add))
                v.scalar_tensor_tensor(col(KEY1), col(TYPE), float(P), col(LO1), ALU.mult, ALU.add)
                then(v.tensor_scalar(part[:, :], d, P - 1, None, ALU.bitwise_and))
                v.tensor_scalar(lo2[:, :], part[:, :], 1.0, None, ALU.add)
                then(v.tensor_scalar(col(DLO1), part[:, :], 1.0, None, ALU.add))
                then(v.tensor_scalar(part[:, :], d, 7, None, ALU.arith_shift_right))
                then(v.tensor_scalar(scratch[:, :], part[:, :], float(R), 1.0, ALU.mult, ALU.add))
                v.tensor_tensor(hi2[:, :], scratch[:, :], col(TYPE), ALU.add)
                then(v.tensor_tensor(col(HI2), scratch[:, :], col(TYPE), ALU.add))
                then(v.tensor_scalar(scratch[:, :], d, float(R), 1.0, ALU.mult, ALU.add))
                then(v.tensor_tensor(col(SEG2), scratch[:, :], col(TYPE), ALU.add))

    def layernorm_relu_input(hn):
        with ExitStack() as st:
            square = sb(st, [P, WINDOWS, D])
            stat = sb(st, [P, WINDOWS])
            spread = sb(st, [P, WINDOWS])
            eps = sb(st, [P, 1])
            step = sem("step")
            summed = sem("summed")
            rooted = sem("rooted")
            over = stat[:, :].unsqueeze(2).to_broadcast([P, WINDOWS, D])
            with nc.Block() as block:

                @block.vector
                def _(dve):
                    done = [0]

                    def then(instruction):
                        done[0] += 1
                        instruction.then_inc(step, 1)
                        dve.wait_ge(step, done[0])

                    v = nc.vector
                    v.memset(eps[:, :], EPS)
                    then(v.tensor_reduce(stat[:, :], x_sb[:, :, :], AX_X, ALU.add))
                    then(v.tensor_scalar(stat[:, :], stat[:, :], 1.0 / D, None, ALU.mult))
                    then(v.tensor_tensor(hn[:, :, :], x_sb[:, :, :], over, ALU.subtract))
                    then(v.tensor_tensor(square[:, :, :], hn[:, :, :], hn[:, :, :], ALU.mult))
                    v.tensor_reduce(spread[:, :], square[:, :, :], AX_X, ALU.add).then_inc(summed, 1)
                    dve.wait_ge(rooted, 1)
                    then(v.reciprocal(stat[:, :], spread[:, :]))
                    v.tensor_tensor(hn[:, :, :], hn[:, :, :], over, ALU.mult)

                @block.scalar
                def _(act):
                    act.wait_ge(summed, 1)
                    nc.scalar.activation(spread[:, :], spread[:, :], ACT.Sqrt, bias=eps[:, 0:1],
                                         scale=1.0 / D).then_inc(rooted, 1)

    with ExitStack() as st:
        hn = sb(st, [P, WINDOWS, D])
        layernorm_relu_input(hn)
        w_qkv = sb(st, [P, 3, D])
        h = sb(st, [P, SLOTS, D])
        h_t = sb(st, [P, SLOTS, P])
        kv = sb(st, [P, SLOTS, KV])
        ps_t = [ps(st, [P, 512]) for _ in range(SLOTS)]
        ps_qkv = [ps(st, [P, 512]) for _ in range(SLOTS)]
        weights = sem("weights")
        relu_done = sem("relu_done")
        turned = sem("turned")
        turned_copied = sem("turned_copied")
        projected = sem("projected")
        taken = sem("taken")
        stored = [sem(f"stored{s}") for s in range(SLOTS)]
        with nc.Block() as block:

            @block.sync
            def _(sp):
                for n, w in enumerate((Wq, Wk, Wv)):
                    sp.dma_start(w_qkv[:, n, :], w).then_inc(weights, 16)

                def store(i, slot, turn):
                    sp.wait_ge(taken, i + 1)
                    sp.dma_start(kv_table[bass.ds(i * P, P), :], kv[:, slot, :]).then_inc(stored[slot], 16)

                pipelined(sp, WINDOWS, [store])
                for s in range(SLOTS):
                    sp.wait_ge(stored[s], 16 * len(range(s, WINDOWS, SLOTS)))

            @block.scalar
            def _(act):
                def rectify(i, slot, turn):
                    wait(act, turned, i - SLOTS + 1)
                    nc.scalar.activation(h[:, slot, :], hn[:, bass.ds(i, 1), :].rearrange("p a d -> p (a d)"),
                                         ACT.Relu).then_inc(relu_done, 1)

                def copy_turned(i, slot, turn):
                    act.wait_ge(turned, i + 1)
                    wait(act, projected, i - SLOTS + 1)
                    nc.scalar.activation(h_t[:, slot, :], ps_t[slot][:, 0:P], ACT.Copy).then_inc(turned_copied, 1)

                pipelined(act, WINDOWS, [rectify, copy_turned])

            @block.tensor
            def _(pe):
                pe.wait_ge(weights, 3 * 16)

                def turn_h(i, slot, turn):
                    pe.wait_ge(relu_done, i + 1)
                    wait(pe, turned_copied, i - SLOTS + 1)
                    nc.tensor.transpose(ps_t[slot][:, 0:P], h[:, slot, :], ident[:, :]).then_inc(turned, 1)

                def project(i, slot, turn):
                    pe.wait_ge(turned_copied, i + 1)
                    wait(pe, taken, i - SLOTS + 1)
                    nc.tensor.matmul(ps_qkv[slot][:, 0:3 * D], h_t[:, slot, :],
                                     w_qkv[:, :, :].rearrange("p a d -> p (a d)"), start=True,
                                     stop=True).then_inc(projected, 1)

                pipelined(pe, WINDOWS, [turn_h, project])

            @block.vector
            def _(dve):
                def take(i, slot, turn):
                    dve.wait_ge(projected, i + 1)
                    wait(dve, stored[slot], 16 * turn)
                    nc.vector.tensor_copy(q_sb[:, bass.ds(i, 1), :].rearrange("p a d -> p (a d)"),
                                          ps_qkv[slot][:, 0:D])
                    nc.vector.tensor_copy(kv[:, slot, :], ps_qkv[slot][:, D:3 * D]).then_inc(taken, 1)

                pipelined(dve, WINDOWS, [take])

    counts = ExitStack()
    count_src = sb(counts, [P, WINDOWS])
    count_dst = sb(counts, [P, KEYS2])
    with ExitStack() as st:
        ZEROS = 7216
        pieces = NPOS * PAY // (P * ZEROS)
        assert pieces * P * ZEROS == NPOS * PAY
        zeros = sb(st, [P, ZEROS])
        hot = [sb(st, [P, SLOTS, TILES, P], BF16) for _ in range(2)]
        hot_hi = [sb(st, [P, SLOTS, TILES, n], BF16) for n in (WINDOWS, KEYS2)]
        ps_count = [ps(st, [P, n]) for n in (WINDOWS, KEYS2)]
        zeroed = sem("zeroed")
        cleared = sem("cleared")
        hot_ready = sem("hot_ready")
        counted = sem("counted")
        with nc.Block() as block:

            @block.sync
            def _(sp):
                sp.wait_ge(zeroed, 1)
                for buffer in (by_src, by_dst):
                    flat = buffer.rearrange("a b -> (a b)").rearrange("(n p c) -> n p c", p=P, c=ZEROS)
                    for n in range(pieces):
                        sp.dma_start(flat[n, :, :], zeros[:, :]).then_inc(cleared, 16)
                sp.wait_ge(cleared, 2 * pieces * 16)

            @block.gpsimd
            def _(pool):
                pool.memset(zeros[:, :], 0.0).then_inc(zeroed, 1)

            @block.vector
            def _(dve):
                def one_hots(i, slot, turn):
                    wait(dve, counted, i - SLOTS + 1)
                    for n, (lo, hi, width) in enumerate(((lo1, hi1, WINDOWS), (lo2, hi2, KEYS2))):
                        nc.vector.tensor_tensor(
                            hot[n][:, slot, :, :],
                            lo[:, bass.ds(i * TILES, TILES)].unsqueeze(2).to_broadcast([P, TILES, P]),
                            count1_bf[:, 0:P].unsqueeze(1).to_broadcast([P, TILES, P]), ALU.is_equal)
                        last = nc.vector.tensor_tensor(
                            hot_hi[n][:, slot, :, :],
                            hi[:, bass.ds(i * TILES, TILES)].unsqueeze(2).to_broadcast([P, TILES, width]),
                            count1_bf[:, 0:width].unsqueeze(1).to_broadcast([P, TILES, width]), ALU.is_equal)
                    last.then_inc(hot_ready, 1)

                pipelined(dve, IN_GROUPS, [one_hots])
                dve.wait_ge(counted, IN_GROUPS)
                nc.vector.tensor_copy(count_src[:, :], ps_count[0][:, :])
                nc.vector.tensor_copy(count_dst[:, :], ps_count[1][:, :])

            @block.tensor
            def _(pe):
                def count(i, slot, turn):
                    pe.wait_ge(hot_ready, i + 1)
                    for n in range(2):
                        for j in range(TILES):
                            first = isinstance(i, int) and i == 0 and j == 0
                            final = isinstance(i, int) and i == IN_GROUPS - 1 and j == TILES - 1
                            last = nc.tensor.matmul(ps_count[n][:, :], hot[n][:, slot, j, :],
                                                    hot_hi[n][:, slot, j, :], start=first, stop=final)
                    last.then_inc(counted, 1)

                pipelined(pe, IN_GROUPS, [count])

    with ExitStack() as st:
        total = sb(st, [P, KEYS2])
        column = sb(st, [P, KEYS2])
        edges_of = sb(st, [P, WINDOWS])
        whole_groups = sb(st, [P, WINDOWS], I32)
        groups_of = sb(st, [P, WINDOWS])
        groups_upto = sb(st, [P, WINDOWS])
        zero_w = sb(st, [P, WINDOWS])
        group_no = sb(st, [1, GROUPS])
        window_f = [sb(st, [1, GROUPS]) for _ in range(2)]
        ps_total = ps(st, [P, 512])
        ps_before = ps(st, [P, 512])
        numbered = sem("numbered")
        summed = sem("summed")
        used = sem("used")
        step = sem("step")
        sorts = ((count_src, WINDOWS, 1, base1, window1), (count_dst, KEYS2, R, base2, window2))
        with nc.Block() as block:

            @block.gpsimd
            def _(pool):
                pool.iota(group_no[:, :], pattern=[[1, GROUPS]], base=0, channel_multiplier=0,
                          allow_small_or_imprecise_dtypes=True).then_inc(numbered, 1)

            @block.tensor
            def _(pe):
                for n, (count, keys, _, _, _) in enumerate(sorts):
                    wait(pe, used, n)
                    nc.tensor.matmul(ps_total[:, 0:keys], ones[:, :], count[:, :], start=True, stop=True)
                    nc.tensor.matmul(ps_before[:, 0:keys], before[:, :], count[:, :], start=True,
                                     stop=True).then_inc(summed, 1)

            @block.vector
            def _(dve):
                done = [0]

                def then(instruction):
                    done[0] += 1
                    instruction.then_inc(step, 1)
                    dve.wait_ge(step, done[0])

                v = nc.vector
                dve.wait_ge(numbered, 1)
                v.memset(zero_w[:, :], 0.0)
                for n, (_, keys, per, base, window) in enumerate(sorts):
                    dve.wait_ge(summed, n + 1)
                    then(v.tensor_copy(total[:, 0:keys], ps_total[:, 0:keys]))
                    by_window = total[:, 0:keys].rearrange("p (w k) -> p w k", k=per)
                    then(v.tensor_reduce(edges_of[:, :], by_window, AX_X, ALU.add))
                    then(v.tensor_scalar(whole_groups[:, :], edges_of[:, :], float(GROUP - 1), None, ALU.add))
                    then(v.tensor_scalar(whole_groups[:, :], whole_groups[:, :], GROUP.bit_length() - 1, None,
                                         ALU.arith_shift_right))
                    then(v.tensor_copy(groups_of[:, :], whole_groups[:, :]))
                    then(v.tensor_tensor_scan(groups_upto[:, :], groups_of[:, :], zero_w[:, :], 0.0, ALU.add, ALU.add))
                    offset = column[:, 0:keys].rearrange("p (w k) -> p w k", k=per)
                    then(v.tensor_tensor(offset[:, :, 0], groups_upto[:, :], groups_of[:, :], ALU.subtract))
                    then(v.tensor_scalar(offset[:, :, 0], offset[:, :, 0], float(GROUP), None, ALU.mult))
                    for k in range(1, per):
                        then(v.tensor_tensor(offset[:, :, k], offset[:, :, k - 1], by_window[:, :, k - 1], ALU.add))
                    then(v.tensor_tensor(base[:, :], column[:, 0:keys], ps_before[:, 0:keys], ALU.add))
                    then(v.memset(window_f[0][:, :], 0.0))
                    for w in range(WINDOWS - 1):
                        then(v.scalar_tensor_tensor(window_f[(w + 1) % 2][:, :], group_no[:, :],
                                                    groups_upto[0:1, w:w + 1], window_f[w % 2][:, :],
                                                    ALU.is_ge, ALU.add))
                    v.tensor_copy(window[:, :], window_f[(WINDOWS - 1) % 2][:, :]).then_inc(used, 1)
                    dve.wait_ge(used, n + 1)
    counts.close()

    def window_of(engine, window, i):
        return engine.value_load(window[0:1, bass.ds(i, 1)], min_val=0, max_val=WINDOWS - 1)

    def place_rows(steps, keys, base, target, load, features=None):
        def columns(i, slot, tag_rows):
            if features is None:
                here = bass.ds(i * TILES, TILES)
                return rows[:, slot, :, D + SRC1], lo1[:, here], hi1[:, here]
            return (tag_rows[:, slot, :, HE + c] for c in (SEG2, DLO1, HI2))

        with ExitStack() as st:
            hot = sb(st, [P, SLOTS, TILES, P], BF16)
            hot_hi = sb(st, [P, SLOTS, TILES, keys], BF16)
            hot_t = sb(st, [P, SLOTS, TILES, P])
            table = sb(st, [P, SLOTS, TILES, keys])
            rank = sb(st, [P, SLOTS, TILES])
            found = sb(st, [P, SLOTS, TILES])
            nowhere = sb(st, [P, SLOTS, TILES])
            spot = sb(st, [P, SLOTS, TILES])
            index = sb(st, [P, SLOTS, TILES], I32)
            same = sb(st, [P, TILES, P])
            picked = sb(st, [P, TILES, keys])
            rows = sb(st, [P, SLOTS, TILES, PAY])
            ps_hot_t = ps(st, [P, TILES, P], BF16)
            ps_keys = ps(st, [P, TILES, P])
            ps_table = ps(st, [P, 512])
            ps_found = ps(st, [P, TILES, 256])
            loaded = [sem(f"loaded{s}") for s in range(SLOTS)]
            scattered = [gpsimd_dma_sem(f"scattered{s}") for s in range(SLOTS)]
            hot_ready = sem("hot_ready")
            keys_spread = sem("keys_spread")
            ranked = sem("ranked")
            hot_turned = sem("hot_turned")
            hot_copied = sem("hot_copied")
            table_grown = sem("table_grown")
            table_copied = sem("table_copied")
            looked_up = sem("looked_up")
            found_read = sem("found_read")
            part_ready = sem("part_ready")
            spot_ready = sem("spot_ready")
            index_ready = sem("index_ready")
            tagged = sem("tagged")
            begun = sem("begun")
            tag_rows = None
            if features is not None:
                tag_rows = sb(st, [P, SLOTS, TILES, SROW])
                pick = sb(st, [P, SLOTS, R, GROUP])
                ps_pick = ps(st, [P, GROUP])
                ps_feat = ps(st, [P, TILES, 256])
                pick_spread = sem("pick_spread")
                pick_ready = sem("pick_ready")
                feat_ready = sem("feat_ready")
            with nc.Block() as block:

                @block.sync
                def _(sp):
                    if features is not None:
                        load(sp, tag_rows, loaded, tagged, index_ready)
                    else:
                        load(sp, rows, loaded, scattered)

                @block.gpsimd
                def _(pool):
                    def scatter(i, slot, turn):
                        pool.wait_ge(index_ready, i + 1)
                        pool.wait_ge(tagged, i + 1)
                        if features is None:
                            pool.wait_ge(loaded[slot], PARTS * (turn + 1))
                        pool.sem_inc(begun, 1)
                        for j in range(TILES):
                            pool.indirect_dma_start(
                                target[:, :], bass.IndirectOffsetOnAxis(ap=index[:, slot, j:j + 1], axis=0),
                                rows[:, slot, j, :], None, bounds_check=NPOS - 1,
                                oob_is_err=False).then_inc(scattered[slot], 16)

                    pipelined(pool, steps, [scatter])
                    for s in range(SLOTS):
                        pool.wait_ge(scattered[s], 64 * len(range(s, steps, SLOTS)))

                @block.vector
                def _(dve):
                    v = nc.vector

                    def one_hots(i, slot, turn):
                        key, lo, hi = columns(i, slot, tag_rows)
                        if features is not None:
                            dve.wait_ge(loaded[slot], 16 * (turn + 1))
                        wait(dve, looked_up, i - SLOTS + 1)
                        v.tensor_tensor(hot[:, slot, :, :], lo.unsqueeze(2).to_broadcast([P, TILES, P]),
                                        count1_bf[:, 0:P].unsqueeze(1).to_broadcast([P, TILES, P]), ALU.is_equal)
                        v.tensor_tensor(hot_hi[:, slot, :, :], hi.unsqueeze(2).to_broadcast([P, TILES, keys]),
                                        count1_bf[:, 0:keys].unsqueeze(1).to_broadcast([P, TILES, keys]),
                                        ALU.is_equal).then_inc(hot_ready, 1)
                        if features is not None:
                            dve.wait_ge(pick_spread, i + 1)
                            wait(dve, feat_ready, i - SLOTS + 1)
                            for t in range(R):
                                last = v.tensor_scalar(pick[:, slot, t, :], ps_pick[:, :], row1[:, t:t + 1], None,
                                                       ALU.is_equal)
                            last.then_inc(pick_ready, 1)

                    def positions(i, slot, turn):
                        key, lo, hi = columns(i, slot, tag_rows)
                        dve.wait_ge(keys_spread, i + 1)
                        for j in range(TILES):
                            last = v.scalar_tensor_tensor(same[:, j, :], ps_keys[:, j, :], key[:, j:j + 1], after[:, :],
                                                          ALU.is_equal, ALU.mult, accum_out=rank[:, slot, j:j + 1])
                        last.then_inc(ranked, 1)
                        wait(dve, scattered[slot], 64 * turn)
                        v.tensor_scalar(nowhere[:, slot, :], hi, 0.5, NOWHERE, ALU.is_lt, ALU.mult)
                        dve.wait_ge(looked_up, i + 1)
                        for j in range(TILES):
                            last = v.scalar_tensor_tensor(picked[:, j, :], ps_found[:, j, 0:keys], 1.0,
                                                          hot_hi[:, slot, j, :], ALU.mult, ALU.mult,
                                                          accum_out=found[:, slot, j:j + 1])
                        last.then_inc(found_read, 1)
                        dve.wait_ge(found_read, i + 1)
                        v.tensor_tensor(spot[:, slot, :], found[:, slot, :], rank[:, slot, :],
                                        ALU.add).then_inc(spot_ready, 1)
                        dve.wait_ge(spot_ready, i + 1)
                        v.tensor_tensor(index[:, slot, :], spot[:, slot, :], nowhere[:, slot, :],
                                        ALU.add).then_inc(index_ready, 1)

                    pipelined(dve, steps, [one_hots, positions])

                @block.tensor
                def _(pe):
                    nc.tensor.matmul(ps_table[:, 0:keys], ident[:, :], base[:, :], start=True,
                                     stop=True).then_inc(table_grown, 1)
                    def turn_and_spread(i, slot, turn):
                        key, lo, hi = columns(i, slot, tag_rows)
                        if features is not None:
                            pe.wait_ge(loaded[slot], 16 * (turn + 1))
                            wait(pe, pick_ready, i)
                            for j in range(TILES):
                                last = nc.tensor.transpose(
                                    ps_pick[:, j * P:(j + 1) * P],
                                    tag_rows[:, slot, j, HE + KEY1:HE + KEY1 + 1].to_broadcast([P, P]), ident[:, :])
                            last.then_inc(pick_spread, 1)
                        else:
                            pe.wait_ge(tagged, i + 1)
                        wait(pe, ranked, i)
                        for j in range(TILES):
                            last = nc.tensor.transpose(ps_keys[:, j, :], key[:, j:j + 1].to_broadcast([P, P]),
                                                       ident[:, :])
                        last.then_inc(keys_spread, 1)
                        pe.wait_ge(hot_ready, i + 1)
                        wait(pe, hot_copied, i)
                        for j in range(TILES):
                            last = nc.tensor.transpose(ps_hot_t[:, j, :], hot[:, slot, j, :], ident_bf[:, :])
                        last.then_inc(hot_turned, 1)
                        for j in range(TILES):
                            pe.wait_ge(table_copied, i * TILES + j + 1)
                            nc.tensor.matmul(ps_table[:, 0:keys], hot[:, slot, j, :], hot_hi[:, slot, j, :],
                                             start=False, stop=True, skip_group_check=True).then_inc(table_grown, 1)

                    def look_up(i, slot, turn):
                        pe.wait_ge(hot_copied, i + 1)
                        wait(pe, found_read, i)
                        for j in range(TILES):
                            last = nc.tensor.matmul(ps_found[:, j, 0:keys], hot_t[:, slot, j, :],
                                                    table[:, slot, j, :], start=True, stop=True)
                        last.then_inc(looked_up, 1)
                        if features is not None:
                            w = window_of(pe, window1, i)
                            pe.wait_ge(pick_ready, i + 1)
                            wait(pe, tagged, i)
                            for j in range(TILES):
                                for t in range(R):
                                    last = nc.tensor.matmul(ps_feat[:, j, 0:FEAT], pick[:, slot, t, j * P:(j + 1) * P],
                                                            features[:, bass.ds(w, 1), t, :].rearrange("p a c -> p (a c)"), start=(t == 0), stop=(t == R - 1))
                            last.then_inc(feat_ready, 1)

                    pipelined(pe, steps, [turn_and_spread, look_up])

                @block.scalar
                def _(act):
                    a = nc.scalar

                    def copies(i, slot, turn):
                        if features is None:
                            wait(act, scattered[slot], 64 * turn)
                            a.activation(rows[:, slot, :, D:PAY], tags[:, bass.ds(i * TILES, TILES), :],
                                         ACT.Copy).then_inc(tagged, 1)
                        for j in range(TILES):
                            act.wait_ge(table_grown, i * TILES + j + 1)
                            if j == 0:
                                wait(act, looked_up, i - SLOTS + 1)
                            a.activation(table[:, slot, j, :], ps_table[:, 0:keys], ACT.Copy).then_inc(table_copied, 1)
                            if j == 0:
                                act.wait_ge(hot_turned, i + 1)
                                a.activation(hot_t[:, slot, :, :], ps_hot_t[:, :, :], ACT.Copy).then_inc(hot_copied, 1)

                    def tag(i, slot, turn):
                        wait(act, scattered[slot], 64 * turn)
                        act.wait_ge(loaded[slot], 16 * (turn + 1))
                        a.activation(rows[:, slot, :, FEAT:YROW], tag_rows[:, slot, :, SROW - 4:SROW], ACT.Copy)
                        act.wait_ge(feat_ready, i + 1)
                        a.activation(rows[:, slot, :, 0:FEAT], ps_feat[:, :, 0:FEAT], ACT.Copy).then_inc(tagged, 1)

                    pipelined(act, steps, [copies] if features is None else [copies, tag])

    PARTS = 48
    cut = (P - 1) // 16 * 16
    spare = TAIL % TILES
    assert FULL % SLOTS == 0 and spare > 0
    edges_of_partition = edge_attr[0:(P - 1) * COLS, :].rearrange("(p c) d -> p c d", p=P - 1)

    def load_edges(sp, rows, loaded, scattered):
        def whole_group(i, slot, turn):
            wait(sp, scattered[slot], 64 * turn)
            sp.dma_start(rows[:, slot, :, 0:D],
                         bass.AP(edge_attr.tensor, i * (TILES * D), [[COLS * D, P], [D, TILES], [1, D]])
                         ).then_inc(loaded[slot], PARTS)

        def cut_group(i, slot, turn):
            wait(sp, scattered[slot], 64 * turn)
            here = bass.ds(i * TILES, TILES)
            sp.dma_start(rows[0:cut, slot, :, 0:D], edges_of_partition[0:cut, here, :]).then_inc(loaded[slot], 16)
            sp.dma_start(rows[cut:P - 1, slot, :, 0:D],
                         edges_of_partition[cut:P - 1, here, :]).then_inc(loaded[slot], 16)
            sp.dma_start(rows[P - 1:P, slot, 0:spare, 0:D],
                         edge_attr[E - spare:E, :].unsqueeze(0)).then_inc(loaded[slot], 16)

        pipelined(sp, FULL, [whole_group])
        rounds = (IN_GROUPS - FULL) // SLOTS
        with sp.Fori(0, rounds) as k:
            for u in range(SLOTS):
                cut_group(k * SLOTS + FULL + u, u, k + FULL // SLOTS)
        for i in range(FULL + rounds * SLOTS, IN_GROUPS):
            cut_group(i, i % SLOTS, i // SLOTS)

    place_rows(IN_GROUPS, WINDOWS, base1, by_src, load_edges)
    edges.close()

    by_src_g = by_src.rearrange("(g p j) c -> g p (j c)", p=P, j=TILES)
    values_g = values.rearrange("(g p j) c -> g p j c", p=P, j=TILES)
    scores_g = scores.rearrange("(g p j) c -> g p (j c)", p=P, j=TILES)
    with ExitStack() as st:
        w_e = sb(st, [P, 2, D])
        w_exp = sb(st, [P, HE])
        rows = sb(st, [P, SLOTS, TILES, PAY])
        target = sb(st, [P, SLOTS, TILES], I32)
        kv = sb(st, [P, SLOTS, TILES, KV])
        edge_t = sb(st, [P, SLOTS, GROUP])
        pick = sb(st, [P, SLOTS, GROUP])
        product = sb(st, [P, SLOTS, TILES, D])
        product_t = sb(st, [P, SLOTS, GROUP])
        scored = sb(st, [P, SLOTS, TILES, SROW])
        ps_edge_t = ps(st, [P, GROUP])
        ps_pick = ps(st, [P, GROUP])
        ps_kv = ps(st, [P, TILES, KV])
        ps_q = ps(st, [P, TILES, D])
        ps_product_t = ps(st, [P, GROUP])
        ps_score = ps(st, [P, TILES, HE])
        weights = sem("weights")
        loaded = [sem(f"loaded{s}") for s in range(SLOTS)]
        fetched = [gpsimd_dma_sem(f"fetched{s}") for s in range(SLOTS)]
        stored = [sem(f"stored{s}") for s in range(SLOTS)]
        target_ready = sem("target_ready")
        begun = sem("begun")
        tags_copied = sem("tags_copied")
        edge_turned = sem("edge_turned")
        edge_copied = sem("edge_copied")
        pick_spread = sem("pick_spread")
        pick_ready = sem("pick_ready")
        edge_projected = sem("edge_projected")
        q_fetched = sem("q_fetched")
        kv_ready = sem("kv_ready")
        product_ready = sem("product_ready")
        product_turned = sem("product_turned")
        product_copied = sem("product_copied")
        score_ready = sem("score_ready")
        score_copied = sem("score_copied")
        with nc.Block() as block:

            @block.sync
            def _(sp):
                sp.dma_start(w_e[:, 0, :], Wek).then_inc(weights, 16)
                sp.dma_start(w_e[:, 1, :], Wev).then_inc(weights, 16)
                for h in range(H0):
                    width = D // H0
                    sp.dma_start(w_exp[h * width:(h + 1) * width, :],
                                 Wexp[h:h + 1, :].to_broadcast([width, HE])).then_inc(weights, 16)

                def load(i, slot, turn):
                    wait(sp, edge_turned, i - SLOTS + 1)
                    wait(sp, pick_spread, i - SLOTS + 1)
                    wait(sp, tags_copied, i - SLOTS + 1)
                    sp.dma_start(rows[:, slot, :, :].rearrange("p j c -> p (j c)"),
                                 by_src_g[bass.ds(i, 1), :, :].rearrange("a p c -> (a p) c")
                                 ).then_inc(loaded[slot], 16)

                def store(i, slot, turn):
                    sp.wait_ge(kv_ready, i + 1)
                    sp.dma_start(values_g[bass.ds(i, 1), :, :, :].rearrange("a p j c -> (a p) j c"),
                                 kv[:, slot, :, D:KV]).then_inc(stored[slot], 16)
                    sp.wait_ge(score_copied, i + 1)
                    sp.wait_ge(tags_copied, i + 1)
                    sp.dma_start(scores_g[bass.ds(i, 1), :, :].rearrange("a p c -> (a p) c"),
                                 scored[:, slot, :, :].rearrange("p j c -> p (j c)")).then_inc(stored[slot], 16)

                def nothing(i, slot, turn):
                    pass

                pipelined(sp, GROUPS, [load, nothing, store])
                for s in range(SLOTS):
                    sp.wait_ge(stored[s], 32 * len(range(s, GROUPS, SLOTS)))

            @block.gpsimd
            def _(pool):
                def fetch(i, slot, turn):
                    pool.wait_ge(target_ready, i + 1)
                    wait(pool, stored[slot], 32 * turn)
                    wait(pool, product_ready, i - SLOTS + 1)
                    pool.sem_inc(begun, 1)
                    for j in range(TILES):
                        pool.indirect_dma_start(
                            kv[:, slot, j, :], None, kv_table[:, :],
                            bass.IndirectOffsetOnAxis(ap=target[:, slot, j:j + 1], axis=0)).then_inc(fetched[slot], 16)

                pipelined(pool, GROUPS, [fetch])

            @block.scalar
            def _(act):
                a = nc.scalar

                def early(i, slot, turn):
                    act.wait_ge(loaded[slot], 16 * (turn + 1))
                    wait(act, fetched[slot], 64 * turn)
                    a.activation(target[:, slot, :], rows[:, slot, :, D + DST], ACT.Copy).then_inc(target_ready, 1)
                    wait(act, stored[slot], 32 * turn)
                    a.activation(scored[:, slot, :, HE:SROW], rows[:, slot, :, D:PAY], ACT.Copy).then_inc(tags_copied, 1)
                    act.wait_ge(edge_turned, i + 1)
                    wait(act, edge_projected, i - SLOTS + 1)
                    a.activation(edge_t[:, slot, :], ps_edge_t[:, :], ACT.Copy).then_inc(edge_copied, 1)

                def late(i, slot, turn):
                    act.wait_ge(product_turned, i + 1)
                    wait(act, score_ready, i - SLOTS + 1)
                    a.activation(product_t[:, slot, :], ps_product_t[:, :], ACT.Copy).then_inc(product_copied, 1)
                    act.wait_ge(score_ready, i + 1)
                    a.activation(scored[:, slot, :, 0:HE], ps_score[:, :, :], ACT.Copy,
                                 scale=SCALE).then_inc(score_copied, 1)

                pipelined(act, GROUPS, [early, late])

            @block.vector
            def _(dve):
                v = nc.vector

                def choose(i, slot, turn):
                    dve.wait_ge(pick_spread, i + 1)
                    wait(dve, q_fetched, i - SLOTS + 1)
                    v.tensor_scalar(pick[:, slot, :], ps_pick[:, :], row1[:, 0:1], None,
                                    ALU.is_equal).then_inc(pick_ready, 1)

                def combine(i, slot, turn):
                    dve.wait_ge(fetched[slot], 64 * (turn + 1))
                    dve.wait_ge(edge_projected, i + 1)
                    v.tensor_tensor(kv[:, slot, :, :], kv[:, slot, :, :], ps_kv[:, :, :], ALU.add).then_inc(kv_ready, 1)
                    dve.wait_ge(kv_ready, i + 1)
                    dve.wait_ge(q_fetched, i + 1)
                    wait(dve, product_turned, i - SLOTS + 1)
                    v.tensor_tensor(product[:, slot, :, :], kv[:, slot, :, 0:D], ps_q[:, :, :],
                                    ALU.mult).then_inc(product_ready, 1)

                pipelined(dve, GROUPS, [choose, combine])

            @block.tensor
            def _(pe):
                pe.wait_ge(weights, (2 + H0) * 16)

                def turn_edges(i, slot, turn):
                    pe.wait_ge(loaded[slot], 16 * (turn + 1))
                    wait(pe, pick_ready, i)
                    for j in range(TILES):
                        last = nc.tensor.transpose(ps_pick[:, j * P:(j + 1) * P],
                                                   rows[:, slot, j, D + LO1:D + LO1 + 1].to_broadcast([P, P]),
                                                   ident[:, :])
                    last.then_inc(pick_spread, 1)
                    wait(pe, edge_copied, i)
                    for j in range(TILES):
                        last = nc.tensor.transpose(ps_edge_t[:, j * P:(j + 1) * P], rows[:, slot, j, 0:D], ident[:, :])
                    last.then_inc(edge_turned, 1)

                def project(i, slot, turn):
                    w = window_of(pe, window1, i)
                    pe.wait_ge(edge_copied, i + 1)
                    wait(pe, kv_ready, i)
                    for j in range(TILES):
                        last = nc.tensor.matmul(ps_kv[:, j, :], edge_t[:, slot, j * P:(j + 1) * P],
                                                w_e[:, :, :].rearrange("p a d -> p (a d)"), start=True, stop=True)
                    last.then_inc(edge_projected, 1)
                    pe.wait_ge(pick_ready, i + 1)
                    wait(pe, product_ready, i)
                    for j in range(TILES):
                        last = nc.tensor.matmul(ps_q[:, j, :], pick[:, slot, j * P:(j + 1) * P],
                                                q_sb[:, bass.ds(w, 1), :].rearrange("p a d -> p (a d)"),
                                                start=True, stop=True)
                    last.then_inc(q_fetched, 1)

                def score(i, slot, turn):
                    pe.wait_ge(product_ready, i + 1)
                    wait(pe, product_copied, i)
                    for j in range(TILES):
                        last = nc.tensor.transpose(ps_product_t[:, j * P:(j + 1) * P], product[:, slot, j, :],
                                                   ident[:, :])
                    last.then_inc(product_turned, 1)
                    pe.wait_ge(product_copied, i + 1)
                    wait(pe, score_copied, i)
                    for j in range(TILES):
                        last = nc.tensor.matmul(ps_score[:, j, :], product_t[:, slot, j * P:(j + 1) * P],
                                                w_exp[:, :], start=True, stop=True)
                    last.then_inc(score_ready, 1)

                pipelined(pe, GROUPS, [turn_edges, project, score])
    tables0.close()

    def segment_softmax(table, width, heads, seg, self_minus):
        in_runs = table.rearrange("(p t) c -> p t c", p=P)
        flat = table.rearrange("(p t) c -> p (t c)", p=P)
        with ExitStack() as st:
            data = sb(st, [P, RUN, width])
            seg_before = sb(st, [P, 1])
            seg_behind = sb(st, [P, 1])
            same_f = sb(st, [P, RUN])
            same_b = sb(st, [P, RUN])
            low_f = sb(st, [P, RUN])
            low_b = sb(st, [P, RUN])
            fwd = sb(st, [P, RUN])
            bwd = sb(st, [P, RUN])
            ends = sb(st, [P, 4, heads])
            ends_t = sb(st, [heads, 4, P])
            through = sb(st, [P, 4])
            chain = sb(st, [heads, 2, P])
            carry_t = sb(st, [heads, 2, P])
            carry = sb(st, [P, 2, heads])
            ps_ends = ps(st, [heads, 4, P])
            ps_carry = ps(st, [P, 2, heads])
            filled = sem("filled")
            loaded = sem("loaded")
            stored = sem("stored")
            step = sem("step")
            ends_ready = sem("ends_ready")
            ends_turned = sem("ends_turned")
            carry_ready = sem("carry_ready")
            carry_turned = sem("carry_turned")
            shifted = sem("shifted")
            exponent = sem("exponent")
            weights_ready = sem("weights_ready")
            with nc.Block() as block:

                @block.sync
                def _(sp):
                    sp.dma_start(data[:, :, :].rearrange("p t c -> p (t c)"), flat).then_inc(loaded, 16)
                    sp.wait_ge(filled, 1)
                    sp.dma_start(seg_before[1:P, :], in_runs[0:P - 1, RUN - 1, seg:seg + 1],
                                 allow_slow_non_contiguous=True).then_inc(loaded, 16)
                    sp.dma_start(seg_behind[0:P - 1, :], in_runs[1:P, 0, seg:seg + 1],
                                 allow_slow_non_contiguous=True).then_inc(loaded, 16)
                    sp.wait_ge(weights_ready, heads)
                    sp.dma_start(flat, data[:, :, :].rearrange("p t c -> p (t c)")).then_inc(stored, 16)
                    sp.wait_ge(stored, 16)

                @block.tensor
                def _(pe):
                    for n in range(2):
                        pe.wait_ge(ends_ready, n + 1)
                        for k in range(4):
                            last = nc.tensor.transpose(ps_ends[:, k, :], ends[:, k, :], ident[:, :])
                        last.then_inc(ends_turned, 1)
                        pe.wait_ge(carry_ready, n + 1)
                        for k in range(2):
                            last = nc.tensor.transpose(ps_carry[:, k, :], carry_t[:, k, :], ident[0:heads, 0:heads])
                        last.then_inc(carry_turned, 1)

                @block.scalar
                def _(act):
                    for h in range(heads):
                        act.wait_ge(shifted, h + 1)
                        nc.scalar.activation(data[:, :, h], data[:, :, h], ACT.Exp).then_inc(exponent, 1)

                @block.vector
                def _(dve):
                    done = [0]

                    def then(instruction):
                        done[0] += 1
                        instruction.then_inc(step, 1)
                        dve.wait_ge(step, done[0])

                    v = nc.vector
                    v.memset(seg_before[:, :], -1.0)
                    v.memset(seg_behind[:, :], -1.0).then_inc(filled, 1)
                    dve.wait_ge(loaded, 3 * 16)
                    segs = data[:, :, seg]
                    v.tensor_tensor(same_f[:, 0:1], segs[:, 0:1], seg_before[:, :], ALU.is_equal)
                    v.tensor_tensor(same_f[:, 1:RUN], segs[:, 1:RUN], segs[:, 0:RUN - 1], ALU.is_equal)
                    v.tensor_tensor(same_b[:, RUN - 1:RUN], segs[:, RUN - 1:RUN], seg_behind[:, :], ALU.is_equal)
                    then(v.tensor_tensor(same_b[:, 0:RUN - 1], segs[:, 0:RUN - 1], segs[:, 1:RUN], ALU.is_equal))
                    v.tensor_scalar(low_f[:, :], same_f[:, :], 1.0, -LOW, ALU.subtract, ALU.mult)
                    v.tensor_scalar(low_b[:, :], same_b[:, :], 1.0, -LOW, ALU.subtract, ALU.mult)
                    v.tensor_reduce(through[:, 2:3], same_f[:, :], AX_X, ALU.min)
                    then(v.tensor_reduce(through[:, 3:4], same_b[:, :], AX_X, ALU.min))
                    then(v.tensor_scalar(through[:, 0:2], through[:, 2:4], 1.0, -LOW, ALU.subtract, ALU.mult))

                    def scans(h, flags, start, op, first, second):
                        v.tensor_tensor_scan(fwd[:, :], flags[0][:, :], data[:, :, h], first, op[0], op[1])
                        then(v.tensor_tensor_scan(bwd[:, ::-1], flags[1][:, ::-1], data[:, ::-1, h], second,
                                                  op[0], op[1]))

                    for n, (flags, start, op) in enumerate((
                            ((low_f, low_b), LOW, (ALU.add, ALU.max)),
                            ((same_f, same_b), 0.0, (ALU.mult, ALU.add)))):
                        for h in range(heads):
                            if n == 1:
                                dve.wait_ge(exponent, h + 1)
                            scans(h, flags, start, op, start, start)
                            v.tensor_copy(ends[:, 0, h:h + 1], fwd[:, RUN - 1:RUN])
                            then(v.tensor_copy(ends[:, 1, h:h + 1], bwd[:, 0:1]))
                        v.tensor_copy(ends[:, 2, :], through[:, 2 * n:2 * n + 1].to_broadcast([P, heads]))
                        v.tensor_copy(ends[:, 3, :], through[:, 2 * n + 1:2 * n + 2].to_broadcast([P, heads])
                                      ).then_inc(ends_ready, 1)
                        dve.wait_ge(ends_turned, n + 1)
                        then(v.tensor_copy(ends_t[:, :, :], ps_ends[:, :, :]))
                        v.tensor_tensor_scan(chain[:, 0, :], ends_t[:, 2, :], ends_t[:, 0, :], start, op[0], op[1])
                        v.tensor_tensor_scan(chain[:, 1, ::-1], ends_t[:, 3, ::-1], ends_t[:, 1, ::-1], start,
                                             op[0], op[1])
                        then(v.memset(carry_t[:, :, :], start))
                        v.tensor_copy(carry_t[:, 0, 1:P], chain[:, 0, 0:P - 1])
                        v.tensor_copy(carry_t[:, 1, 0:P - 1], chain[:, 1, 1:P]).then_inc(carry_ready, 1)
                        dve.wait_ge(carry_turned, n + 1)
                        then(v.tensor_copy(carry[:, :, :], ps_carry[:, :, :]))
                        if n == 1 and self_minus:
                            then(v.scalar_tensor_tensor(low_f[:, :], data[:, :, HE + DST], 1.0,
                                                        data[:, :, HE + SRC1], ALU.add, ALU.is_equal))
                        for h in range(heads):
                            scans(h, flags, start, op, carry[:, 0, h:h + 1], carry[:, 1, h:h + 1])
                            if n == 0:
                                then(v.tensor_tensor(fwd[:, :], fwd[:, :], bwd[:, :], ALU.max))
                                v.tensor_tensor(data[:, :, h], data[:, :, h], fwd[:, :],
                                                ALU.subtract).then_inc(shifted, 1)
                                dve.wait_ge(shifted, h + 1)
                            else:
                                then(v.tensor_tensor(bwd[:, :], bwd[:, :], data[:, :, h], ALU.subtract))
                                then(v.tensor_tensor(fwd[:, :], fwd[:, :], bwd[:, :], ALU.add))
                                then(v.reciprocal(fwd[:, :], fwd[:, :]))
                                last = v.tensor_tensor(data[:, :, h], data[:, :, h], fwd[:, :], ALU.mult)
                                if self_minus:
                                    then(last)
                                    last = v.tensor_tensor(data[:, :, h], low_f[:, :], data[:, :, h], ALU.subtract)
                                last.then_inc(weights_ready, 1)
                                dve.wait_ge(weights_ready, h + 1)

    def weighted_sums(total, value_groups, weight_groups, width, heads, lo, window):
        with ExitStack() as st:
            value = sb(st, [P, SLOTS, TILES, D])
            weight = sb(st, [P, SLOTS, TILES, width])
            pick = sb(st, [P, SLOTS, TILES, P])
            ps_sum = [ps(st, [P, 512]) for _ in range(SLOTS)]
            loaded = [sem(f"loaded{s}") for s in range(SLOTS)]
            weighted = sem("weighted")
            pick_ready = sem("pick_ready")
            summed = sem("summed")
            added = sem("added")
            cleared = sem("cleared")
            with nc.Block() as block:

                @block.sync
                def _(sp):
                    def load(i, slot, turn):
                        wait(sp, summed, i - SLOTS + 1)
                        sp.dma_start(value[:, slot, :, :], value_groups(i)).then_inc(loaded[slot], 16)
                        sp.dma_start(weight[:, slot, :, :].rearrange("p j c -> p (j c)"),
                                     weight_groups[bass.ds(i, 1), :, :].rearrange("a p c -> (a p) c")
                                     ).then_inc(loaded[slot], 16)

                    pipelined(sp, GROUPS, [load])

                @block.gpsimd
                def _(pool):
                    def weigh(i, slot, turn):
                        pool.wait_ge(loaded[slot], 32 * (turn + 1))
                        by_head = value[:, slot, :, :].rearrange("p j (h d) -> p j h d", h=heads)
                        pool.tensor_tensor(by_head, by_head,
                                           weight[:, slot, :, 0:heads].unsqueeze(3)
                                           .to_broadcast([P, TILES, heads, D // heads]), ALU.mult).then_inc(weighted, 1)

                    pipelined(pool, GROUPS, [weigh])

                @block.vector
                def _(dve):
                    v = nc.vector
                    v.memset(total[:, :, :], 0.0).then_inc(cleared, 1)
                    dve.wait_ge(cleared, 1)

                    def choose(i, slot, turn):
                        dve.wait_ge(loaded[slot], 32 * (turn + 1))
                        wait(dve, summed, i - SLOTS + 1)
                        v.tensor_tensor(pick[:, slot, :, :],
                                        weight[:, slot, :, lo:lo + 1].to_broadcast([P, TILES, P]),
                                        count1[:, :].unsqueeze(1).to_broadcast([P, TILES, P]),
                                        ALU.is_equal).then_inc(pick_ready, 1)

                    def add(i, slot, turn):
                        w = window_of(dve, window, i)
                        dve.wait_ge(summed, i + 1)
                        wait(dve, added, i)
                        here = total[:, bass.ds(w, 1), :].rearrange("p a d -> p (a d)")
                        v.tensor_tensor(here, here, ps_sum[slot][:, 0:D], ALU.add).then_inc(added, 1)

                    pipelined(dve, GROUPS, [choose, add])

                @block.tensor
                def _(pe):
                    def add_up(i, slot, turn):
                        pe.wait_ge(weighted, i + 1)
                        pe.wait_ge(pick_ready, i + 1)
                        wait(pe, added, i - SLOTS + 1)
                        for j in range(TILES):
                            last = nc.tensor.matmul(ps_sum[slot][:, 0:D], pick[:, slot, j, :], value[:, slot, j, :],
                                                    start=(j == 0), stop=(j == TILES - 1))
                        last.then_inc(summed, 1)

                    pipelined(pe, GROUPS, [add_up])

    segment_softmax(scores, SROW, HE, HE + SRC1, True)

    tables1 = ExitStack()
    features = sb(tables1, [P, WINDOWS, R, FEAT])
    dst_score = sb(tables1, [P, WINDOWS, R * H1])
    with ExitStack() as sums:
        total = sb(sums, [P, WINDOWS, D])

        def values_of(i):
            return values_g[bass.ds(i, 1), :, :, :].rearrange("a p j c -> (a p) j c")

        weighted_sums(total, values_of, scores_g, SROW, HE, HE + LO1, window1)

        with ExitStack() as st:
            w_out = sb(st, [P, D])
            b_out = sb(st, [1, D])
            rows = sb(st, [P, SLOTS, D])
            rows_t = sb(st, [P, SLOTS, P])
            ps_t = [ps(st, [P, 512]) for _ in range(SLOTS)]
            ps_out = [ps(st, [P, 512]) for _ in range(SLOTS)]
            weights = sem("weights")
            copied = sem("copied")
            turned = sem("turned")
            turned_copied = sem("turned_copied")
            projected = sem("projected")
            added = sem("added")
            with nc.Block() as block:

                @block.sync
                def _(sp):
                    sp.dma_start(w_out[:, :], Wout).then_inc(weights, 16)
                    sp.dma_start(b_out[:, :], bout.rearrange("(a d) -> a d", a=1)).then_inc(weights, 16)

                @block.scalar
                def _(act):
                    def copy_rows(i, slot, turn):
                        wait(act, turned, i - SLOTS + 1)
                        nc.scalar.activation(rows[:, slot, :], total[:, bass.ds(i, 1), :].rearrange("p a d -> p (a d)"),
                                             ACT.Copy).then_inc(copied, 1)

                    def copy_turned(i, slot, turn):
                        act.wait_ge(turned, i + 1)
                        wait(act, projected, i - SLOTS + 1)
                        nc.scalar.activation(rows_t[:, slot, :], ps_t[slot][:, 0:P], ACT.Copy).then_inc(turned_copied, 1)

                    pipelined(act, WINDOWS, [copy_rows, copy_turned])

                @block.tensor
                def _(pe):
                    pe.wait_ge(weights, 32)

                    def turn_rows(i, slot, turn):
                        pe.wait_ge(copied, i + 1)
                        wait(pe, turned_copied, i - SLOTS + 1)
                        nc.tensor.transpose(ps_t[slot][:, 0:P], rows[:, slot, :], ident[:, :]).then_inc(turned, 1)

                    def project(i, slot, turn):
                        pe.wait_ge(turned_copied, i + 1)
                        wait(pe, added, i - SLOTS + 1)
                        nc.tensor.matmul(ps_out[slot][:, 0:D], rows_t[:, slot, :], w_out[:, :], start=True, stop=False)
                        nc.tensor.matmul(ps_out[slot][:, 0:D], ones[0:1, :], b_out[:, :], start=False,
                                         stop=True).then_inc(projected, 1)

                    pipelined(pe, WINDOWS, [turn_rows, project])

                @block.vector
                def _(dve):
                    def add(i, slot, turn):
                        dve.wait_ge(projected, i + 1)
                        here = x_sb[:, bass.ds(i, 1), :].rearrange("p a d -> p (a d)")
                        nc.vector.tensor_tensor(here, here, ps_out[slot][:, 0:D], ALU.add).then_inc(added, 1)

                    pipelined(dve, WINDOWS, [add])

    with ExitStack() as st:
        hn = sb(st, [P, WINDOWS, D])
        layernorm_relu_input(hn)
        w_all = sb(st, [P, R, D])
        attn_all = sb(st, [P, R * H1, 2 * HD1])
        h = sb(st, [P, SLOTS, D])
        h_t = sb(st, [P, SLOTS, P])
        product = sb(st, [P, 2, R * H1, HD1])
        ps_t = [ps(st, [P, 512]) for _ in range(SLOTS)]
        ps_feat = [ps(st, [P, R, D]) for _ in range(SLOTS)]
        weights = sem("weights")
        relu_done = sem("relu_done")
        turned = sem("turned")
        turned_copied = sem("turned_copied")
        projected = sem("projected")
        product_ready = sem("product_ready")
        scored = sem("scored")
        kept = sem("kept")
        with nc.Block() as block:

            @block.sync
            def _(sp):
                for r in range(R):
                    sp.dma_start(w_all[:, r, :], W_rel[r, :, :]).then_inc(weights, 16)
                sp.dma_start(attn_all[:, :, :].rearrange("p a b -> p (a b)"),
                             attn.rearrange("(o a) b c -> o (a b c)", o=1).to_broadcast([P, R * H1 * 2 * HD1])
                             ).then_inc(weights, 16)

            @block.scalar
            def _(act):
                def rectify(i, slot, turn):
                    wait(act, turned, i - SLOTS + 1)
                    nc.scalar.activation(h[:, slot, :], hn[:, bass.ds(i, 1), :].rearrange("p a d -> p (a d)"),
                                         ACT.Relu).then_inc(relu_done, 1)

                def copy_turned(i, slot, turn):
                    act.wait_ge(turned, i + 1)
                    wait(act, projected, i - SLOTS + 1)
                    nc.scalar.activation(h_t[:, slot, :], ps_t[slot][:, 0:P], ACT.Copy).then_inc(turned_copied, 1)

                def keep(i, slot, turn):
                    act.wait_ge(projected, i + 1)
                    nc.scalar.activation(features[:, bass.ds(i, 1), :, 0:D].rearrange("p a r d -> p (a r) d"),
                                         ps_feat[slot][:, :, :], ACT.Copy).then_inc(kept, 1)

                pipelined(act, WINDOWS, [rectify, copy_turned, keep])

            @block.tensor
            def _(pe):
                pe.wait_ge(weights, (R + 1) * 16)

                def turn_h(i, slot, turn):
                    pe.wait_ge(relu_done, i + 1)
                    wait(pe, turned_copied, i - SLOTS + 1)
                    nc.tensor.transpose(ps_t[slot][:, 0:P], h[:, slot, :], ident[:, :]).then_inc(turned, 1)

                def project(i, slot, turn):
                    pe.wait_ge(turned_copied, i + 1)
                    wait(pe, kept, i - SLOTS + 1)
                    wait(pe, scored, i - SLOTS + 1)
                    nc.tensor.matmul(ps_feat[slot][:, :, :].rearrange("p r d -> p (r d)"), h_t[:, slot, :],
                                     w_all[:, :, :].rearrange("p r d -> p (r d)"), start=True,
                                     stop=True).then_inc(projected, 1)

                pipelined(pe, WINDOWS, [turn_h, project])

            @block.vector
            def _(dve):
                v = nc.vector
                dve.wait_ge(weights, (R + 1) * 16)

                def score(i, slot, turn):
                    dve.wait_ge(kept, i + 1)
                    wait(dve, scored, i)
                    feat = ps_feat[slot][:, :, :].rearrange("p r (h d) -> p (r h) d", h=H1)
                    v.tensor_tensor(product[:, 0, :, :], feat, attn_all[:, :, 0:HD1], ALU.mult)
                    v.tensor_tensor(product[:, 1, :, :], feat, attn_all[:, :, HD1:2 * HD1],
                                    ALU.mult).then_inc(product_ready, 1)
                    dve.wait_ge(product_ready, i + 1)
                    v.tensor_reduce(features[:, bass.ds(i, 1), :, D:FEAT].rearrange("p a r h -> p (a r) h"),
                                    product[:, 0, :, :].rearrange("p (r h) d -> p r h d", h=H1), AX_X, ALU.add)
                    v.tensor_reduce(dst_score[:, bass.ds(i, 1), :].rearrange("p a c -> p (a c)"),
                                    product[:, 1, :, :], AX_X, ALU.add).then_inc(scored, 1)

                pipelined(dve, WINDOWS, [score])

    fresh_semaphores()

    def load_tags(sp, tag_rows, loaded, tagged, index_ready):
        def load(i, slot, turn):
            wait(sp, tagged, i - SLOTS + 1)
            wait(sp, index_ready, i - SLOTS + 1)
            sp.dma_start(tag_rows[:, slot, :, :].rearrange("p j c -> p (j c)"),
                         scores_g[bass.ds(i, 1), :, :].rearrange("a p c -> (a p) c")).then_inc(loaded[slot], 16)

        pipelined(sp, GROUPS, [load])

    place_rows(GROUPS, KEYS2, base2, by_dst, load_tags, features)

    by_dst_g = by_dst.rearrange("(g p j) c -> g p (j c)", p=P, j=TILES)
    by_dst_rows = by_dst.rearrange("(g p j) c -> g p j c", p=P, j=TILES)
    alphas_g = alphas.rearrange("(g p j) c -> g p (j c)", p=P, j=TILES)
    Y_DLO1, Y_TYPE, Y_SEG = 1, 2, 3
    with ExitStack() as st:
        rows = sb(st, [P, SLOTS, TILES, H1 + 4])
        pick = sb(st, [P, SLOTS, GROUP])
        type_hot = sb(st, [P, SLOTS, TILES, R])
        chosen = sb(st, [P, SLOTS, TILES, R, H1])
        alpha = sb(st, [P, SLOTS, TILES, H1])
        both = sb(st, [P, SLOTS, TILES, H1])
        result = sb(st, [P, SLOTS, TILES, ZROW])
        ps_pick = [ps(st, [P, GROUP]) for _ in range(SLOTS)]
        ps_score = [ps(st, [P, TILES, R * H1]) for _ in range(SLOTS)]
        loaded = [sem(f"loaded{s}") for s in range(SLOTS)]
        stored = [sem(f"stored{s}") for s in range(SLOTS)]
        pick_spread = sem("pick_spread")
        pick_ready = sem("pick_ready")
        dst_ready = sem("dst_ready")
        step = sem("step")
        result_ready = sem("result_ready")
        tags_kept = sem("tags_kept")
        with nc.Block() as block:

            @block.sync
            def _(sp):
                def load(i, slot, turn):
                    wait(sp, result_ready, i - SLOTS + 1)
                    wait(sp, tags_kept, i - SLOTS + 1)
                    sp.dma_start(rows[:, slot, :, :],
                                 by_dst_rows[bass.ds(i, 1), :, :, D:YROW].rearrange("a p j c -> (a p) j c")
                                 ).then_inc(loaded[slot], 16)

                def store(i, slot, turn):
                    sp.wait_ge(result_ready, i + 1)
                    sp.wait_ge(tags_kept, i + 1)
                    sp.dma_start(alphas_g[bass.ds(i, 1), :, :].rearrange("a p c -> (a p) c"),
                                 result[:, slot, :, :].rearrange("p j c -> p (j c)")).then_inc(stored[slot], 16)

                def nothing(i, slot, turn):
                    pass

                pipelined(sp, GROUPS, [load, nothing, store])
                for s in range(SLOTS):
                    sp.wait_ge(stored[s], 16 * len(range(s, GROUPS, SLOTS)))

            @block.scalar
            def _(act):
                def keep_tags(i, slot, turn):
                    act.wait_ge(loaded[slot], 16 * (turn + 1))
                    wait(act, stored[slot], 16 * turn)
                    nc.scalar.activation(result[:, slot, :, H1:ZROW], rows[:, slot, :, H1:H1 + 4],
                                         ACT.Copy).then_inc(tags_kept, 1)

                pipelined(act, GROUPS, [keep_tags])

            @block.tensor
            def _(pe):
                def spread(i, slot, turn):
                    pe.wait_ge(loaded[slot], 16 * (turn + 1))
                    wait(pe, pick_ready, i - SLOTS + 1)
                    for j in range(TILES):
                        last = nc.tensor.transpose(ps_pick[slot][:, j * P:(j + 1) * P],
                                                   rows[:, slot, j, H1 + Y_DLO1:H1 + Y_DLO1 + 1].to_broadcast([P, P]),
                                                   ident[:, :])
                    last.then_inc(pick_spread, 1)

                def fetch(i, slot, turn):
                    w = window_of(pe, window2, i)
                    pe.wait_ge(pick_ready, i + 1)
                    wait(pe, result_ready, i - SLOTS + 1)
                    for j in range(TILES):
                        last = nc.tensor.matmul(ps_score[slot][:, j, :], pick[:, slot, j * P:(j + 1) * P],
                                                dst_score[:, bass.ds(w, 1), :].rearrange("p a c -> p (a c)"),
                                                start=True, stop=True)
                    last.then_inc(dst_ready, 1)

                pipelined(pe, GROUPS, [spread, fetch])

            @block.vector
            def _(dve):
                v = nc.vector

                def choose(i, slot, turn):
                    dve.wait_ge(pick_spread, i + 1)
                    wait(dve, dst_ready, i - SLOTS + 1)
                    v.tensor_tensor(type_hot[:, slot, :, :],
                                    rows[:, slot, :, H1 + Y_TYPE:H1 + Y_TYPE + 1].to_broadcast([P, TILES, R]),
                                    count0[:, :].unsqueeze(1).to_broadcast([P, TILES, R]), ALU.is_equal)
                    v.tensor_scalar(pick[:, slot, :], ps_pick[slot][:, :], row1[:, 0:1], None,
                                    ALU.is_equal).then_inc(pick_ready, 1)

                def score(i, slot, turn):
                    dve.wait_ge(dst_ready, i + 1)
                    v.tensor_tensor(chosen[:, slot, :, :, :],
                                    ps_score[slot][:, :, :].rearrange("p j (r h) -> p j r h", r=R),
                                    type_hot[:, slot, :, :].unsqueeze(3).to_broadcast([P, TILES, R, H1]),
                                    ALU.mult).then_inc(step, 1)
                    dve.wait_ge(step, i * 3 + 1)
                    v.tensor_reduce(alpha[:, slot, :, :], chosen[:, slot, :, :, :].rearrange("p j r h -> p j h r"),
                                    AX_X, ALU.add).then_inc(step, 1)
                    dve.wait_ge(step, i * 3 + 2)
                    v.tensor_tensor(both[:, slot, :, :], alpha[:, slot, :, :], rows[:, slot, :, 0:H1],
                                    ALU.add).then_inc(step, 1)
                    dve.wait_ge(step, i * 3 + 3)
                    wait(dve, stored[slot], 16 * turn)
                    v.scalar_tensor_tensor(result[:, slot, :, 0:H1], both[:, slot, :, :], SLOPE, both[:, slot, :, :],
                                           ALU.mult, ALU.max).then_inc(result_ready, 1)

                pipelined(dve, GROUPS, [choose, score])
    tables1.close()

    segment_softmax(alphas, ZROW, H1, H1 + Y_SEG, False)

    with ExitStack() as st:
        total = sb(st, [P, WINDOWS, D])

        def features_of(i):
            return by_dst_rows[bass.ds(i, 1), :, :, 0:D].rearrange("a p j c -> (a p) j c")

        weighted_sums(total, features_of, alphas_g, ZROW, H1, H1 + Y_DLO1, window2)
        added = sem("added")
        stored = sem("stored")
        with nc.Block() as block:

            @block.vector
            def _(dve):
                nc.vector.tensor_tensor(total[:, :, :], total[:, :, :], x_sb[:, :, :], ALU.add).then_inc(added, 1)

            @block.sync
            def _(sp):
                sp.wait_ge(added, 1)
                sp.dma_start(out[0:(WINDOWS - 1) * P, :].rearrange("(w p) d -> p w d", p=P),
                             total[:, 0:WINDOWS - 1, :]).then_inc(stored, 16)
                sp.dma_start(out[(WINDOWS - 1) * P:N, :], total[0:LAST, WINDOWS - 1, :]).then_inc(stored, 16)
                sp.wait_ge(stored, 32)
    whole.close()


_INS = ["x", "src", "dst", "edge_attr_128", "edge_type_4", "L0_gnn_Wq", "L0_gnn_Wk", "L0_gnn_Wv", "L0_gnn_Wek",
        "L0_gnn_Wev", "L0_gnn_Wexp", "L0_gnn_Wout", "L0_gnn_bout", "L1_gnn_W", "L1_gnn_attn"]


def kernel(**inputs):
    import numpy as _np
    import concourse.bacc as _bacc
    from concourse import mybir as _mybir
    from concourse.bass_utils import run_bass_kernel_spmd as _run

    nc = _bacc.Bacc("TRN2", target_bir_lowering=False, num_devices=1)
    arrays, args = {}, []
    for name in _INS:
        a = _np.ascontiguousarray(inputs[name])
        arrays[f"in_{name}"] = a
        args.append(nc.dram_tensor(f"in_{name}", a.shape, _mybir.dt.from_np(a.dtype), kind="ExternalInput").ap())
    shape = inputs["x"].shape
    args.append(nc.dram_tensor("out", shape, _mybir.dt.float32, kind="ExternalOutput").ap())
    gnn_kernel(nc, *args)
    r = _run(nc, [arrays], core_ids=[0])
    return r.results[0]["out"]
```

```python
from contextlib import ExitStack

import concourse.bass as bass
from concourse import mybir

F32 = mybir.dt.float32
BF16 = mybir.dt.bfloat16
I32 = mybir.dt.int32
ALU = mybir.AluOpType
ACT = mybir.ActivationFunctionType
AX_X = mybir.AxisListType.X

P = 128
SLOTS = 6
BANKS = 3
TILES = 4
GROUP = TILES * P
LOW = -3.0e38
NOWHERE = 4.0e6

SRC1, LO1, DST, HI2, KEY1, DLO1, TYPE, SEG2 = range(8)
SPOT2 = HI2
TAGS = 8


def pipelined(engine, count, stages, slots=SLOTS, start=0):
    depth = len(stages) - 1
    first = start + slots + depth
    rounds = max((count - first - 1) // slots, 0)

    def written_out(t):
        for s, stage in enumerate(stages):
            if stage and start <= t - s < count:
                stage(t - s, (t - s) % slots, (t - s) // slots)

    for t in range(start, min(first, count + depth)):
        written_out(t)
    if rounds:
        with engine.Fori(0, rounds) as k:
            for u in range(slots):
                for s, stage in enumerate(stages):
                    if stage:
                        at = first + u - s
                        stage(k * slots + at, at % slots, k + at // slots)
    for t in range(first + rounds * slots, count + depth):
        written_out(t)


def wait(engine, semaphore, value):
    if isinstance(value, int) and value <= 0:
        return
    engine.wait_ge(semaphore, value)


def gnn_kernel(nc, x, src, dst, edge_attr, edge_type, Wq, Wk, Wv, Wek, Wev, Wexp, Wout, bout, W_rel, attn, out):
    N, D = x.shape
    E = src.shape[0]
    H0, HE = Wexp.shape
    R, H1, two_hd = attn.shape
    HD1 = two_hd // 2
    SCALE = float(D // H0) ** -0.5
    EPS = 1e-5
    SLOPE = 0.2
    WINDOWS = -(-N // P)
    LAST = N - (WINDOWS - 1) * P
    COLS = -(-E // (P * TILES)) * TILES
    TAIL = E - (P - 1) * COLS
    IN_GROUPS = COLS // TILES
    FULL = TAIL // TILES
    GROUPS = (E + WINDOWS * (GROUP - 1)) // GROUP
    NPOS = GROUPS * GROUP
    RUN = NPOS // P
    KV = 2 * D
    PAY = D + TAGS
    SROW = HE + TAGS
    FEAT = D + H1
    YROW = FEAT + 4
    ZROW = H1 + 4
    KEYS2 = WINDOWS * R
    assert HE == 8 and R == 4 and H1 == 4 and D == P and YROW == PAY

    kv_table = nc.dram_tensor("kv_table", [WINDOWS * P, KV], F32).ap()
    by_src = nc.dram_tensor("by_src", [NPOS, PAY], F32).ap()
    values = nc.dram_tensor("values", [NPOS, D], F32).ap()
    scores = nc.dram_tensor("scores", [NPOS, SROW], F32).ap()
    by_dst = nc.dram_tensor("by_dst", [NPOS, YROW], F32).ap()
    alphas = nc.dram_tensor("alphas", [NPOS, ZROW], F32).ap()

    names = [0]

    def sb(stack, shape, dtype=F32):
        names[0] += 1
        return stack.enter_context(nc.sbuf_tensor(f"sb{names[0]}", list(shape), dtype))

    def ps(stack, shape, dtype=F32):
        names[0] += 1
        return stack.enter_context(nc.psum_tensor(f"ps{names[0]}", list(shape), dtype))

    spent = []

    def sem(name):
        names[0] += 1
        spent.append(nc.alloc_semaphore(f"{name}_{names[0]}"))
        return spent[-1]

    def fresh_semaphores():
        nc.clear_and_free_semaphores(list(spent))
        nc.all_engine_barrier()
        spent.clear()

    def gpsimd_dma_sem(name):
        names[0] += 1
        return nc.alloc_semaphore(f"{name}_{names[0]}")

    whole = ExitStack()
    x_sb = sb(whole, [P, WINDOWS, D])
    ident = sb(whole, [P, P])
    ident_bf = sb(whole, [P, P], BF16)
    ones = sb(whole, [P, P])
    before = sb(whole, [P, P])
    after = sb(whole, [P, P])
    count1 = sb(whole, [P, P])
    count1_bf = sb(whole, [P, KEYS2], BF16)
    count0 = sb(whole, [P, R])
    row1 = sb(whole, [P, R])
    base1 = sb(whole, [P, WINDOWS])
    base2 = sb(whole, [P, KEYS2])
    window1 = sb(whole, [1, GROUPS], I32)
    window2 = sb(whole, [1, GROUPS], I32)

    with ExitStack() as st:
        cleared = sem("cleared")
        loaded = sem("loaded")
        made = sem("made")
        with nc.Block() as block:

            @block.vector
            def _(dve):
                nc.vector.memset(x_sb[:, :, :], 0.0).then_inc(cleared, 1)
                nc.vector.memset(ones[:, :], 1.0)

            @block.sync
            def _(sp):
                sp.wait_ge(cleared, 1)
                sp.dma_start(x_sb[:, 0:WINDOWS - 1, :],
                             x[0:(WINDOWS - 1) * P, :].rearrange("(w p) d -> p w d", p=P)).then_inc(loaded, 16)
                sp.dma_start(x_sb[0:LAST, WINDOWS - 1, :], x[(WINDOWS - 1) * P:N, :]).then_inc(loaded, 16)
                sp.wait_ge(loaded, 32)

            @block.gpsimd
            def _(pool):
                for t in (ident, ident_bf, before, after):
                    pool.memset(t[:, :], 0.0).then_inc(made, 1)
                pool.wait_ge(made, 4)
                for t in (ident, ident_bf):
                    pool.affine_select(out=t[:, :], in_=t[:, :], compare_op=ALU.not_equal, fill=1.0, base=0,
                                       pattern=[[-1, P]], channel_multiplier=1)
                pool.affine_select(out=before[:, :], in_=before[:, :], compare_op=ALU.is_ge, fill=1.0, base=0,
                                   pattern=[[-1, P]], channel_multiplier=1)
                pool.affine_select(out=after[:, :], in_=after[:, :], compare_op=ALU.is_ge, fill=1.0, base=0,
                                   pattern=[[1, P]], channel_multiplier=-1)
                for t, pattern, base, step in ((count1, [[1, P]], 1, 0), (count1_bf, [[1, KEYS2]], 1, 0),
                                               (count0, [[1, R]], 0, 0), (row1, [[P, R]], 1, 1)):
                    pool.iota(t[:, :], pattern=pattern, base=base, channel_multiplier=step,
                              allow_small_or_imprecise_dtypes=True)

    tables0 = ExitStack()
    q_sb = sb(tables0, [P, WINDOWS, D])
    edges = ExitStack()
    tags = sb(edges, [P, COLS, TAGS])
    hi1 = sb(edges, [P, COLS])

    with ExitStack() as st:
        ids = [sb(st, [P, COLS], I32) for _ in range(3)]
        part = sb(st, [P, COLS], I32)
        scratch = sb(st, [P, COLS])
        cleared = sem("cleared")
        loaded = sem("loaded")
        step = sem("step")
        with nc.Block() as block:

            @block.gpsimd
            def _(pool):
                for t in ids:
                    pool.memset(t[:, :], -1).then_inc(cleared, 1)

            @block.sync
            def _(sp):
                sp.wait_ge(cleared, 3)
                for t, given in zip(ids, (src, dst, edge_type)):
                    sp.dma_start(t[0:P - 1, :],
                                 given[0:(P - 1) * COLS].rearrange("(p c) -> p c", p=P - 1)).then_inc(loaded, 16)
                    sp.dma_start(t[P - 1:P, 0:TAIL],
                                 given[(P - 1) * COLS:E].rearrange("(p c) -> p c", p=1)).then_inc(loaded, 16)

            @block.vector
            def _(dve):
                done = [0]

                def then(instruction):
                    done[0] += 1
                    instruction.then_inc(step, 1)
                    dve.wait_ge(step, done[0])

                s, d, t = (i[:, :] for i in ids)
                v = nc.vector

                def col(c):
                    return tags[:, :, c]

                dve.wait_ge(loaded, 6 * 16)
                v.tensor_scalar(col(SRC1), s, 1.0, None, ALU.add)
                v.tensor_copy(col(DST), d)
                v.tensor_copy(col(TYPE), t)
                then(v.tensor_scalar(part[:, :], s, P - 1, None, ALU.bitwise_and))
                then(v.tensor_scalar(col(LO1), part[:, :], 1.0, None, ALU.add))
                then(v.tensor_scalar(part[:, :], s, 7, None, ALU.arith_shift_right))
                then(v.tensor_scalar(hi1[:, :], part[:, :], 1.0, None, ALU.add))
                v.scalar_tensor_tensor(col(KEY1), col(TYPE), float(P), col(LO1), ALU.mult, ALU.add)
                then(v.tensor_scalar(part[:, :], d, P - 1, None, ALU.bitwise_and))
                then(v.tensor_scalar(col(DLO1), part[:, :], 1.0, None, ALU.add))
                then(v.tensor_scalar(part[:, :], d, 7, None, ALU.arith_shift_right))
                then(v.tensor_scalar(scratch[:, :], part[:, :], float(R), 1.0, ALU.mult, ALU.add))
                then(v.tensor_tensor(col(HI2), scratch[:, :], col(TYPE), ALU.add))
                then(v.tensor_scalar(scratch[:, :], d, float(R), 1.0, ALU.mult, ALU.add))
                then(v.tensor_tensor(col(SEG2), scratch[:, :], col(TYPE), ALU.add))

    def layernorm_relu_input(hn):
        with ExitStack() as st:
            square = sb(st, [P, WINDOWS, D])
            stat = sb(st, [P, WINDOWS])
            spread = sb(st, [P, WINDOWS])
            eps = sb(st, [P, 1])
            step = sem("step")
            summed = sem("summed")
            rooted = sem("rooted")
            over = stat[:, :].unsqueeze(2).to_broadcast([P, WINDOWS, D])
            with nc.Block() as block:

                @block.vector
                def _(dve):
                    done = [0]

                    def then(instruction):
                        done[0] += 1
                        instruction.then_inc(step, 1)
                        dve.wait_ge(step, done[0])

                    v = nc.vector
                    v.memset(eps[:, :], EPS)
                    then(v.tensor_reduce(stat[:, :], x_sb[:, :, :], AX_X, ALU.add))
                    then(v.tensor_scalar(stat[:, :], stat[:, :], 1.0 / D, None, ALU.mult))
                    then(v.tensor_tensor(hn[:, :, :], x_sb[:, :, :], over, ALU.subtract))
                    then(v.tensor_tensor(square[:, :, :], hn[:, :, :], hn[:, :, :], ALU.mult))
                    v.tensor_reduce(spread[:, :], square[:, :, :], AX_X, ALU.add).then_inc(summed, 1)
                    dve.wait_ge(rooted, 1)
                    then(v.reciprocal(stat[:, :], spread[:, :]))
                    v.tensor_tensor(hn[:, :, :], hn[:, :, :], over, ALU.mult)

                @block.scalar
                def _(act):
                    act.wait_ge(summed, 1)
                    nc.scalar.activation(spread[:, :], spread[:, :], ACT.Sqrt, bias=eps[:, 0:1],
                                         scale=1.0 / D).then_inc(rooted, 1)

    with ExitStack() as st:
        hn = sb(st, [P, WINDOWS, D])
        layernorm_relu_input(hn)
        w_qkv = sb(st, [P, 3, D])
        h = sb(st, [P, SLOTS, D])
        h_t = sb(st, [P, SLOTS, P])
        kv = sb(st, [P, SLOTS, KV])
        ps_t = [ps(st, [P, 512]) for _ in range(BANKS)]
        ps_qkv = [ps(st, [P, 512]) for _ in range(BANKS)]
        weights = sem("weights")
        relu_done = sem("relu_done")
        turned = sem("turned")
        turned_copied = sem("turned_copied")
        projected = sem("projected")
        taken = sem("taken")
        stored = [sem(f"stored{s}") for s in range(SLOTS)]
        with nc.Block() as block:

            @block.sync
            def _(sp):
                for n, w in enumerate((Wq, Wk, Wv)):
                    sp.dma_start(w_qkv[:, n, :], w).then_inc(weights, 16)

                def store(i, slot, turn):
                    sp.wait_ge(taken, i + 1)
                    sp.dma_start(kv_table[bass.ds(i * P, P), :], kv[:, slot, :]).then_inc(stored[slot], 16)

                pipelined(sp, WINDOWS, [store])
                for s in range(SLOTS):
                    sp.wait_ge(stored[s], 16 * len(range(s, WINDOWS, SLOTS)))

            @block.scalar
            def _(act):
                def rectify(i, slot, turn):
                    wait(act, turned, i - SLOTS + 1)
                    nc.scalar.activation(h[:, slot, :], hn[:, bass.ds(i, 1), :].rearrange("p a d -> p (a d)"),
                                         ACT.Relu).then_inc(relu_done, 1)

                def copy_turned(i, slot, turn):
                    act.wait_ge(turned, i + 1)
                    wait(act, projected, i - SLOTS + 1)
                    nc.scalar.activation(h_t[:, slot, :], ps_t[slot % BANKS][:, 0:P], ACT.Copy).then_inc(turned_copied, 1)

                pipelined(act, WINDOWS, [rectify, copy_turned])

            @block.tensor
            def _(pe):
                pe.wait_ge(weights, 3 * 16)

                def turn_h(i, slot, turn):
                    pe.wait_ge(relu_done, i + 1)
                    wait(pe, turned_copied, i - BANKS + 1)
                    nc.tensor.transpose(ps_t[slot % BANKS][:, 0:P], h[:, slot, :], ident[:, :]).then_inc(turned, 1)

                def project(i, slot, turn):
                    pe.wait_ge(turned_copied, i + 1)
                    wait(pe, taken, i - BANKS + 1)
                    nc.tensor.matmul(ps_qkv[slot % BANKS][:, 0:3 * D], h_t[:, slot, :],
                                     w_qkv[:, :, :].rearrange("p a d -> p (a d)"), start=True,
                                     stop=True).then_inc(projected, 1)

                pipelined(pe, WINDOWS, [turn_h, project])

            @block.vector
            def _(dve):
                def take(i, slot, turn):
                    dve.wait_ge(projected, i + 1)
                    wait(dve, stored[slot], 16 * turn)
                    nc.vector.tensor_copy(q_sb[:, bass.ds(i, 1), :].rearrange("p a d -> p (a d)"),
                                          ps_qkv[slot % BANKS][:, 0:D])
                    nc.vector.tensor_copy(kv[:, slot, :], ps_qkv[slot % BANKS][:, D:3 * D]).then_inc(taken, 1)

                pipelined(dve, WINDOWS, [take])

    counts = ExitStack()
    count_src = sb(counts, [P, WINDOWS])
    count_dst = sb(counts, [P, KEYS2])
    with ExitStack() as st:
        ZEROS = 7216
        pieces = NPOS * PAY // (P * ZEROS)
        assert pieces * P * ZEROS == NPOS * PAY
        zeros = sb(st, [P, ZEROS])
        hot = sb(st, [P, SLOTS, 2, TILES, P], BF16)
        hot_hi = [sb(st, [P, SLOTS, TILES, n], BF16) for n in (WINDOWS, KEYS2)]
        keys = sb(st, [P, SLOTS, TILES, TAGS])
        high = sb(st, [P, SLOTS, TILES])
        ps_count = [ps(st, [P, n]) for n in (WINDOWS, KEYS2)]
        zeroed = sem("zeroed")
        cleared = sem("cleared")
        copied = sem("copied")
        hot_ready = sem("hot_ready")
        counted = sem("counted")
        with nc.Block() as block:

            @block.sync
            def _(sp):
                sp.wait_ge(zeroed, 1)
                for buffer in (by_src, by_dst):
                    flat = buffer.rearrange("a b -> (a b)").rearrange("(n p c) -> n p c", p=P, c=ZEROS)
                    for n in range(pieces):
                        sp.dma_start(flat[n, :, :], zeros[:, :]).then_inc(cleared, 16)
                sp.wait_ge(cleared, 2 * pieces * 16)

            @block.gpsimd
            def _(pool):
                pool.memset(zeros[:, :], 0.0).then_inc(zeroed, 1)

            @block.scalar
            def _(act):
                def copy_keys(i, slot, turn):
                    wait(act, hot_ready, i - SLOTS + 1)
                    nc.scalar.activation(keys[:, slot, :, :], tags[:, bass.ds(i * TILES, TILES), :], ACT.Copy)
                    nc.scalar.activation(high[:, slot, :], hi1[:, bass.ds(i * TILES, TILES)],
                                         ACT.Copy).then_inc(copied, 1)

                pipelined(act, IN_GROUPS, [copy_keys])

            @block.vector
            def _(dve):
                def one_hots(i, slot, turn):
                    dve.wait_ge(copied, i + 1)
                    wait(dve, counted, i - SLOTS + 1)
                    for j in range(TILES):
                        for n, (lo, hi, width) in enumerate((
                                (keys[:, slot, j, LO1:LO1 + 1], high[:, slot, j:j + 1], WINDOWS),
                                (keys[:, slot, j, DLO1:DLO1 + 1], keys[:, slot, j, HI2:HI2 + 1], KEYS2))):
                            nc.vector.tensor_scalar(hot[:, slot, n, j, :], count1_bf[:, 0:P], lo, None, ALU.is_equal)
                            last = nc.vector.tensor_scalar(hot_hi[n][:, slot, j, :], count1_bf[:, 0:width], hi, None,
                                                           ALU.is_equal)
                    last.then_inc(hot_ready, 1)

                pipelined(dve, IN_GROUPS, [one_hots])
                dve.wait_ge(counted, IN_GROUPS)
                nc.vector.tensor_copy(count_src[:, :], ps_count[0][:, :])
                nc.vector.tensor_copy(count_dst[:, :], ps_count[1][:, :])

            @block.tensor
            def _(pe):
                def count(i, slot, turn):
                    pe.wait_ge(hot_ready, i + 1)
                    for n in range(2):
                        for j in range(TILES):
                            first = isinstance(i, int) and i == 0 and j == 0
                            final = isinstance(i, int) and i == IN_GROUPS - 1 and j == TILES - 1
                            last = nc.tensor.matmul(ps_count[n][:, :], hot[:, slot, n, j, :],
                                                    hot_hi[n][:, slot, j, :], start=first, stop=final)
                    last.then_inc(counted, 1)

                pipelined(pe, IN_GROUPS, [count])

    with ExitStack() as st:
        total = sb(st, [P, KEYS2])
        column = sb(st, [P, KEYS2])
        edges_of = sb(st, [P, WINDOWS])
        whole_groups = sb(st, [P, WINDOWS], I32)
        groups_of = sb(st, [P, WINDOWS])
        groups_upto = sb(st, [P, WINDOWS])
        zero_w = sb(st, [P, WINDOWS])
        group_no = sb(st, [1, GROUPS])
        window_f = [sb(st, [1, GROUPS]) for _ in range(2)]
        ps_total = ps(st, [P, 512])
        ps_before = ps(st, [P, 512])
        numbered = sem("numbered")
        summed = sem("summed")
        used = sem("used")
        step = sem("step")
        sorts = ((count_src, WINDOWS, 1, base1, window1), (count_dst, KEYS2, R, base2, window2))
        with nc.Block() as block:

            @block.gpsimd
            def _(pool):
                pool.iota(group_no[:, :], pattern=[[1, GROUPS]], base=0, channel_multiplier=0,
                          allow_small_or_imprecise_dtypes=True).then_inc(numbered, 1)

            @block.tensor
            def _(pe):
                for n, (count, keys, _, _, _) in enumerate(sorts):
                    wait(pe, used, n)
                    nc.tensor.matmul(ps_total[:, 0:keys], ones[:, :], count[:, :], start=True, stop=True)
                    nc.tensor.matmul(ps_before[:, 0:keys], before[:, :], count[:, :], start=True,
                                     stop=True).then_inc(summed, 1)

            @block.vector
            def _(dve):
                done = [0]

                def then(instruction):
                    done[0] += 1
                    instruction.then_inc(step, 1)
                    dve.wait_ge(step, done[0])

                v = nc.vector
                dve.wait_ge(numbered, 1)
                v.memset(zero_w[:, :], 0.0)
                for n, (_, keys, per, base, window) in enumerate(sorts):
                    dve.wait_ge(summed, n + 1)
                    then(v.tensor_copy(total[:, 0:keys], ps_total[:, 0:keys]))
                    by_window = total[:, 0:keys].rearrange("p (w k) -> p w k", k=per)
                    then(v.tensor_reduce(edges_of[:, :], by_window, AX_X, ALU.add))
                    then(v.tensor_scalar(whole_groups[:, :], edges_of[:, :], float(GROUP - 1), None, ALU.add))
                    then(v.tensor_scalar(whole_groups[:, :], whole_groups[:, :], GROUP.bit_length() - 1, None,
                                         ALU.arith_shift_right))
                    then(v.tensor_copy(groups_of[:, :], whole_groups[:, :]))
                    then(v.tensor_tensor_scan(groups_upto[:, :], groups_of[:, :], zero_w[:, :], 0.0, ALU.add, ALU.add))
                    offset = column[:, 0:keys].rearrange("p (w k) -> p w k", k=per)
                    then(v.tensor_tensor(offset[:, :, 0], groups_upto[:, :], groups_of[:, :], ALU.subtract))
                    then(v.tensor_scalar(offset[:, :, 0], offset[:, :, 0], float(GROUP), None, ALU.mult))
                    for k in range(1, per):
                        then(v.tensor_tensor(offset[:, :, k], offset[:, :, k - 1], by_window[:, :, k - 1], ALU.add))
                    then(v.tensor_tensor(base[:, :], column[:, 0:keys], ps_before[:, 0:keys], ALU.add))
                    then(v.memset(window_f[0][:, :], 0.0))
                    for w in range(WINDOWS - 1):
                        then(v.scalar_tensor_tensor(window_f[(w + 1) % 2][:, :], group_no[:, :],
                                                    groups_upto[0:1, w:w + 1], window_f[w % 2][:, :],
                                                    ALU.is_ge, ALU.add))
                    v.tensor_copy(window[:, :], window_f[(WINDOWS - 1) % 2][:, :]).then_inc(used, 1)
                    dve.wait_ge(used, n + 1)
    counts.close()

    def window_of(engine, window, i):
        return engine.value_load(window[0:1, bass.ds(i, 1)], min_val=0, max_val=WINDOWS - 1)

    PARTS = 48
    cut = (P - 1) // 16 * 16
    spare = TAIL % TILES
    assert spare > 0
    edges_of_partition = edge_attr[0:(P - 1) * COLS, :].rearrange("(p c) d -> p c d", p=P - 1)

    def load_edges(sp, rows, loaded, scattered):
        def whole_group(i, slot, turn):
            wait(sp, scattered[slot], 64 * turn)
            sp.dma_start(rows[:, slot, :, 0:D],
                         bass.AP(edge_attr.tensor, i * (TILES * D), [[COLS * D, P], [D, TILES], [1, D]])
                         ).then_inc(loaded[slot], PARTS)

        def cut_group(i, slot, turn):
            wait(sp, scattered[slot], 64 * turn)
            here = bass.ds(i * TILES, TILES)
            sp.dma_start(rows[0:cut, slot, :, 0:D], edges_of_partition[0:cut, here, :]).then_inc(loaded[slot], 16)
            sp.dma_start(rows[cut:P - 1, slot, :, 0:D],
                         edges_of_partition[cut:P - 1, here, :]).then_inc(loaded[slot], 16)
            sp.dma_start(rows[P - 1:P, slot, 0:spare, 0:D],
                         edge_attr[E - spare:E, :].unsqueeze(0)).then_inc(loaded[slot], 16)

        pipelined(sp, FULL, [whole_group])
        pipelined(sp, IN_GROUPS, [cut_group], start=FULL)

    HALF = TILES // 2
    BANK = HALF * (KEYS2 + WINDOWS)

    def table_part(tables, n, j):
        at = (j % HALF) * KEYS2 if n else HALF * KEYS2 + (j % HALF) * WINDOWS
        return tables[:, j // HALF, at:at + (KEYS2 if n else WINDOWS)]

    with ExitStack() as st:
        base = sb(st, [P, BANK])
        rows = sb(st, [P, SLOTS, TILES, PAY])
        high = sb(st, [P, SLOTS, TILES])
        hot = sb(st, [P, SLOTS, 2, TILES, P], BF16)
        hot_hi = [sb(st, [P, SLOTS, TILES, n], BF16) for n in (WINDOWS, KEYS2)]
        hot_t = sb(st, [P, BANKS, 2, TILES, P])
        table = sb(st, [P, BANKS, 2, BANK])
        same = sb(st, [P, 2, TILES, P])
        picked = [sb(st, [P, TILES, n]) for n in (WINDOWS, KEYS2)]
        rank = sb(st, [P, SLOTS, 2, TILES])
        found = sb(st, [P, SLOTS, 2, TILES])
        spot = sb(st, [P, SLOTS, 2, TILES])
        nowhere = sb(st, [P, SLOTS, TILES])
        index = sb(st, [P, SLOTS, TILES], I32)
        ps_keys = [ps(st, [P, TILES, P]) for _ in range(2)]
        ps_hot_t = ps(st, [P, 2, TILES, P], BF16)
        ps_table = ps(st, [P, 2, 512])
        ps_found = ps(st, [P, 2, 512])
        loaded = [sem(f"loaded{s}") for s in range(SLOTS)]
        scattered = [gpsimd_dma_sem(f"scattered{s}") for s in range(SLOTS)]
        base_copied = sem("base_copied")
        tagged = sem("tagged")
        hot_ready = sem("hot_ready")
        keys_spread = sem("keys_spread")
        ranked = sem("ranked")
        hot_turned = sem("hot_turned")
        hot_copied = sem("hot_copied")
        table_grown = sem("table_grown")
        table_copied = sem("table_copied")
        looked_up = sem("looked_up")
        found_read = sem("found_read")
        spot_ready = sem("spot_ready")
        index_ready = sem("index_ready")
        begun = sem("begun")
        with nc.Block() as block:

            @block.sync
            def _(sp):
                load_edges(sp, rows, loaded, scattered)

            @block.gpsimd
            def _(pool):
                def scatter(i, slot, turn):
                    pool.wait_ge(index_ready, i + 1)
                    pool.wait_ge(loaded[slot], PARTS * (turn + 1))
                    pool.sem_inc(begun, 1)
                    for j in range(TILES):
                        pool.indirect_dma_start(
                            by_src[:, :], bass.IndirectOffsetOnAxis(ap=index[:, slot, j:j + 1], axis=0),
                            rows[:, slot, j, :], None, bounds_check=NPOS - 1,
                            oob_is_err=False).then_inc(scattered[slot], 16)

                pipelined(pool, IN_GROUPS, [scatter])
                for s in range(SLOTS):
                    pool.wait_ge(scattered[s], 64 * len(range(s, IN_GROUPS, SLOTS)))

            @block.scalar
            def _(act):
                a = nc.scalar

                def tag(i, slot, turn):
                    wait(act, scattered[slot], 64 * turn)
                    a.activation(rows[:, slot, :, D:PAY], tags[:, bass.ds(i * TILES, TILES), :], ACT.Copy)
                    a.activation(high[:, slot, :], hi1[:, bass.ds(i * TILES, TILES)], ACT.Copy).then_inc(tagged, 1)

                def copies(i, slot, turn):
                    act.wait_ge(hot_turned, i + 1)
                    wait(act, looked_up, i - BANKS + 1)
                    a.activation(hot_t[:, slot % BANKS, :, :, :], ps_hot_t[:, :, :, :], ACT.Copy).then_inc(hot_copied, 1)
                    act.wait_ge(table_grown, i + 1)
                    a.activation(table[:, slot % BANKS, :, :], ps_table[:, :, 0:BANK], ACT.Copy).then_inc(table_copied, 1)

                pipelined(act, IN_GROUPS, [tag, None, copies])

            @block.tensor
            def _(pe):
                pe.wait_ge(base_copied, 1)
                for half in range(2):
                    nc.tensor.matmul(ps_table[:, half, 0:BANK], ident[:, :], base[:, :], start=True, stop=True)

                def grow(n, j, slot, k):
                    return nc.tensor.matmul(table_part(ps_table, n, j), hot[:, slot, n, k, :],
                                            hot_hi[n][:, slot, k, :], start=False, stop=True, skip_group_check=True)

                def spread_and_grow(i, slot, turn):
                    pe.wait_ge(tagged, i + 1)
                    wait(pe, ranked, i)
                    for n, key in enumerate((SRC1, SEG2)):
                        for j in range(TILES):
                            last = nc.tensor.transpose(ps_keys[n][:, j, :],
                                                       rows[:, slot, j, D + key:D + key + 1].to_broadcast([P, P]),
                                                       ident[:, :])
                    last.then_inc(keys_spread, 1)
                    pe.wait_ge(hot_ready, i + 1)
                    wait(pe, hot_copied, i)
                    for n in range(2):
                        for j in range(TILES):
                            last = nc.tensor.transpose(ps_hot_t[:, n, j, :], hot[:, slot, n, j, :], ident_bf[:, :])
                    last.then_inc(hot_turned, 1)
                    wait(pe, table_copied, i)
                    for n in range(2):
                        for j in range(TILES):
                            if not (isinstance(i, int) and i == 0):
                                for k in range(j, TILES):
                                    last = grow(n, j, (slot - 1) % SLOTS, k)
                            for k in range(j):
                                last = grow(n, j, slot, k)
                    last.then_inc(table_grown, 1)

                def look_up(i, slot, turn):
                    pe.wait_ge(hot_copied, i + 1)
                    pe.wait_ge(table_copied, i + 1)
                    wait(pe, found_read, i)
                    for n in range(2):
                        for j in range(TILES):
                            last = nc.tensor.matmul(table_part(ps_found, n, j), hot_t[:, slot % BANKS, n, j, :],
                                                    table_part(table[:, slot % BANKS, :, :], n, j),
                                                    start=True, stop=True)
                    last.then_inc(looked_up, 1)

                pipelined(pe, IN_GROUPS, [spread_and_grow, None, look_up])

            @block.vector
            def _(dve):
                v = nc.vector
                for half in range(HALF):
                    v.tensor_copy(base[:, half * KEYS2:(half + 1) * KEYS2], base2[:, :])
                for half in range(HALF):
                    last = v.tensor_copy(base[:, HALF * KEYS2 + half * WINDOWS:HALF * KEYS2 + (half + 1) * WINDOWS],
                                         base1[:, :])
                last.then_inc(base_copied, 1)

                def one_hots(i, slot, turn):
                    dve.wait_ge(tagged, i + 1)
                    wait(dve, table_grown, i - SLOTS + 2)
                    for j in range(TILES):
                        for n, (lo, hi, width) in enumerate((
                                (rows[:, slot, j, D + LO1:D + LO1 + 1], high[:, slot, j:j + 1], WINDOWS),
                                (rows[:, slot, j, D + DLO1:D + DLO1 + 1], rows[:, slot, j, D + HI2:D + HI2 + 1],
                                 KEYS2))):
                            v.tensor_scalar(hot[:, slot, n, j, :], count1_bf[:, 0:P], lo, None, ALU.is_equal)
                            last = v.tensor_scalar(hot_hi[n][:, slot, j, :], count1_bf[:, 0:width], hi, None,
                                                   ALU.is_equal)
                    last.then_inc(hot_ready, 1)

                def ranks(i, slot, turn):
                    dve.wait_ge(keys_spread, i + 1)
                    v.tensor_scalar(nowhere[:, slot, :], high[:, slot, :], 0.5, NOWHERE, ALU.is_lt, ALU.mult)
                    for n, key in enumerate((SRC1, SEG2)):
                        for j in range(TILES):
                            last = v.scalar_tensor_tensor(same[:, n, j, :], ps_keys[n][:, j, :],
                                                          rows[:, slot, j, D + key:D + key + 1], after[:, :],
                                                          ALU.is_equal, ALU.mult,
                                                          accum_out=rank[:, slot, n, j:j + 1])
                    last.then_inc(ranked, 1)

                def positions(i, slot, turn):
                    dve.wait_ge(looked_up, i + 1)
                    for n, width in enumerate((WINDOWS, KEYS2)):
                        for j in range(TILES):
                            last = v.scalar_tensor_tensor(picked[n][:, j, :], table_part(ps_found, n, j), 1.0,
                                                          hot_hi[n][:, slot, j, :], ALU.mult, ALU.mult,
                                                          accum_out=found[:, slot, n, j:j + 1])
                    last.then_inc(found_read, 1)
                    dve.wait_ge(found_read, i + 1)
                    v.tensor_tensor(spot[:, slot, :, :], found[:, slot, :, :], rank[:, slot, :, :],
                                    ALU.add).then_inc(spot_ready, 1)
                    dve.wait_ge(spot_ready, i + 1)
                    v.tensor_scalar(rows[:, slot, :, D + SPOT2], spot[:, slot, 1, :], 1.0, None, ALU.add)
                    v.tensor_tensor(index[:, slot, :], spot[:, slot, 0, :], nowhere[:, slot, :],
                                    ALU.add).then_inc(index_ready, 1)

                pipelined(dve, IN_GROUPS, [one_hots, ranks, positions])
    edges.close()

    by_src_g = by_src.rearrange("(g p j) c -> g p (j c)", p=P, j=TILES)
    values_g = values.rearrange("(g p j) c -> g p j c", p=P, j=TILES)
    scores_g = scores.rearrange("(g p j) c -> g p (j c)", p=P, j=TILES)
    with ExitStack() as st:
        w_e = sb(st, [P, 2, D])
        w_exp = sb(st, [P, HE])
        rows = sb(st, [P, SLOTS, TILES, PAY])
        target = sb(st, [P, SLOTS, TILES], I32)
        kv = sb(st, [P, SLOTS, TILES, KV])
        edge_t = sb(st, [P, SLOTS, GROUP])
        pick = sb(st, [P, SLOTS, GROUP])
        product = sb(st, [P, SLOTS, TILES, D])
        product_t = sb(st, [P, SLOTS, GROUP])
        scored = sb(st, [P, SLOTS, TILES, SROW])
        ps_edge_t = ps(st, [P, GROUP])
        source = sb(st, [P, SLOTS, TILES], BF16)
        ps_pick = ps(st, [P, GROUP], BF16)
        ps_kv = ps(st, [P, TILES, KV])
        ps_q = ps(st, [P, TILES, D])
        ps_product_t = ps(st, [P, GROUP])
        ps_score = ps(st, [P, TILES, HE])
        weights = sem("weights")
        loaded = [sem(f"loaded{s}") for s in range(SLOTS)]
        fetched = [gpsimd_dma_sem(f"fetched{s}") for s in range(SLOTS)]
        stored = [sem(f"stored{s}") for s in range(SLOTS)]
        source_ready = sem("source_ready")
        target_ready = sem("target_ready")
        begun = sem("begun")
        tags_copied = sem("tags_copied")
        edge_turned = sem("edge_turned")
        edge_copied = sem("edge_copied")
        pick_spread = sem("pick_spread")
        pick_ready = sem("pick_ready")
        edge_projected = sem("edge_projected")
        q_fetched = sem("q_fetched")
        kv_ready = sem("kv_ready")
        product_ready = sem("product_ready")
        product_turned = sem("product_turned")
        product_copied = sem("product_copied")
        score_ready = sem("score_ready")
        score_copied = sem("score_copied")
        with nc.Block() as block:

            @block.sync
            def _(sp):
                sp.dma_start(w_e[:, 0, :], Wek).then_inc(weights, 16)
                sp.dma_start(w_e[:, 1, :], Wev).then_inc(weights, 16)
                for h in range(H0):
                    width = D // H0
                    sp.dma_start(w_exp[h * width:(h + 1) * width, :],
                                 Wexp[h:h + 1, :].to_broadcast([width, HE])).then_inc(weights, 16)

                def load(i, slot, turn):
                    wait(sp, edge_turned, i - SLOTS + 1)
                    wait(sp, source_ready, i - SLOTS + 1)
                    wait(sp, tags_copied, i - SLOTS + 1)
                    sp.dma_start(rows[:, slot, :, :].rearrange("p j c -> p (j c)"),
                                 by_src_g[bass.ds(i, 1), :, :].rearrange("a p c -> (a p) c")
                                 ).then_inc(loaded[slot], 16)

                def store(i, slot, turn):
                    sp.wait_ge(kv_ready, i + 1)
                    sp.dma_start(values_g[bass.ds(i, 1), :, :, :].rearrange("a p j c -> (a p) j c"),
                                 kv[:, slot, :, D:KV]).then_inc(stored[slot], 16)
                    sp.wait_ge(score_copied, i + 1)
                    sp.wait_ge(tags_copied, i + 1)
                    sp.dma_start(scores_g[bass.ds(i, 1), :, :].rearrange("a p c -> (a p) c"),
                                 scored[:, slot, :, :].rearrange("p j c -> p (j c)")).then_inc(stored[slot], 16)

                pipelined(sp, GROUPS, [load, None, None, None, store])
                for s in range(SLOTS):
                    sp.wait_ge(stored[s], 32 * len(range(s, GROUPS, SLOTS)))

            @block.gpsimd
            def _(pool):
                def fetch(i, slot, turn):
                    pool.wait_ge(target_ready, i + 1)
                    wait(pool, stored[slot], 32 * turn)
                    wait(pool, product_ready, i - SLOTS + 1)
                    pool.sem_inc(begun, 1)
                    for j in range(TILES):
                        pool.indirect_dma_start(
                            kv[:, slot, j, :], None, kv_table[:, :],
                            bass.IndirectOffsetOnAxis(ap=target[:, slot, j:j + 1], axis=0)).then_inc(fetched[slot], 16)

                pipelined(pool, GROUPS, [fetch])

            @block.scalar
            def _(act):
                a = nc.scalar

                def early(i, slot, turn):
                    act.wait_ge(loaded[slot], 16 * (turn + 1))
                    wait(act, fetched[slot], 64 * turn)
                    a.activation(target[:, slot, :], rows[:, slot, :, D + DST], ACT.Copy).then_inc(target_ready, 1)
                    wait(act, pick_spread, i - SLOTS + 1)
                    a.activation(source[:, slot, :], rows[:, slot, :, D + LO1], ACT.Copy).then_inc(source_ready, 1)
                    wait(act, stored[slot], 32 * turn)
                    a.activation(scored[:, slot, :, HE:SROW], rows[:, slot, :, D:PAY], ACT.Copy).then_inc(tags_copied, 1)
                    act.wait_ge(edge_turned, i + 1)
                    wait(act, edge_projected, i - SLOTS + 1)
                    a.activation(edge_t[:, slot, :], ps_edge_t[:, :], ACT.Copy).then_inc(edge_copied, 1)

                def late(i, slot, turn):
                    act.wait_ge(product_turned, i + 1)
                    wait(act, score_ready, i - SLOTS + 1)
                    a.activation(product_t[:, slot, :], ps_product_t[:, :], ACT.Copy).then_inc(product_copied, 1)

                def keep_scores(i, slot, turn):
                    act.wait_ge(score_ready, i + 1)
                    a.activation(scored[:, slot, :, 0:HE], ps_score[:, :, :], ACT.Copy,
                                 scale=SCALE).then_inc(score_copied, 1)

                pipelined(act, GROUPS, [early, None, late, keep_scores])

            @block.vector
            def _(dve):
                v = nc.vector

                def choose(i, slot, turn):
                    dve.wait_ge(pick_spread, i + 1)
                    wait(dve, q_fetched, i - SLOTS + 1)
                    v.tensor_scalar(pick[:, slot, :], ps_pick[:, :], row1[:, 0:1], None,
                                    ALU.is_equal).then_inc(pick_ready, 1)

                def combine(i, slot, turn):
                    dve.wait_ge(fetched[slot], 64 * (turn + 1))
                    dve.wait_ge(edge_projected, i + 1)
                    v.tensor_tensor(kv[:, slot, :, :], kv[:, slot, :, :], ps_kv[:, :, :], ALU.add).then_inc(kv_ready, 1)
                    dve.wait_ge(kv_ready, i + 1)
                    dve.wait_ge(q_fetched, i + 1)
                    wait(dve, product_turned, i - SLOTS + 1)
                    v.tensor_tensor(product[:, slot, :, :], kv[:, slot, :, 0:D], ps_q[:, :, :],
                                    ALU.mult).then_inc(product_ready, 1)

                pipelined(dve, GROUPS, [choose, combine])

            @block.tensor
            def _(pe):
                pe.wait_ge(weights, (2 + H0) * 16)

                def turn_edges(i, slot, turn):
                    pe.wait_ge(source_ready, i + 1)
                    wait(pe, pick_ready, i)
                    for j in range(TILES):
                        last = nc.tensor.transpose(ps_pick[:, j * P:(j + 1) * P],
                                                   source[:, slot, j:j + 1].to_broadcast([P, P]), ident_bf[:, :])
                    last.then_inc(pick_spread, 1)
                    wait(pe, edge_copied, i)
                    for j in range(TILES):
                        last = nc.tensor.transpose(ps_edge_t[:, j * P:(j + 1) * P], rows[:, slot, j, 0:D], ident[:, :])
                    last.then_inc(edge_turned, 1)

                def project(i, slot, turn):
                    w = window_of(pe, window1, i)
                    pe.wait_ge(edge_copied, i + 1)
                    wait(pe, kv_ready, i)
                    for j in range(TILES):
                        last = nc.tensor.matmul(ps_kv[:, j, :], edge_t[:, slot, j * P:(j + 1) * P],
                                                w_e[:, :, :].rearrange("p a d -> p (a d)"), start=True, stop=True)
                    last.then_inc(edge_projected, 1)
                    pe.wait_ge(pick_ready, i + 1)
                    wait(pe, product_ready, i)
                    for j in range(TILES):
                        last = nc.tensor.matmul(ps_q[:, j, :], pick[:, slot, j * P:(j + 1) * P],
                                                q_sb[:, bass.ds(w, 1), :].rearrange("p a d -> p (a d)"),
                                                start=True, stop=True)
                    last.then_inc(q_fetched, 1)

                def turn_product(i, slot, turn):
                    pe.wait_ge(product_ready, i + 1)
                    wait(pe, product_copied, i)
                    for j in range(TILES):
                        last = nc.tensor.transpose(ps_product_t[:, j * P:(j + 1) * P], product[:, slot, j, :],
                                                   ident[:, :])
                    last.then_inc(product_turned, 1)

                def score(i, slot, turn):
                    pe.wait_ge(product_copied, i + 1)
                    wait(pe, score_copied, i)
                    for j in range(TILES):
                        last = nc.tensor.matmul(ps_score[:, j, :], product_t[:, slot, j * P:(j + 1) * P],
                                                w_exp[:, :], start=True, stop=True)
                    last.then_inc(score_ready, 1)

                pipelined(pe, GROUPS, [turn_edges, project, turn_product, score])
    tables0.close()

    def segment_softmax(table, width, heads, seg, self_minus):
        in_runs = table.rearrange("(p t) c -> p t c", p=P)
        flat = table.rearrange("(p t) c -> p (t c)", p=P)
        with ExitStack() as st:
            data = sb(st, [P, RUN, width])
            seg_before = sb(st, [P, 1])
            seg_behind = sb(st, [P, 1])
            same_f = sb(st, [P, RUN])
            same_b = sb(st, [P, RUN])
            low_f = sb(st, [P, RUN])
            low_b = sb(st, [P, RUN])
            fwd = sb(st, [P, RUN])
            bwd = sb(st, [P, RUN])
            ends = sb(st, [P, 4, heads])
            ends_t = sb(st, [heads, 4, P])
            through = sb(st, [P, 4])
            chain = sb(st, [heads, 2, P])
            carry_t = sb(st, [heads, 2, P])
            carry = sb(st, [P, 2, heads])
            ps_ends = ps(st, [heads, 4, P])
            ps_carry = ps(st, [P, 2, heads])
            filled = sem("filled")
            loaded = sem("loaded")
            stored = sem("stored")
            step = sem("step")
            ends_ready = sem("ends_ready")
            ends_turned = sem("ends_turned")
            carry_ready = sem("carry_ready")
            carry_turned = sem("carry_turned")
            shifted = sem("shifted")
            exponent = sem("exponent")
            weights_ready = sem("weights_ready")
            with nc.Block() as block:

                @block.sync
                def _(sp):
                    sp.dma_start(data[:, :, :].rearrange("p t c -> p (t c)"), flat).then_inc(loaded, 16)
                    sp.wait_ge(filled, 1)
                    sp.dma_start(seg_before[1:P, :], in_runs[0:P - 1, RUN - 1, seg:seg + 1],
                                 allow_slow_non_contiguous=True).then_inc(loaded, 16)
                    sp.dma_start(seg_behind[0:P - 1, :], in_runs[1:P, 0, seg:seg + 1],
                                 allow_slow_non_contiguous=True).then_inc(loaded, 16)
                    sp.wait_ge(weights_ready, heads)
                    sp.dma_start(flat, data[:, :, :].rearrange("p t c -> p (t c)")).then_inc(stored, 16)
                    sp.wait_ge(stored, 16)

                @block.tensor
                def _(pe):
                    for n in range(2):
                        pe.wait_ge(ends_ready, n + 1)
                        for k in range(4):
                            last = nc.tensor.transpose(ps_ends[:, k, :], ends[:, k, :], ident[:, :])
                        last.then_inc(ends_turned, 1)
                        pe.wait_ge(carry_ready, n + 1)
                        for k in range(2):
                            last = nc.tensor.transpose(ps_carry[:, k, :], carry_t[:, k, :], ident[0:heads, 0:heads])
                        last.then_inc(carry_turned, 1)

                @block.scalar
                def _(act):
                    for h in range(heads):
                        act.wait_ge(shifted, h + 1)
                        nc.scalar.activation(data[:, :, h], data[:, :, h], ACT.Exp).then_inc(exponent, 1)

                @block.vector
                def _(dve):
                    done = [0]

                    def then(instruction):
                        done[0] += 1
                        instruction.then_inc(step, 1)
                        dve.wait_ge(step, done[0])

                    v = nc.vector
                    v.memset(seg_before[:, :], -1.0)
                    v.memset(seg_behind[:, :], -1.0).then_inc(filled, 1)
                    dve.wait_ge(loaded, 3 * 16)
                    segs = data[:, :, seg]
                    v.tensor_tensor(same_f[:, 0:1], segs[:, 0:1], seg_before[:, :], ALU.is_equal)
                    v.tensor_tensor(same_f[:, 1:RUN], segs[:, 1:RUN], segs[:, 0:RUN - 1], ALU.is_equal)
                    v.tensor_tensor(same_b[:, RUN - 1:RUN], segs[:, RUN - 1:RUN], seg_behind[:, :], ALU.is_equal)
                    then(v.tensor_tensor(same_b[:, 0:RUN - 1], segs[:, 0:RUN - 1], segs[:, 1:RUN], ALU.is_equal))
                    v.tensor_scalar(low_f[:, :], same_f[:, :], 1.0, -LOW, ALU.subtract, ALU.mult)
                    v.tensor_scalar(low_b[:, :], same_b[:, :], 1.0, -LOW, ALU.subtract, ALU.mult)
                    v.tensor_reduce(through[:, 2:3], same_f[:, :], AX_X, ALU.min)
                    then(v.tensor_reduce(through[:, 3:4], same_b[:, :], AX_X, ALU.min))
                    then(v.tensor_scalar(through[:, 0:2], through[:, 2:4], 1.0, -LOW, ALU.subtract, ALU.mult))

                    def scans(h, flags, start, op, first, second):
                        v.tensor_tensor_scan(fwd[:, :], flags[0][:, :], data[:, :, h], first, op[0], op[1])
                        then(v.tensor_tensor_scan(bwd[:, ::-1], flags[1][:, ::-1], data[:, ::-1, h], second,
                                                  op[0], op[1]))

                    for n, (flags, start, op) in enumerate((
                            ((low_f, low_b), LOW, (ALU.add, ALU.max)),
                            ((same_f, same_b), 0.0, (ALU.mult, ALU.add)))):
                        for h in range(heads):
                            if n == 1:
                                dve.wait_ge(exponent, h + 1)
                            scans(h, flags, start, op, start, start)
                            v.tensor_copy(ends[:, 0, h:h + 1], fwd[:, RUN - 1:RUN])
                            then(v.tensor_copy(ends[:, 1, h:h + 1], bwd[:, 0:1]))
                        v.tensor_copy(ends[:, 2, :], through[:, 2 * n:2 * n + 1].to_broadcast([P, heads]))
                        v.tensor_copy(ends[:, 3, :], through[:, 2 * n + 1:2 * n + 2].to_broadcast([P, heads])
                                      ).then_inc(ends_ready, 1)
                        dve.wait_ge(ends_turned, n + 1)
                        then(v.tensor_copy(ends_t[:, :, :], ps_ends[:, :, :]))
                        v.tensor_tensor_scan(chain[:, 0, :], ends_t[:, 2, :], ends_t[:, 0, :], start, op[0], op[1])
                        v.tensor_tensor_scan(chain[:, 1, ::-1], ends_t[:, 3, ::-1], ends_t[:, 1, ::-1], start,
                                             op[0], op[1])
                        then(v.memset(carry_t[:, :, :], start))
                        v.tensor_copy(carry_t[:, 0, 1:P], chain[:, 0, 0:P - 1])
                        v.tensor_copy(carry_t[:, 1, 0:P - 1], chain[:, 1, 1:P]).then_inc(carry_ready, 1)
                        dve.wait_ge(carry_turned, n + 1)
                        then(v.tensor_copy(carry[:, :, :], ps_carry[:, :, :]))
                        if n == 1 and self_minus:
                            then(v.scalar_tensor_tensor(low_f[:, :], data[:, :, HE + DST], 1.0,
                                                        data[:, :, HE + SRC1], ALU.add, ALU.is_equal))
                        for h in range(heads):
                            scans(h, flags, start, op, carry[:, 0, h:h + 1], carry[:, 1, h:h + 1])
                            if n == 0:
                                then(v.tensor_tensor(fwd[:, :], fwd[:, :], bwd[:, :], ALU.max))
                                v.tensor_tensor(data[:, :, h], data[:, :, h], fwd[:, :],
                                                ALU.subtract).then_inc(shifted, 1)
                                dve.wait_ge(shifted, h + 1)
                            else:
                                then(v.tensor_tensor(bwd[:, :], bwd[:, :], data[:, :, h], ALU.subtract))
                                then(v.tensor_tensor(fwd[:, :], fwd[:, :], bwd[:, :], ALU.add))
                                then(v.reciprocal(fwd[:, :], fwd[:, :]))
                                last = v.tensor_tensor(data[:, :, h], data[:, :, h], fwd[:, :], ALU.mult)
                                if self_minus:
                                    then(last)
                                    last = v.tensor_tensor(data[:, :, h], low_f[:, :], data[:, :, h], ALU.subtract)
                                last.then_inc(weights_ready, 1)
                                dve.wait_ge(weights_ready, h + 1)

    def weighted_sums(total, value_groups, weight_groups, width, heads, lo, window):
        with ExitStack() as st:
            value = sb(st, [P, SLOTS, TILES, D])
            weight = sb(st, [P, SLOTS, TILES, width])
            pick = sb(st, [P, SLOTS, TILES, P])
            ps_sum = [ps(st, [P, 512]) for _ in range(BANKS)]
            loaded = [sem(f"loaded{s}") for s in range(SLOTS)]
            weighted = sem("weighted")
            pick_ready = sem("pick_ready")
            summed = sem("summed")
            added = sem("added")
            cleared = sem("cleared")
            with nc.Block() as block:

                @block.sync
                def _(sp):
                    def load(i, slot, turn):
                        wait(sp, summed, i - SLOTS + 1)
                        sp.dma_start(value[:, slot, :, :], value_groups(i)).then_inc(loaded[slot], 16)
                        sp.dma_start(weight[:, slot, :, :].rearrange("p j c -> p (j c)"),
                                     weight_groups[bass.ds(i, 1), :, :].rearrange("a p c -> (a p) c")
                                     ).then_inc(loaded[slot], 16)

                    pipelined(sp, GROUPS, [load])

                @block.gpsimd
                def _(pool):
                    def weigh(i, slot, turn):
                        pool.wait_ge(loaded[slot], 32 * (turn + 1))
                        by_head = value[:, slot, :, :].rearrange("p j (h d) -> p j h d", h=heads)
                        pool.tensor_tensor(by_head, by_head,
                                           weight[:, slot, :, 0:heads].unsqueeze(3)
                                           .to_broadcast([P, TILES, heads, D // heads]), ALU.mult).then_inc(weighted, 1)

                    pipelined(pool, GROUPS, [weigh])

                @block.vector
                def _(dve):
                    v = nc.vector
                    v.memset(total[:, :, :], 0.0).then_inc(cleared, 1)
                    dve.wait_ge(cleared, 1)

                    def choose(i, slot, turn):
                        dve.wait_ge(loaded[slot], 32 * (turn + 1))
                        wait(dve, summed, i - SLOTS + 1)
                        v.tensor_tensor(pick[:, slot, :, :],
                                        weight[:, slot, :, lo:lo + 1].to_broadcast([P, TILES, P]),
                                        count1[:, :].unsqueeze(1).to_broadcast([P, TILES, P]),
                                        ALU.is_equal).then_inc(pick_ready, 1)

                    def add(i, slot, turn):
                        w = window_of(dve, window, i)
                        dve.wait_ge(summed, i + 1)
                        wait(dve, added, i)
                        here = total[:, bass.ds(w, 1), :].rearrange("p a d -> p (a d)")
                        v.tensor_tensor(here, here, ps_sum[slot % BANKS][:, 0:D], ALU.add).then_inc(added, 1)

                    pipelined(dve, GROUPS, [choose, add])

                @block.tensor
                def _(pe):
                    def add_up(i, slot, turn):
                        pe.wait_ge(weighted, i + 1)
                        pe.wait_ge(pick_ready, i + 1)
                        wait(pe, added, i - BANKS + 1)
                        for j in range(TILES):
                            last = nc.tensor.matmul(ps_sum[slot % BANKS][:, 0:D], pick[:, slot, j, :], value[:, slot, j, :],
                                                    start=(j == 0), stop=(j == TILES - 1))
                        last.then_inc(summed, 1)

                    pipelined(pe, GROUPS, [add_up])

    segment_softmax(scores, SROW, HE, HE + SRC1, True)

    tables1 = ExitStack()
    features = sb(tables1, [P, WINDOWS, R, FEAT])
    dst_score = sb(tables1, [P, WINDOWS, R * H1])
    with ExitStack() as sums:
        total = sb(sums, [P, WINDOWS, D])

        def values_of(i):
            return values_g[bass.ds(i, 1), :, :, :].rearrange("a p j c -> (a p) j c")

        weighted_sums(total, values_of, scores_g, SROW, HE, HE + LO1, window1)

        with ExitStack() as st:
            w_out = sb(st, [P, D])
            b_out = sb(st, [1, D])
            rows = sb(st, [P, SLOTS, D])
            rows_t = sb(st, [P, SLOTS, P])
            ps_t = [ps(st, [P, 512]) for _ in range(BANKS)]
            ps_out = [ps(st, [P, 512]) for _ in range(BANKS)]
            weights = sem("weights")
            copied = sem("copied")
            turned = sem("turned")
            turned_copied = sem("turned_copied")
            projected = sem("projected")
            added = sem("added")
            with nc.Block() as block:

                @block.sync
                def _(sp):
                    sp.dma_start(w_out[:, :], Wout).then_inc(weights, 16)
                    sp.dma_start(b_out[:, :], bout.rearrange("(a d) -> a d", a=1)).then_inc(weights, 16)

                @block.scalar
                def _(act):
                    def copy_rows(i, slot, turn):
                        wait(act, turned, i - SLOTS + 1)
                        nc.scalar.activation(rows[:, slot, :], total[:, bass.ds(i, 1), :].rearrange("p a d -> p (a d)"),
                                             ACT.Copy).then_inc(copied, 1)

                    def copy_turned(i, slot, turn):
                        act.wait_ge(turned, i + 1)
                        wait(act, projected, i - SLOTS + 1)
                        nc.scalar.activation(rows_t[:, slot, :], ps_t[slot % BANKS][:, 0:P], ACT.Copy).then_inc(turned_copied, 1)

                    pipelined(act, WINDOWS, [copy_rows, copy_turned])

                @block.tensor
                def _(pe):
                    pe.wait_ge(weights, 32)

                    def turn_rows(i, slot, turn):
                        pe.wait_ge(copied, i + 1)
                        wait(pe, turned_copied, i - BANKS + 1)
                        nc.tensor.transpose(ps_t[slot % BANKS][:, 0:P], rows[:, slot, :], ident[:, :]).then_inc(turned, 1)

                    def project(i, slot, turn):
                        pe.wait_ge(turned_copied, i + 1)
                        wait(pe, added, i - BANKS + 1)
                        nc.tensor.matmul(ps_out[slot % BANKS][:, 0:D], rows_t[:, slot, :], w_out[:, :], start=True, stop=False)
                        nc.tensor.matmul(ps_out[slot % BANKS][:, 0:D], ones[0:1, :], b_out[:, :], start=False,
                                         stop=True).then_inc(projected, 1)

                    pipelined(pe, WINDOWS, [turn_rows, project])

                @block.vector
                def _(dve):
                    def add(i, slot, turn):
                        dve.wait_ge(projected, i + 1)
                        here = x_sb[:, bass.ds(i, 1), :].rearrange("p a d -> p (a d)")
                        nc.vector.tensor_tensor(here, here, ps_out[slot % BANKS][:, 0:D], ALU.add).then_inc(added, 1)

                    pipelined(dve, WINDOWS, [add])

    with ExitStack() as st:
        hn = sb(st, [P, WINDOWS, D])
        layernorm_relu_input(hn)
        w_all = sb(st, [P, R, D])
        attn_all = sb(st, [P, R * H1, 2 * HD1])
        h = sb(st, [P, SLOTS, D])
        h_t = sb(st, [P, SLOTS, P])
        product = sb(st, [P, 2, R * H1, HD1])
        ps_t = [ps(st, [P, 512]) for _ in range(BANKS)]
        ps_feat = [ps(st, [P, R, D]) for _ in range(BANKS)]
        weights = sem("weights")
        relu_done = sem("relu_done")
        turned = sem("turned")
        turned_copied = sem("turned_copied")
        projected = sem("projected")
        product_ready = sem("product_ready")
        scored = sem("scored")
        kept = sem("kept")
        with nc.Block() as block:

            @block.sync
            def _(sp):
                for r in range(R):
                    sp.dma_start(w_all[:, r, :], W_rel[r, :, :]).then_inc(weights, 16)
                sp.dma_start(attn_all[:, :, :].rearrange("p a b -> p (a b)"),
                             attn.rearrange("(o a) b c -> o (a b c)", o=1).to_broadcast([P, R * H1 * 2 * HD1])
                             ).then_inc(weights, 16)

            @block.scalar
            def _(act):
                def rectify(i, slot, turn):
                    wait(act, turned, i - SLOTS + 1)
                    nc.scalar.activation(h[:, slot, :], hn[:, bass.ds(i, 1), :].rearrange("p a d -> p (a d)"),
                                         ACT.Relu).then_inc(relu_done, 1)

                def copy_turned(i, slot, turn):
                    act.wait_ge(turned, i + 1)
                    wait(act, projected, i - SLOTS + 1)
                    nc.scalar.activation(h_t[:, slot, :], ps_t[slot % BANKS][:, 0:P], ACT.Copy).then_inc(turned_copied, 1)

                def keep(i, slot, turn):
                    act.wait_ge(projected, i + 1)
                    nc.scalar.activation(features[:, bass.ds(i, 1), :, 0:D].rearrange("p a r d -> p (a r) d"),
                                         ps_feat[slot % BANKS][:, :, :], ACT.Copy).then_inc(kept, 1)

                pipelined(act, WINDOWS, [rectify, copy_turned, keep])

            @block.tensor
            def _(pe):
                pe.wait_ge(weights, (R + 1) * 16)

                def turn_h(i, slot, turn):
                    pe.wait_ge(relu_done, i + 1)
                    wait(pe, turned_copied, i - BANKS + 1)
                    nc.tensor.transpose(ps_t[slot % BANKS][:, 0:P], h[:, slot, :], ident[:, :]).then_inc(turned, 1)

                def project(i, slot, turn):
                    pe.wait_ge(turned_copied, i + 1)
                    wait(pe, kept, i - BANKS + 1)
                    wait(pe, scored, i - BANKS + 1)
                    nc.tensor.matmul(ps_feat[slot % BANKS][:, :, :].rearrange("p r d -> p (r d)"), h_t[:, slot, :],
                                     w_all[:, :, :].rearrange("p r d -> p (r d)"), start=True,
                                     stop=True).then_inc(projected, 1)

                pipelined(pe, WINDOWS, [turn_h, project])

            @block.vector
            def _(dve):
                v = nc.vector
                dve.wait_ge(weights, (R + 1) * 16)

                def score(i, slot, turn):
                    dve.wait_ge(kept, i + 1)
                    wait(dve, scored, i)
                    feat = ps_feat[slot % BANKS][:, :, :].rearrange("p r (h d) -> p (r h) d", h=H1)
                    v.tensor_tensor(product[:, 0, :, :], feat, attn_all[:, :, 0:HD1], ALU.mult)
                    v.tensor_tensor(product[:, 1, :, :], feat, attn_all[:, :, HD1:2 * HD1],
                                    ALU.mult).then_inc(product_ready, 1)
                    dve.wait_ge(product_ready, i + 1)
                    v.tensor_reduce(features[:, bass.ds(i, 1), :, D:FEAT].rearrange("p a r h -> p (a r) h"),
                                    product[:, 0, :, :].rearrange("p (r h) d -> p r h d", h=H1), AX_X, ALU.add)
                    v.tensor_reduce(dst_score[:, bass.ds(i, 1), :].rearrange("p a c -> p (a c)"),
                                    product[:, 1, :, :], AX_X, ALU.add).then_inc(scored, 1)

                pipelined(dve, WINDOWS, [score])

    fresh_semaphores()

    with ExitStack() as st:
        tag_rows = sb(st, [P, SLOTS, TILES, SROW])
        sources = sb(st, [P, BANKS, GROUP])
        pick = sb(st, [P, 2, R, GROUP])
        rows = sb(st, [P, SLOTS, TILES, YROW])
        nowhere = sb(st, [P, SLOTS, TILES])
        index = sb(st, [P, SLOTS, TILES], I32)
        ps_pick = [ps(st, [P, GROUP]) for _ in range(2)]
        ps_feat = [ps(st, [P, TILES, 256]) for _ in range(2)]
        loaded = [sem(f"loaded{s}") for s in range(SLOTS)]
        scattered = [gpsimd_dma_sem(f"scattered{s}") for s in range(SLOTS)]
        sources_spread = sem("sources_spread")
        sources_copied = sem("sources_copied")
        pick_ready = sem("pick_ready")
        feat_ready = sem("feat_ready")
        tags_kept = sem("tags_kept")
        feat_kept = sem("feat_kept")
        nowhere_ready = sem("nowhere_ready")
        index_ready = sem("index_ready")
        begun = sem("begun")
        with nc.Block() as block:

            @block.sync
            def _(sp):
                def load(i, slot, turn):
                    wait(sp, tags_kept, i - SLOTS + 1)
                    wait(sp, index_ready, i - SLOTS + 1)
                    wait(sp, sources_spread, i - SLOTS + 1)
                    sp.dma_start(tag_rows[:, slot, :, :].rearrange("p j c -> p (j c)"),
                                 scores_g[bass.ds(i, 1), :, :].rearrange("a p c -> (a p) c")).then_inc(loaded[slot], 16)

                pipelined(sp, GROUPS, [load], SLOTS)

            @block.gpsimd
            def _(pool):
                def scatter(i, slot, turn):
                    pool.wait_ge(index_ready, i + 1)
                    pool.wait_ge(feat_kept, i + 1)
                    pool.sem_inc(begun, 1)
                    for j in range(TILES):
                        pool.indirect_dma_start(
                            by_dst[:, :], bass.IndirectOffsetOnAxis(ap=index[:, slot, j:j + 1], axis=0),
                            rows[:, slot, j, :], None, bounds_check=NPOS - 1,
                            oob_is_err=False).then_inc(scattered[slot], 16)

                pipelined(pool, GROUPS, [scatter])
                for s in range(SLOTS):
                    pool.wait_ge(scattered[s], 64 * len(range(s, GROUPS, SLOTS)))

            @block.tensor
            def _(pe):
                def spread(i, slot, turn):
                    pe.wait_ge(loaded[slot], 16 * (turn + 1))
                    wait(pe, sources_copied, i - 1)
                    for j in range(TILES):
                        last = nc.tensor.transpose(
                            ps_pick[slot % 2][:, j * P:(j + 1) * P],
                            tag_rows[:, slot, j, HE + KEY1:HE + KEY1 + 1].to_broadcast([P, P]), ident[:, :])
                    last.then_inc(sources_spread, 1)

                def fetch(i, slot, turn):
                    w = window_of(pe, window1, i)
                    pe.wait_ge(pick_ready, i + 1)
                    wait(pe, feat_kept, i - 1)
                    for j in range(TILES):
                        for t in range(R):
                            last = nc.tensor.matmul(ps_feat[slot % 2][:, j, 0:FEAT],
                                                    pick[:, slot % 2, t, j * P:(j + 1) * P],
                                                    features[:, bass.ds(w, 1), t, :].rearrange("p a c -> p (a c)"),
                                                    start=(t == 0), stop=(t == R - 1))
                    last.then_inc(feat_ready, 1)

                pipelined(pe, GROUPS, [spread, None, fetch])

            @block.scalar
            def _(act):
                def keep_tags(i, slot, turn):
                    act.wait_ge(loaded[slot], 16 * (turn + 1))
                    wait(act, scattered[slot], 64 * turn)
                    nc.scalar.activation(rows[:, slot, :, FEAT:YROW], tag_rows[:, slot, :, SROW - 4:SROW],
                                         ACT.Copy).then_inc(tags_kept, 1)
                    act.wait_ge(sources_spread, i + 1)
                    wait(act, pick_ready, i - BANKS + 1)
                    nc.scalar.activation(sources[:, slot % BANKS, :], ps_pick[slot % 2][:, :],
                                         ACT.Copy).then_inc(sources_copied, 1)

                def keep_features(i, slot, turn):
                    act.wait_ge(feat_ready, i + 1)
                    nc.scalar.activation(rows[:, slot, :, 0:FEAT], ps_feat[slot % 2][:, :, 0:FEAT],
                                         ACT.Copy).then_inc(feat_kept, 1)

                pipelined(act, GROUPS, [keep_tags, None, keep_features])

            @block.vector
            def _(dve):
                v = nc.vector

                def choose(i, slot, turn):
                    dve.wait_ge(sources_copied, i + 1)
                    wait(dve, feat_ready, i - 1)
                    for t in range(R):
                        last = v.tensor_scalar(pick[:, slot % 2, t, :], sources[:, slot % BANKS, :], row1[:, t:t + 1],
                                               None, ALU.is_equal)
                    last.then_inc(pick_ready, 1)
                    spot = tag_rows[:, slot, :, HE + SPOT2]
                    wait(dve, scattered[slot], 64 * turn)
                    v.tensor_scalar(nowhere[:, slot, :], spot, 0.5, NOWHERE, ALU.is_lt, ALU.mult).then_inc(nowhere_ready, 1)
                    dve.wait_ge(nowhere_ready, i + 1)
                    v.scalar_tensor_tensor(index[:, slot, :], spot, -1.0, nowhere[:, slot, :], ALU.add,
                                           ALU.add).then_inc(index_ready, 1)

                pipelined(dve, GROUPS, [choose])

    by_dst_g = by_dst.rearrange("(g p j) c -> g p (j c)", p=P, j=TILES)
    by_dst_rows = by_dst.rearrange("(g p j) c -> g p j c", p=P, j=TILES)
    alphas_g = alphas.rearrange("(g p j) c -> g p (j c)", p=P, j=TILES)
    Y_DLO1, Y_TYPE, Y_SEG = 1, 2, 3
    with ExitStack() as st:
        rows = sb(st, [P, SLOTS, TILES, H1 + 4])
        pick = sb(st, [P, SLOTS, GROUP])
        type_hot = sb(st, [P, SLOTS, TILES, R])
        chosen = sb(st, [P, SLOTS, TILES, R, H1])
        alpha = sb(st, [P, SLOTS, TILES, H1])
        both = sb(st, [P, SLOTS, TILES, H1])
        result = sb(st, [P, SLOTS, TILES, ZROW])
        ps_pick = [ps(st, [P, GROUP]) for _ in range(BANKS)]
        ps_score = [ps(st, [P, TILES, R * H1]) for _ in range(BANKS)]
        loaded = [sem(f"loaded{s}") for s in range(SLOTS)]
        stored = [sem(f"stored{s}") for s in range(SLOTS)]
        pick_spread = sem("pick_spread")
        pick_ready = sem("pick_ready")
        dst_ready = sem("dst_ready")
        step = sem("step")
        result_ready = sem("result_ready")
        tags_kept = sem("tags_kept")
        with nc.Block() as block:

            @block.sync
            def _(sp):
                def load(i, slot, turn):
                    wait(sp, result_ready, i - SLOTS + 1)
                    wait(sp, tags_kept, i - SLOTS + 1)
                    sp.dma_start(rows[:, slot, :, :],
                                 by_dst_rows[bass.ds(i, 1), :, :, D:YROW].rearrange("a p j c -> (a p) j c")
                                 ).then_inc(loaded[slot], 16)

                def store(i, slot, turn):
                    sp.wait_ge(result_ready, i + 1)
                    sp.wait_ge(tags_kept, i + 1)
                    sp.dma_start(alphas_g[bass.ds(i, 1), :, :].rearrange("a p c -> (a p) c"),
                                 result[:, slot, :, :].rearrange("p j c -> p (j c)")).then_inc(stored[slot], 16)

                pipelined(sp, GROUPS, [load, None, None, None, store])
                for s in range(SLOTS):
                    sp.wait_ge(stored[s], 16 * len(range(s, GROUPS, SLOTS)))

            @block.scalar
            def _(act):
                def keep_tags(i, slot, turn):
                    act.wait_ge(loaded[slot], 16 * (turn + 1))
                    wait(act, stored[slot], 16 * turn)
                    nc.scalar.activation(result[:, slot, :, H1:ZROW], rows[:, slot, :, H1:H1 + 4],
                                         ACT.Copy).then_inc(tags_kept, 1)

                pipelined(act, GROUPS, [keep_tags])

            @block.tensor
            def _(pe):
                def spread(i, slot, turn):
                    pe.wait_ge(loaded[slot], 16 * (turn + 1))
                    wait(pe, pick_ready, i - BANKS + 1)
                    for j in range(TILES):
                        last = nc.tensor.transpose(ps_pick[slot % BANKS][:, j * P:(j + 1) * P],
                                                   rows[:, slot, j, H1 + Y_DLO1:H1 + Y_DLO1 + 1].to_broadcast([P, P]),
                                                   ident[:, :])
                    last.then_inc(pick_spread, 1)

                def fetch(i, slot, turn):
                    w = window_of(pe, window2, i)
                    pe.wait_ge(pick_ready, i + 1)
                    wait(pe, result_ready, i - BANKS + 1)
                    for j in range(TILES):
                        last = nc.tensor.matmul(ps_score[slot % BANKS][:, j, :], pick[:, slot, j * P:(j + 1) * P],
                                                dst_score[:, bass.ds(w, 1), :].rearrange("p a c -> p (a c)"),
                                                start=True, stop=True)
                    last.then_inc(dst_ready, 1)

                pipelined(pe, GROUPS, [spread, fetch])

            @block.vector
            def _(dve):
                v = nc.vector

                def choose(i, slot, turn):
                    dve.wait_ge(pick_spread, i + 1)
                    wait(dve, dst_ready, i - SLOTS + 1)
                    v.tensor_tensor(type_hot[:, slot, :, :],
                                    rows[:, slot, :, H1 + Y_TYPE:H1 + Y_TYPE + 1].to_broadcast([P, TILES, R]),
                                    count0[:, :].unsqueeze(1).to_broadcast([P, TILES, R]), ALU.is_equal)
                    v.tensor_scalar(pick[:, slot, :], ps_pick[slot % BANKS][:, :], row1[:, 0:1], None,
                                    ALU.is_equal).then_inc(pick_ready, 1)

                def score(i, slot, turn):
                    dve.wait_ge(dst_ready, i + 1)
                    v.tensor_tensor(chosen[:, slot, :, :, :],
                                    ps_score[slot % BANKS][:, :, :].rearrange("p j (r h) -> p j r h", r=R),
                                    type_hot[:, slot, :, :].unsqueeze(3).to_broadcast([P, TILES, R, H1]),
                                    ALU.mult).then_inc(step, 1)
                    dve.wait_ge(step, i * 3 + 1)
                    v.tensor_reduce(alpha[:, slot, :, :], chosen[:, slot, :, :, :].rearrange("p j r h -> p j h r"),
                                    AX_X, ALU.add).then_inc(step, 1)
                    dve.wait_ge(step, i * 3 + 2)
                    v.tensor_tensor(both[:, slot, :, :], alpha[:, slot, :, :], rows[:, slot, :, 0:H1],
                                    ALU.add).then_inc(step, 1)
                    dve.wait_ge(step, i * 3 + 3)
                    wait(dve, stored[slot], 16 * turn)
                    v.scalar_tensor_tensor(result[:, slot, :, 0:H1], both[:, slot, :, :], SLOPE, both[:, slot, :, :],
                                           ALU.mult, ALU.max).then_inc(result_ready, 1)

                pipelined(dve, GROUPS, [choose, score])
    tables1.close()

    segment_softmax(alphas, ZROW, H1, H1 + Y_SEG, False)

    with ExitStack() as st:
        total = sb(st, [P, WINDOWS, D])

        def features_of(i):
            return by_dst_rows[bass.ds(i, 1), :, :, 0:D].rearrange("a p j c -> (a p) j c")

        weighted_sums(total, features_of, alphas_g, ZROW, H1, H1 + Y_DLO1, window2)
        added = sem("added")
        stored = sem("stored")
        with nc.Block() as block:

            @block.vector
            def _(dve):
                nc.vector.tensor_tensor(total[:, :, :], total[:, :, :], x_sb[:, :, :], ALU.add).then_inc(added, 1)

            @block.sync
            def _(sp):
                sp.wait_ge(added, 1)
                sp.dma_start(out[0:(WINDOWS - 1) * P, :].rearrange("(w p) d -> p w d", p=P),
                             total[:, 0:WINDOWS - 1, :]).then_inc(stored, 16)
                sp.dma_start(out[(WINDOWS - 1) * P:N, :], total[0:LAST, WINDOWS - 1, :]).then_inc(stored, 16)
                sp.wait_ge(stored, 32)
    whole.close()


_INS = ["x", "src", "dst", "edge_attr_128", "edge_type_4", "L0_gnn_Wq", "L0_gnn_Wk", "L0_gnn_Wv", "L0_gnn_Wek",
        "L0_gnn_Wev", "L0_gnn_Wexp", "L0_gnn_Wout", "L0_gnn_bout", "L1_gnn_W", "L1_gnn_attn"]


def kernel(**inputs):
    import numpy as _np
    import concourse.bacc as _bacc
    from concourse import mybir as _mybir
    from concourse.bass_utils import run_bass_kernel_spmd as _run

    nc = _bacc.Bacc("TRN2", target_bir_lowering=False, num_devices=1)
    arrays, args = {}, []
    for name in _INS:
        a = _np.ascontiguousarray(inputs[name])
        arrays[f"in_{name}"] = a
        args.append(nc.dram_tensor(f"in_{name}", a.shape, _mybir.dt.from_np(a.dtype), kind="ExternalInput").ap())
    shape = inputs["x"].shape
    args.append(nc.dram_tensor("out", shape, _mybir.dt.float32, kind="ExternalOutput").ap())
    gnn_kernel(nc, *args)
    r = _run(nc, [arrays], core_ids=[0])
    return r.results[0]["out"]
```

```python
from contextlib import ExitStack

import concourse.bass as bass
from concourse import mybir

F32 = mybir.dt.float32
BF16 = mybir.dt.bfloat16
I32 = mybir.dt.int32
ALU = mybir.AluOpType
ACT = mybir.ActivationFunctionType
AX_X = mybir.AxisListType.X

P = 128
SLOTS = 6
DEEP = 9
WIDE = 12
BANKS = 3
TILES = 4
GROUP = TILES * P
LOW = -3.0e38
NOWHERE = 4.0e6

SRC1, LO1, DST, HI2, KEY1, DLO1, TYPE, SEG2 = range(8)
SPOT2 = HI2
TAGS = 8


def pipelined(engine, count, stages, slots=SLOTS, start=0, newest_last=False):
    in_turn = [stage if isinstance(stage, tuple) else (s, stage) for s, stage in enumerate(stages)]
    depth = max(s for s, _ in in_turn)
    if newest_last:
        in_turn.reverse()
    first = start + slots + depth
    rounds = max((count - first - 1) // slots, 0)

    def written_out(t):
        for s, stage in in_turn:
            if stage and start <= t - s < count:
                stage(t - s, (t - s) % slots, (t - s) // slots)

    for t in range(start, min(first, count + depth)):
        written_out(t)
    if rounds:
        with engine.Fori(0, rounds) as k:
            for u in range(slots):
                for s, stage in in_turn:
                    if stage:
                        at = first + u - s
                        stage(k * slots + at, at % slots, k + at // slots)
    for t in range(first + rounds * slots, count + depth):
        written_out(t)


def wait(engine, semaphore, value):
    if isinstance(value, int) and value <= 0:
        return
    engine.wait_ge(semaphore, value)


def gnn_kernel(nc, x, src, dst, edge_attr, edge_type, Wq, Wk, Wv, Wek, Wev, Wexp, Wout, bout, W_rel, attn, out):
    N, D = x.shape
    E = src.shape[0]
    H0, HE = Wexp.shape
    R, H1, two_hd = attn.shape
    HD1 = two_hd // 2
    SCALE = float(D // H0) ** -0.5
    EPS = 1e-5
    SLOPE = 0.2
    WINDOWS = -(-N // P)
    LAST = N - (WINDOWS - 1) * P
    COLS = -(-E // (P * TILES)) * TILES
    TAIL = E - (P - 1) * COLS
    IN_GROUPS = COLS // TILES
    FULL = TAIL // TILES
    GROUPS = (E + WINDOWS * (GROUP - 1)) // GROUP
    NPOS = GROUPS * GROUP
    RUN = NPOS // P
    KV = 2 * D
    PAY = D + TAGS
    SROW = HE + TAGS
    FEAT = D + H1
    YROW = FEAT + 4
    ZROW = H1 + 4
    KEYS2 = WINDOWS * R
    assert HE == 8 and R == 4 and H1 == 4 and D == P and YROW == PAY

    kv_table = nc.dram_tensor("kv_table", [WINDOWS * P, KV], F32).ap()
    by_src = nc.dram_tensor("by_src", [NPOS + WINDOWS * GROUP, PAY], F32).ap()
    values = nc.dram_tensor("values", [NPOS, D], F32).ap()
    scores = nc.dram_tensor("scores", [NPOS, SROW], F32).ap()
    by_dst = nc.dram_tensor("by_dst", [NPOS + WINDOWS * GROUP, YROW], F32).ap()
    alphas = nc.dram_tensor("alphas", [NPOS, ZROW], F32).ap()

    names = [0]

    def sb(stack, shape, dtype=F32):
        names[0] += 1
        return stack.enter_context(nc.sbuf_tensor(f"sb{names[0]}", list(shape), dtype))

    def ps(stack, shape, dtype=F32):
        names[0] += 1
        return stack.enter_context(nc.psum_tensor(f"ps{names[0]}", list(shape), dtype))

    spent = []

    def sem(name):
        names[0] += 1
        spent.append(nc.alloc_semaphore(f"{name}_{names[0]}"))
        return spent[-1]

    def fresh_semaphores():
        nc.clear_and_free_semaphores(list(spent))
        nc.all_engine_barrier()
        spent.clear()

    def gpsimd_dma_sem(name):
        names[0] += 1
        return nc.alloc_semaphore(f"{name}_{names[0]}")

    whole = ExitStack()
    x_sb = sb(whole, [P, WINDOWS, D])
    ident = sb(whole, [P, P])
    ident_bf = sb(whole, [P, P], BF16)
    ones = sb(whole, [P, P])
    before = sb(whole, [P, P])
    after = sb(whole, [P, P])
    count1 = sb(whole, [P, P])
    count8 = sb(whole, [P, P, 2 * TILES], BF16)
    count4 = sb(whole, [P, KEYS2, TILES], BF16)
    count0 = sb(whole, [P, R])
    row1 = sb(whole, [P, R])
    base1 = sb(whole, [P, WINDOWS])
    base2 = sb(whole, [P, KEYS2])
    window1 = sb(whole, [1, GROUPS], I32)
    window2 = sb(whole, [1, GROUPS], I32)
    clear1 = sb(whole, [1, 2 * WINDOWS], I32)
    clear2 = sb(whole, [1, 2 * WINDOWS], I32)
    zeros = sb(whole, [P, TILES * PAY])

    with ExitStack() as st:
        cleared = sem("cleared")
        loaded = sem("loaded")
        made = sem("made")
        with nc.Block() as block:

            @block.vector
            def _(dve):
                nc.vector.memset(x_sb[:, :, :], 0.0).then_inc(cleared, 1)
                nc.vector.memset(ones[:, :], 1.0)

            @block.sync
            def _(sp):
                sp.wait_ge(cleared, 1)
                sp.dma_start(x_sb[:, 0:WINDOWS - 1, :],
                             x[0:(WINDOWS - 1) * P, :].rearrange("(w p) d -> p w d", p=P)).then_inc(loaded, 16)
                sp.dma_start(x_sb[0:LAST, WINDOWS - 1, :], x[(WINDOWS - 1) * P:N, :]).then_inc(loaded, 16)
                sp.wait_ge(loaded, 32)

            @block.gpsimd
            def _(pool):
                for t in (ident, ident_bf, before, after):
                    pool.memset(t[:, :], 0.0).then_inc(made, 1)
                pool.wait_ge(made, 4)
                for t in (ident, ident_bf):
                    pool.affine_select(out=t[:, :], in_=t[:, :], compare_op=ALU.not_equal, fill=1.0, base=0,
                                       pattern=[[-1, P]], channel_multiplier=1)
                pool.affine_select(out=before[:, :], in_=before[:, :], compare_op=ALU.is_ge, fill=1.0, base=0,
                                   pattern=[[-1, P]], channel_multiplier=1)
                pool.affine_select(out=after[:, :], in_=after[:, :], compare_op=ALU.is_ge, fill=1.0, base=0,
                                   pattern=[[1, P]], channel_multiplier=-1)
                for t, pattern, base, step in ((count1, [[1, P]], 1, 0), (count8, [[1, P], [0, 2 * TILES]], 1, 0),
                                               (count4, [[1, KEYS2], [0, TILES]], 1, 0),
                                               (count0, [[1, R]], 0, 0), (row1, [[P, R]], 1, 1)):
                    pool.iota(t[:, :, :] if t in (count8, count4) else t[:, :], pattern=pattern, base=base, channel_multiplier=step,
                              allow_small_or_imprecise_dtypes=True)

    tables0 = ExitStack()
    q_sb = sb(tables0, [P, WINDOWS, D])
    edges = ExitStack()
    tags = sb(edges, [P, COLS, TAGS])
    hi1 = sb(edges, [P, COLS])

    with ExitStack() as st:
        ids = [sb(st, [P, COLS], I32) for _ in range(3)]
        part = sb(st, [P, COLS], I32)
        scratch = sb(st, [P, COLS])
        cleared = sem("cleared")
        loaded = sem("loaded")
        step = sem("step")
        with nc.Block() as block:

            @block.gpsimd
            def _(pool):
                for t in ids:
                    pool.memset(t[:, :], -1).then_inc(cleared, 1)

            @block.sync
            def _(sp):
                sp.wait_ge(cleared, 3)
                for t, given in zip(ids, (src, dst, edge_type)):
                    sp.dma_start(t[0:P - 1, :],
                                 given[0:(P - 1) * COLS].rearrange("(p c) -> p c", p=P - 1)).then_inc(loaded, 16)
                    sp.dma_start(t[P - 1:P, 0:TAIL],
                                 given[(P - 1) * COLS:E].rearrange("(p c) -> p c", p=1)).then_inc(loaded, 16)

            @block.vector
            def _(dve):
                done = [0]

                def then(instruction):
                    done[0] += 1
                    instruction.then_inc(step, 1)
                    dve.wait_ge(step, done[0])

                s, d, t = (i[:, :] for i in ids)
                v = nc.vector

                def col(c):
                    return tags[:, :, c]

                dve.wait_ge(loaded, 6 * 16)
                v.tensor_scalar(col(SRC1), s, 1.0, None, ALU.add)
                v.tensor_copy(col(DST), d)
                v.tensor_copy(col(TYPE), t)
                then(v.tensor_scalar(part[:, :], s, P - 1, None, ALU.bitwise_and))
                then(v.tensor_scalar(col(LO1), part[:, :], 1.0, None, ALU.add))
                then(v.tensor_scalar(part[:, :], s, 7, None, ALU.arith_shift_right))
                then(v.tensor_scalar(hi1[:, :], part[:, :], 1.0, None, ALU.add))
                v.scalar_tensor_tensor(col(KEY1), col(TYPE), float(P), col(LO1), ALU.mult, ALU.add)
                then(v.tensor_scalar(part[:, :], d, P - 1, None, ALU.bitwise_and))
                then(v.tensor_scalar(col(DLO1), part[:, :], 1.0, None, ALU.add))
                then(v.tensor_scalar(part[:, :], d, 7, None, ALU.arith_shift_right))
                then(v.tensor_scalar(scratch[:, :], part[:, :], float(R), 1.0, ALU.mult, ALU.add))
                then(v.tensor_tensor(col(HI2), scratch[:, :], col(TYPE), ALU.add))
                then(v.tensor_scalar(scratch[:, :], d, float(R), 1.0, ALU.mult, ALU.add))
                then(v.tensor_tensor(col(SEG2), scratch[:, :], col(TYPE), ALU.add))

    def layernorm_relu_input(hn):
        with ExitStack() as st:
            square = sb(st, [P, WINDOWS, D])
            stat = sb(st, [P, WINDOWS])
            spread = sb(st, [P, WINDOWS])
            eps = sb(st, [P, 1])
            step = sem("step")
            summed = sem("summed")
            rooted = sem("rooted")
            over = stat[:, :].unsqueeze(2).to_broadcast([P, WINDOWS, D])
            with nc.Block() as block:

                @block.vector
                def _(dve):
                    done = [0]

                    def then(instruction):
                        done[0] += 1
                        instruction.then_inc(step, 1)
                        dve.wait_ge(step, done[0])

                    v = nc.vector
                    v.memset(eps[:, :], EPS)
                    then(v.tensor_reduce(stat[:, :], x_sb[:, :, :], AX_X, ALU.add))
                    then(v.tensor_scalar(stat[:, :], stat[:, :], 1.0 / D, None, ALU.mult))
                    then(v.tensor_tensor(hn[:, :, :], x_sb[:, :, :], over, ALU.subtract))
                    then(v.tensor_tensor(square[:, :, :], hn[:, :, :], hn[:, :, :], ALU.mult))
                    v.tensor_reduce(spread[:, :], square[:, :, :], AX_X, ALU.add).then_inc(summed, 1)
                    dve.wait_ge(rooted, 1)
                    then(v.reciprocal(stat[:, :], spread[:, :]))
                    v.tensor_tensor(hn[:, :, :], hn[:, :, :], over, ALU.mult)

                @block.scalar
                def _(act):
                    act.wait_ge(summed, 1)
                    nc.scalar.activation(spread[:, :], spread[:, :], ACT.Sqrt, bias=eps[:, 0:1],
                                         scale=1.0 / D).then_inc(rooted, 1)

    with ExitStack() as st:
        hn = sb(st, [P, WINDOWS, D])
        layernorm_relu_input(hn)
        w_qkv = sb(st, [P, 3, D])
        h = sb(st, [P, SLOTS, D])
        h_t = sb(st, [P, SLOTS, P])
        kv = sb(st, [P, SLOTS, KV])
        ps_t = [ps(st, [P, 512]) for _ in range(BANKS)]
        ps_qkv = [ps(st, [P, 512]) for _ in range(BANKS)]
        weights = sem("weights")
        relu_done = sem("relu_done")
        turned = sem("turned")
        turned_copied = sem("turned_copied")
        projected = sem("projected")
        taken = sem("taken")
        stored = [sem(f"stored{s}") for s in range(SLOTS)]
        with nc.Block() as block:

            @block.sync
            def _(sp):
                for n, w in enumerate((Wq, Wk, Wv)):
                    sp.dma_start(w_qkv[:, n, :], w).then_inc(weights, 16)

                def store(i, slot, turn):
                    sp.wait_ge(taken, i + 1)
                    sp.dma_start(kv_table[bass.ds(i * P, P), :], kv[:, slot, :]).then_inc(stored[slot], 16)

                pipelined(sp, WINDOWS, [store])
                for s in range(SLOTS):
                    sp.wait_ge(stored[s], 16 * len(range(s, WINDOWS, SLOTS)))

            @block.scalar
            def _(act):
                def rectify(i, slot, turn):
                    wait(act, turned, i - SLOTS + 1)
                    nc.scalar.activation(h[:, slot, :], hn[:, bass.ds(i, 1), :].rearrange("p a d -> p (a d)"),
                                         ACT.Relu).then_inc(relu_done, 1)

                def copy_turned(i, slot, turn):
                    act.wait_ge(turned, i + 1)
                    wait(act, projected, i - SLOTS + 1)
                    nc.scalar.activation(h_t[:, slot, :], ps_t[slot % BANKS][:, 0:P], ACT.Copy).then_inc(turned_copied, 1)

                pipelined(act, WINDOWS, [rectify, copy_turned])

            @block.tensor
            def _(pe):
                pe.wait_ge(weights, 3 * 16)

                def turn_h(i, slot, turn):
                    pe.wait_ge(relu_done, i + 1)
                    wait(pe, turned_copied, i - BANKS + 1)
                    nc.tensor.transpose(ps_t[slot % BANKS][:, 0:P], h[:, slot, :], ident[:, :]).then_inc(turned, 1)

                def project(i, slot, turn):
                    pe.wait_ge(turned_copied, i + 1)
                    wait(pe, taken, i - BANKS + 1)
                    nc.tensor.matmul(ps_qkv[slot % BANKS][:, 0:3 * D], h_t[:, slot, :],
                                     w_qkv[:, :, :].rearrange("p a d -> p (a d)"), start=True,
                                     stop=True).then_inc(projected, 1)

                pipelined(pe, WINDOWS, [turn_h, project])

            @block.vector
            def _(dve):
                def take(i, slot, turn):
                    dve.wait_ge(projected, i + 1)
                    wait(dve, stored[slot], 16 * turn)
                    nc.vector.tensor_copy(q_sb[:, bass.ds(i, 1), :].rearrange("p a d -> p (a d)"),
                                          ps_qkv[slot % BANKS][:, 0:D])
                    nc.vector.tensor_copy(kv[:, slot, :], ps_qkv[slot % BANKS][:, D:3 * D]).then_inc(taken, 1)

                pipelined(dve, WINDOWS, [take])

    def one_hots_of(low, high1, high2, hot, hot_hi):
        nc.vector.tensor_tensor(hot, low.rearrange("p n j -> p (n j)").unsqueeze(1).to_broadcast([P, P, 2 * TILES]),
                                count8[:, :, :], ALU.is_equal)
        nc.vector.tensor_tensor(hot_hi[0], high1.unsqueeze(1).to_broadcast([P, WINDOWS, TILES]),
                                count4[:, 0:WINDOWS, :], ALU.is_equal)
        return nc.vector.tensor_tensor(hot_hi[1], high2.unsqueeze(1).to_broadcast([P, KEYS2, TILES]),
                                       count4[:, :, :], ALU.is_equal)

    counts = ExitStack()
    count_src = sb(counts, [P, WINDOWS])
    count_dst = sb(counts, [P, KEYS2])
    with ExitStack() as st:
        hot = sb(st, [P, SLOTS, P, 2 * TILES], BF16)
        hot_hi = [sb(st, [P, SLOTS, n, TILES], BF16) for n in (WINDOWS, KEYS2)]
        low = sb(st, [P, SLOTS, 2, TILES], BF16)
        high = sb(st, [P, SLOTS, 2, TILES], BF16)
        ps_count = [ps(st, [P, n]) for n in (WINDOWS, KEYS2)]
        copied = sem("copied")
        hot_ready = sem("hot_ready")
        counted = sem("counted")
        with nc.Block() as block:

            @block.scalar
            def _(act):
                def copy_keys(i, slot, turn):
                    here = bass.ds(i * TILES, TILES)
                    wait(act, hot_ready, i - SLOTS + 1)
                    nc.scalar.activation(low[:, slot, 0, :], tags[:, here, LO1], ACT.Copy)
                    nc.scalar.activation(low[:, slot, 1, :], tags[:, here, DLO1], ACT.Copy)
                    nc.scalar.activation(high[:, slot, 0, :], hi1[:, here], ACT.Copy)
                    nc.scalar.activation(high[:, slot, 1, :], tags[:, here, HI2], ACT.Copy).then_inc(copied, 1)

                pipelined(act, IN_GROUPS, [copy_keys])

            @block.vector
            def _(dve):
                def one_hots(i, slot, turn):
                    dve.wait_ge(copied, i + 1)
                    wait(dve, counted, i - SLOTS + 1)
                    last = one_hots_of(low[:, slot, :, :], high[:, slot, 0, :], high[:, slot, 1, :],
                                       hot[:, slot, :, :], [hot_hi[n][:, slot, :, :] for n in range(2)])
                    last.then_inc(hot_ready, 1)

                pipelined(dve, IN_GROUPS, [one_hots])
                dve.wait_ge(counted, IN_GROUPS)
                nc.vector.tensor_copy(count_src[:, :], ps_count[0][:, :])
                nc.vector.tensor_copy(count_dst[:, :], ps_count[1][:, :])

            @block.tensor
            def _(pe):
                def count(i, slot, turn):
                    pe.wait_ge(hot_ready, i + 1)
                    for n in range(2):
                        for j in range(TILES):
                            first = isinstance(i, int) and i == 0 and j == 0
                            final = isinstance(i, int) and i == IN_GROUPS - 1 and j == TILES - 1
                            last = nc.tensor.matmul(ps_count[n][:, :], hot[:, slot, :, n * TILES + j],
                                                    hot_hi[n][:, slot, :, j], start=first, stop=final)
                    last.then_inc(counted, 1)

                pipelined(pe, IN_GROUPS, [count])

    with ExitStack() as st:
        total = sb(st, [P, KEYS2])
        column = sb(st, [P, KEYS2])
        edges_of = sb(st, [P, WINDOWS])
        whole_groups = sb(st, [P, WINDOWS], I32)
        groups_of = sb(st, [P, WINDOWS])
        groups_upto = sb(st, [P, WINDOWS])
        zero_w = sb(st, [P, WINDOWS])
        group_no = sb(st, [1, GROUPS])
        window_f = [sb(st, [1, GROUPS]) for _ in range(2)]
        ps_total = ps(st, [P, 512])
        ps_before = ps(st, [P, 512])
        numbered = sem("numbered")
        summed = sem("summed")
        used = sem("used")
        step = sem("step")
        sorts = ((count_src, WINDOWS, 1, base1, window1, clear1), (count_dst, KEYS2, R, base2, window2, clear2))
        with nc.Block() as block:

            @block.gpsimd
            def _(pool):
                pool.iota(group_no[:, :], pattern=[[1, GROUPS]], base=0, channel_multiplier=0,
                          allow_small_or_imprecise_dtypes=True).then_inc(numbered, 1)

            @block.tensor
            def _(pe):
                for n, (count, keys, _, _, _, _) in enumerate(sorts):
                    wait(pe, used, n)
                    nc.tensor.matmul(ps_total[:, 0:keys], ones[:, :], count[:, :], start=True, stop=True)
                    nc.tensor.matmul(ps_before[:, 0:keys], before[:, :], count[:, :], start=True,
                                     stop=True).then_inc(summed, 1)

            @block.vector
            def _(dve):
                done = [0]

                def then(instruction):
                    done[0] += 1
                    instruction.then_inc(step, 1)
                    dve.wait_ge(step, done[0])

                v = nc.vector
                dve.wait_ge(numbered, 1)
                v.memset(zero_w[:, :], 0.0)
                for n, (_, keys, per, base, window, clear) in enumerate(sorts):
                    dve.wait_ge(summed, n + 1)
                    then(v.tensor_copy(total[:, 0:keys], ps_total[:, 0:keys]))
                    by_window = total[:, 0:keys].rearrange("p (w k) -> p w k", k=per)
                    then(v.tensor_reduce(edges_of[:, :], by_window, AX_X, ALU.add))
                    then(v.tensor_scalar(whole_groups[:, :], edges_of[:, :], float(GROUP - 1), None, ALU.add))
                    then(v.tensor_scalar(whole_groups[:, :], whole_groups[:, :], GROUP.bit_length() - 1, None,
                                         ALU.arith_shift_right))
                    then(v.tensor_copy(groups_of[:, :], whole_groups[:, :]))
                    then(v.tensor_tensor_scan(groups_upto[:, :], groups_of[:, :], zero_w[:, :], 0.0, ALU.add, ALU.add))
                    offset = column[:, 0:keys].rearrange("p (w k) -> p w k", k=per)
                    then(v.tensor_tensor(offset[:, :, 0], groups_upto[:, :], groups_of[:, :], ALU.subtract))
                    then(v.tensor_scalar(offset[:, :, 0], offset[:, :, 0], float(GROUP), None, ALU.mult))
                    for k in range(1, per):
                        then(v.tensor_tensor(offset[:, :, k], offset[:, :, k - 1], by_window[:, :, k - 1], ALU.add))
                    then(v.tensor_tensor(base[:, :], column[:, 0:keys], ps_before[:, 0:keys], ALU.add))
                    v.tensor_scalar(clear[:, 0:WINDOWS], groups_upto[0:1, :], 1.0, 0.0, ALU.subtract, ALU.max)
                    v.tensor_scalar(clear[:, WINDOWS:2 * WINDOWS], group_no[:, 0:WINDOWS],
                                    groups_upto[0:1, WINDOWS - 1:WINDOWS], None, ALU.add)
                    then(v.memset(window_f[0][:, :], 0.0))
                    for w in range(WINDOWS - 1):
                        then(v.scalar_tensor_tensor(window_f[(w + 1) % 2][:, :], group_no[:, :],
                                                    groups_upto[0:1, w:w + 1], window_f[w % 2][:, :],
                                                    ALU.is_ge, ALU.add))
                    v.tensor_copy(window[:, :], window_f[(WINDOWS - 1) % 2][:, :]).then_inc(used, 1)
                    dve.wait_ge(used, n + 1)
    counts.close()

    def window_of(engine, window, i):
        return engine.value_load(window[0:1, bass.ds(i, 1)], min_val=0, max_val=WINDOWS - 1)

    PARTS = 48
    cut = (P - 1) // 16 * 16
    spare = TAIL % TILES
    assert spare > 0
    edges_of_partition = edge_attr[0:(P - 1) * COLS, :].rearrange("(p c) d -> p c d", p=P - 1)

    def load_edges(sp, rows, loaded, scattered):
        def whole_group(i, slot, turn):
            wait(sp, scattered[slot], 64 * turn)
            sp.dma_start(rows[:, slot, :, 0:D],
                         bass.AP(edge_attr.tensor, i * (TILES * D), [[COLS * D, P], [D, TILES], [1, D]])
                         ).then_inc(loaded[slot], PARTS)

        def cut_group(i, slot, turn):
            wait(sp, scattered[slot], 64 * turn)
            here = bass.ds(i * TILES, TILES)
            sp.dma_start(rows[0:cut, slot, :, 0:D], edges_of_partition[0:cut, here, :]).then_inc(loaded[slot], 16)
            sp.dma_start(rows[cut:P - 1, slot, :, 0:D],
                         edges_of_partition[cut:P - 1, here, :]).then_inc(loaded[slot], 16)
            sp.dma_start(rows[P - 1:P, slot, 0:spare, 0:D],
                         edge_attr[E - spare:E, :].unsqueeze(0)).then_inc(loaded[slot], 16)

        pipelined(sp, FULL, [whole_group])
        pipelined(sp, IN_GROUPS, [cut_group], start=FULL)

    def clear_groups(engine, groups, which, part, cleared):
        with engine.Fori(part * WINDOWS, (part + 1) * WINDOWS) as i:
            g = engine.value_load(which[0:1, bass.ds(i, 1)], min_val=0, max_val=GROUPS + WINDOWS - 1)
            engine.dma_start(groups[bass.ds(g, 1), :, :].rearrange("a p c -> (a p) c"), zeros[:, :]).then_inc(cleared, 16)

    by_src_g = by_src.rearrange("(g p j) c -> g p (j c)", p=P, j=TILES)
    by_dst_g = by_dst.rearrange("(g p j) c -> g p (j c)", p=P, j=TILES)
    zeroed = sem("zeroed")
    cleared_src = [sem(f"cleared_src{part}") for part in range(2)]
    with nc.Block() as block:

        @block.gpsimd
        def _(pool):
            pool.memset(zeros[:, :], 0.0).then_inc(zeroed, 1)

        @block.sync
        def _(sp):
            sp.wait_ge(zeroed, 1)
            clear_groups(sp, by_src_g, clear1, 0, cleared_src[0])
            sp.wait_ge(cleared_src[0], WINDOWS * 16)

        @block.scalar
        def _(act):
            act.wait_ge(zeroed, 1)
            clear_groups(act, by_src_g, clear1, 1, cleared_src[1])
            act.wait_ge(cleared_src[1], WINDOWS * 16)

    HALF = TILES // 2
    BANK = HALF * (KEYS2 + WINDOWS)

    def table_part(tables, n, j):
        at = (j % HALF) * KEYS2 if n else HALF * KEYS2 + (j % HALF) * WINDOWS
        return tables[:, j // HALF, at:at + (KEYS2 if n else WINDOWS)]

    with ExitStack() as st:
        base = sb(st, [P, BANK])
        rows = sb(st, [P, SLOTS, TILES, PAY])
        low = sb(st, [P, SLOTS, 2, TILES], BF16)
        high = sb(st, [P, SLOTS, 2, TILES], BF16)
        hot = sb(st, [P, SLOTS, P, 2 * TILES], BF16)
        hot_hi = [sb(st, [P, SLOTS, n, TILES], BF16) for n in (WINDOWS, KEYS2)]
        hot_t = sb(st, [P, BANKS, 2, TILES, P])
        table = sb(st, [P, BANKS, 2, BANK])
        same = sb(st, [P, 2, TILES, P])
        picked = [sb(st, [P, TILES, n]) for n in (WINDOWS, KEYS2)]
        rank = sb(st, [P, SLOTS, 2, TILES])
        found = sb(st, [P, SLOTS, 2, TILES])
        spot = sb(st, [P, SLOTS, 2, TILES])
        nowhere = sb(st, [P, SLOTS, TILES])
        index = sb(st, [P, SLOTS, TILES], I32)
        ps_keys = [ps(st, [P, TILES, P]) for _ in range(2)]
        ps_hot_t = ps(st, [P, 2, TILES, P], BF16)
        ps_table = ps(st, [P, 2, 512])
        ps_found = ps(st, [P, 2, 512])
        loaded = [sem(f"loaded{s}") for s in range(SLOTS)]
        scattered = [gpsimd_dma_sem(f"scattered{s}") for s in range(SLOTS)]
        base_copied = sem("base_copied")
        tagged = sem("tagged")
        hot_ready = sem("hot_ready")
        keys_spread = sem("keys_spread")
        ranked = sem("ranked")
        hot_turned = sem("hot_turned")
        hot_copied = sem("hot_copied")
        table_grown = sem("table_grown")
        table_copied = sem("table_copied")
        looked_up = sem("looked_up")
        found_read = sem("found_read")
        spot_ready = sem("spot_ready")
        index_ready = sem("index_ready")
        begun = sem("begun")
        with nc.Block() as block:

            @block.sync
            def _(sp):
                load_edges(sp, rows, loaded, scattered)

            @block.gpsimd
            def _(pool):
                def scatter(i, slot, turn):
                    pool.wait_ge(index_ready, i + 1)
                    pool.wait_ge(loaded[slot], PARTS * (turn + 1))
                    pool.sem_inc(begun, 1)
                    for j in range(TILES):
                        pool.indirect_dma_start(
                            by_src[:, :], bass.IndirectOffsetOnAxis(ap=index[:, slot, j:j + 1], axis=0),
                            rows[:, slot, j, :], None, bounds_check=NPOS - 1,
                            oob_is_err=False).then_inc(scattered[slot], 16)

                pipelined(pool, IN_GROUPS, [scatter])
                for s in range(SLOTS):
                    pool.wait_ge(scattered[s], 64 * len(range(s, IN_GROUPS, SLOTS)))

            @block.scalar
            def _(act):
                a = nc.scalar
                def tag(i, slot, turn):
                    wait(act, scattered[slot], 64 * turn)
                    a.activation(rows[:, slot, :, D:PAY], tags[:, bass.ds(i * TILES, TILES), :], ACT.Copy)
                    a.activation(low[:, slot, 0, :], tags[:, bass.ds(i * TILES, TILES), LO1], ACT.Copy)
                    a.activation(low[:, slot, 1, :], tags[:, bass.ds(i * TILES, TILES), DLO1], ACT.Copy)
                    a.activation(high[:, slot, 1, :], tags[:, bass.ds(i * TILES, TILES), HI2], ACT.Copy)
                    a.activation(high[:, slot, 0, :], hi1[:, bass.ds(i * TILES, TILES)], ACT.Copy).then_inc(tagged, 1)

                def copies(i, slot, turn):
                    act.wait_ge(hot_turned, i + 1)
                    wait(act, looked_up, i - BANKS + 1)
                    a.activation(hot_t[:, slot % BANKS, :, :, :], ps_hot_t[:, :, :, :], ACT.Copy).then_inc(hot_copied, 1)
                    act.wait_ge(table_grown, i + 1)
                    a.activation(table[:, slot % BANKS, :, :], ps_table[:, :, 0:BANK], ACT.Copy).then_inc(table_copied, 1)

                pipelined(act, IN_GROUPS, [tag, None, copies])

            @block.tensor
            def _(pe):
                pe.wait_ge(base_copied, 1)
                for half in range(2):
                    nc.tensor.matmul(ps_table[:, half, 0:BANK], ident[:, :], base[:, :], start=True, stop=True)

                def grow(n, j, slot, k):
                    return nc.tensor.matmul(table_part(ps_table, n, j), hot[:, slot, :, n * TILES + k],
                                            hot_hi[n][:, slot, :, k], start=False, stop=True, skip_group_check=True)

                def turn_and_grow(i, slot, turn):
                    pe.wait_ge(hot_ready, i + 1)
                    wait(pe, hot_copied, i)
                    for n in range(2):
                        for j in range(TILES):
                            last = nc.tensor.transpose(ps_hot_t[:, n, j, :], hot[:, slot, :, n * TILES + j],
                                                       ident_bf[:, :])
                    last.then_inc(hot_turned, 1)
                    wait(pe, table_copied, i)
                    for n in range(2):
                        for j in range(TILES):
                            if not (isinstance(i, int) and i == 0):
                                for k in range(j, TILES):
                                    last = grow(n, j, (slot - 1) % SLOTS, k)
                            for k in range(j):
                                last = grow(n, j, slot, k)
                    last.then_inc(table_grown, 1)

                def look_up(i, slot, turn):
                    pe.wait_ge(hot_copied, i + 1)
                    pe.wait_ge(table_copied, i + 1)
                    wait(pe, found_read, i)
                    for n in range(2):
                        for j in range(TILES):
                            last = nc.tensor.matmul(table_part(ps_found, n, j), hot_t[:, slot % BANKS, n, j, :],
                                                    table_part(table[:, slot % BANKS, :, :], n, j),
                                                    start=True, stop=True)
                    last.then_inc(looked_up, 1)

                def spread(i, slot, turn):
                    pe.wait_ge(tagged, i + 1)
                    wait(pe, ranked, i)
                    for n, key in enumerate((SRC1, SEG2)):
                        for j in range(TILES):
                            last = nc.tensor.transpose(ps_keys[n][:, j, :],
                                                       rows[:, slot, j, D + key:D + key + 1].to_broadcast([P, P]),
                                                       ident[:, :])
                    last.then_inc(keys_spread, 1)

                def grow_and_spread(i, slot, turn):
                    turn_and_grow(i, slot, turn)
                    spread(i, slot, turn)

                pipelined(pe, IN_GROUPS, [grow_and_spread, None, look_up], newest_last=True)

            @block.vector
            def _(dve):
                v = nc.vector
                for half in range(HALF):
                    v.tensor_copy(base[:, half * KEYS2:(half + 1) * KEYS2], base2[:, :])
                for half in range(HALF):
                    last = v.tensor_copy(base[:, HALF * KEYS2 + half * WINDOWS:HALF * KEYS2 + (half + 1) * WINDOWS],
                                         base1[:, :])
                last.then_inc(base_copied, 1)

                def one_hots(i, slot, turn):
                    dve.wait_ge(tagged, i + 1)
                    wait(dve, table_grown, i - SLOTS + 2)
                    last = one_hots_of(low[:, slot, :, :], high[:, slot, 0, :], high[:, slot, 1, :],
                                       hot[:, slot, :, :], [hot_hi[n][:, slot, :, :] for n in range(2)])
                    last.then_inc(hot_ready, 1)

                def ranks_of(n, key, i, slot):
                    for j in range(TILES):
                        last = v.scalar_tensor_tensor(same[:, n, j, :], ps_keys[n][:, j, :],
                                                      rows[:, slot, j, D + key:D + key + 1], after[:, :],
                                                      ALU.is_equal, ALU.mult,
                                                      accum_out=rank[:, slot, n, j:j + 1])
                    return last

                def ranks_by_source(i, slot, turn):
                    dve.wait_ge(keys_spread, i + 1)
                    v.tensor_scalar(nowhere[:, slot, :], high[:, slot, 0, :], 0.5, NOWHERE, ALU.is_lt, ALU.mult)
                    ranks_of(0, SRC1, i, slot)

                def ranks_by_target(i, slot, turn):
                    ranks_of(1, SEG2, i, slot).then_inc(ranked, 1)

                def find(i, slot, turn):
                    dve.wait_ge(looked_up, i + 1)
                    for n, width in enumerate((WINDOWS, KEYS2)):
                        for j in range(TILES):
                            last = v.scalar_tensor_tensor(picked[n][:, j, :], table_part(ps_found, n, j), 1.0,
                                                          hot_hi[n][:, slot, :, j], ALU.mult, ALU.mult,
                                                          accum_out=found[:, slot, n, j:j + 1])
                    last.then_inc(found_read, 1)

                def add_ranks(i, slot, turn):
                    dve.wait_ge(found_read, i + 1)
                    dve.wait_ge(ranked, i + 1)
                    v.tensor_tensor(spot[:, slot, :, :], found[:, slot, :, :], rank[:, slot, :, :],
                                    ALU.add).then_inc(spot_ready, 1)

                def keep_positions(i, slot, turn):
                    dve.wait_ge(spot_ready, i + 1)
                    v.tensor_scalar(rows[:, slot, :, D + SPOT2], spot[:, slot, 1, :], 1.0, None, ALU.add)
                    v.tensor_tensor(index[:, slot, :], spot[:, slot, 0, :], nowhere[:, slot, :],
                                    ALU.add).then_inc(index_ready, 1)

                pipelined(dve, IN_GROUPS, [(0, one_hots), (3, add_ranks), (1, ranks_by_source), (3, keep_positions),
                                           (1, ranks_by_target), (2, find)])
    edges.close()

    values_g = values.rearrange("(g p j) c -> g p j c", p=P, j=TILES)
    scores_g = scores.rearrange("(g p j) c -> g p (j c)", p=P, j=TILES)
    with ExitStack() as st:
        w_e = sb(st, [P, 2, D])
        w_exp = sb(st, [P, HE])
        rows = sb(st, [P, DEEP, TILES, PAY])
        target = sb(st, [P, DEEP, TILES], I32)
        kv = sb(st, [P, DEEP, TILES, KV])
        edge_t = sb(st, [P, BANKS, GROUP])
        pick = sb(st, [P, BANKS, GROUP])
        product = sb(st, [P, BANKS, TILES, D])
        product_t = sb(st, [P, BANKS, GROUP])
        scored = sb(st, [P, DEEP, TILES, SROW])
        ps_edge_t = ps(st, [P, GROUP])
        source = sb(st, [P, DEEP, TILES], BF16)
        ps_pick = ps(st, [P, GROUP], BF16)
        ps_kv = ps(st, [P, TILES, KV])
        ps_q = ps(st, [P, TILES, D])
        ps_product_t = ps(st, [P, GROUP])
        ps_score = ps(st, [P, TILES, HE])
        weights = sem("weights")
        loaded = [sem(f"loaded{s}") for s in range(DEEP)]
        fetched = [gpsimd_dma_sem(f"fetched{s}") for s in range(DEEP)]
        stored = [sem(f"stored{s}") for s in range(DEEP)]
        source_ready = sem("source_ready")
        target_ready = sem("target_ready")
        begun = sem("begun")
        tags_copied = sem("tags_copied")
        edge_turned = sem("edge_turned")
        edge_copied = sem("edge_copied")
        pick_spread = sem("pick_spread")
        pick_ready = sem("pick_ready")
        edge_projected = sem("edge_projected")
        q_fetched = sem("q_fetched")
        kv_ready = sem("kv_ready")
        product_ready = sem("product_ready")
        product_turned = sem("product_turned")
        product_copied = sem("product_copied")
        score_ready = sem("score_ready")
        score_copied = sem("score_copied")
        with nc.Block() as block:

            @block.sync
            def _(sp):
                sp.dma_start(w_e[:, 0, :], Wek).then_inc(weights, 16)
                sp.dma_start(w_e[:, 1, :], Wev).then_inc(weights, 16)
                for h in range(H0):
                    width = D // H0
                    sp.dma_start(w_exp[h * width:(h + 1) * width, :],
                                 Wexp[h:h + 1, :].to_broadcast([width, HE])).then_inc(weights, 16)

                def load(i, slot, turn):
                    wait(sp, edge_turned, i - DEEP + 1)
                    wait(sp, source_ready, i - DEEP + 1)
                    wait(sp, tags_copied, i - DEEP + 1)
                    sp.dma_start(rows[:, slot, :, :].rearrange("p j c -> p (j c)"),
                                 by_src_g[bass.ds(i, 1), :, :].rearrange("a p c -> (a p) c")
                                 ).then_inc(loaded[slot], 16)

                pipelined(sp, GROUPS, [load], DEEP)

            @block.gpsimd
            def _(pool):
                def fetch(i, slot, turn):
                    pool.wait_ge(target_ready, i + 1)
                    wait(pool, stored[slot], 32 * turn)
                    wait(pool, product_ready, i - DEEP + 1)
                    pool.sem_inc(begun, 1)
                    for j in range(TILES):
                        pool.indirect_dma_start(
                            kv[:, slot, j, :], None, kv_table[:, :],
                            bass.IndirectOffsetOnAxis(ap=target[:, slot, j:j + 1], axis=0)).then_inc(fetched[slot], 16)

                pipelined(pool, GROUPS, [fetch], DEEP)

            @block.scalar
            def _(act):
                a = nc.scalar

                def early(i, slot, turn):
                    act.wait_ge(loaded[slot], 16 * (turn + 1))
                    wait(act, fetched[slot], 64 * turn)
                    a.activation(target[:, slot, :], rows[:, slot, :, D + DST], ACT.Copy).then_inc(target_ready, 1)
                    wait(act, pick_spread, i - DEEP + 1)
                    a.activation(source[:, slot, :], rows[:, slot, :, D + LO1], ACT.Copy).then_inc(source_ready, 1)
                    wait(act, stored[slot], 32 * turn)
                    a.activation(scored[:, slot, :, HE:SROW], rows[:, slot, :, D:PAY], ACT.Copy).then_inc(tags_copied, 1)

                def copy_edges(i, slot, turn):
                    act.wait_ge(edge_turned, i + 1)
                    wait(act, edge_projected, i - BANKS + 1)
                    a.activation(edge_t[:, slot % BANKS, :], ps_edge_t[:, :], ACT.Copy).then_inc(edge_copied, 1)

                def late(i, slot, turn):
                    act.wait_ge(product_turned, i + 1)
                    wait(act, score_ready, i - BANKS + 1)
                    a.activation(product_t[:, slot % BANKS, :], ps_product_t[:, :], ACT.Copy).then_inc(product_copied, 1)

                def keep_scores(i, slot, turn):
                    act.wait_ge(score_ready, i + 1)
                    a.activation(scored[:, slot, :, 0:HE], ps_score[:, :, :], ACT.Copy,
                                 scale=SCALE).then_inc(score_copied, 1)

                def store(i, slot, turn):
                    act.wait_ge(kv_ready, i + 1)
                    act.dma_start(values_g[bass.ds(i, 1), :, :, :].rearrange("a p j c -> (a p) j c"),
                                 kv[:, slot, :, D:KV]).then_inc(stored[slot], 16)
                    act.wait_ge(score_copied, i + 1)
                    act.wait_ge(tags_copied, i + 1)
                    act.dma_start(scores_g[bass.ds(i, 1), :, :].rearrange("a p c -> (a p) c"),
                                 scored[:, slot, :, :].rearrange("p j c -> p (j c)")).then_inc(stored[slot], 16)

                pipelined(act, GROUPS, [early, None, None, copy_edges, None, late, keep_scores, store], DEEP)
                for s in range(DEEP):
                    act.wait_ge(stored[s], 32 * len(range(s, GROUPS, DEEP)))

            @block.vector
            def _(dve):
                v = nc.vector

                def choose(i, slot, turn):
                    dve.wait_ge(pick_spread, i + 1)
                    wait(dve, q_fetched, i - BANKS + 1)
                    v.tensor_scalar(pick[:, slot % BANKS, :], ps_pick[:, :], row1[:, 0:1], None,
                                    ALU.is_equal).then_inc(pick_ready, 1)

                def combine(i, slot, turn):
                    dve.wait_ge(fetched[slot], 64 * (turn + 1))
                    dve.wait_ge(edge_projected, i + 1)
                    v.tensor_tensor(kv[:, slot, :, :], kv[:, slot, :, :], ps_kv[:, :, :], ALU.add).then_inc(kv_ready, 1)
                    dve.wait_ge(kv_ready, i + 1)
                    dve.wait_ge(q_fetched, i + 1)
                    wait(dve, product_turned, i - BANKS + 1)
                    v.tensor_tensor(product[:, slot % BANKS, :, :], kv[:, slot, :, 0:D], ps_q[:, :, :],
                                    ALU.mult).then_inc(product_ready, 1)

                pipelined(dve, GROUPS, [choose, combine], DEEP)

            @block.tensor
            def _(pe):
                pe.wait_ge(weights, (2 + H0) * 16)

                def turn_edges(i, slot, turn):
                    pe.wait_ge(source_ready, i + 1)
                    wait(pe, pick_ready, i)
                    for j in range(TILES):
                        last = nc.tensor.transpose(ps_pick[:, j * P:(j + 1) * P],
                                                   source[:, slot, j:j + 1].to_broadcast([P, P]), ident_bf[:, :])
                    last.then_inc(pick_spread, 1)
                    wait(pe, edge_copied, i)
                    for j in range(TILES):
                        last = nc.tensor.transpose(ps_edge_t[:, j * P:(j + 1) * P], rows[:, slot, j, 0:D], ident[:, :])
                    last.then_inc(edge_turned, 1)

                def project(i, slot, turn):
                    w = window_of(pe, window1, i)
                    pe.wait_ge(edge_copied, i + 1)
                    wait(pe, kv_ready, i)
                    for j in range(TILES):
                        last = nc.tensor.matmul(ps_kv[:, j, :], edge_t[:, slot % BANKS, j * P:(j + 1) * P],
                                                w_e[:, :, :].rearrange("p a d -> p (a d)"), start=True, stop=True)
                    last.then_inc(edge_projected, 1)
                    pe.wait_ge(pick_ready, i + 1)
                    wait(pe, product_ready, i)
                    for j in range(TILES):
                        last = nc.tensor.matmul(ps_q[:, j, :], pick[:, slot % BANKS, j * P:(j + 1) * P],
                                                q_sb[:, bass.ds(w, 1), :].rearrange("p a d -> p (a d)"),
                                                start=True, stop=True)
                    last.then_inc(q_fetched, 1)

                def turn_product(i, slot, turn):
                    pe.wait_ge(product_ready, i + 1)
                    wait(pe, product_copied, i)
                    for j in range(TILES):
                        last = nc.tensor.transpose(ps_product_t[:, j * P:(j + 1) * P], product[:, slot % BANKS, j, :],
                                                   ident[:, :])
                    last.then_inc(product_turned, 1)

                def score(i, slot, turn):
                    pe.wait_ge(product_copied, i + 1)
                    wait(pe, score_copied, i)
                    for j in range(TILES):
                        last = nc.tensor.matmul(ps_score[:, j, :], product_t[:, slot % BANKS, j * P:(j + 1) * P],
                                                w_exp[:, :], start=True, stop=True)
                    last.then_inc(score_ready, 1)

                pipelined(pe, GROUPS, [turn_edges, project, turn_product, score], DEEP)
    tables0.close()

    def segment_softmax(table, width, heads, seg, self_minus, beside=None):
        in_runs = table.rearrange("(p t) c -> p t c", p=P)
        flat = table.rearrange("(p t) c -> p (t c)", p=P)
        with ExitStack() as st:
            data = sb(st, [P, RUN, width])
            seg_before = sb(st, [P, 1])
            seg_behind = sb(st, [P, 1])
            same_f = sb(st, [P, RUN])
            same_b = sb(st, [P, RUN])
            low_f = sb(st, [P, RUN])
            low_b = sb(st, [P, RUN])
            fwd = [sb(st, [P, RUN]) for _ in range(2)]
            bwd = (sb(st, [P, RUN]), low_b, low_f)
            ends = sb(st, [P, 4, heads])
            ends_t = sb(st, [heads, 4, P])
            through = sb(st, [P, 4])
            chain = sb(st, [heads, 2, P])
            carry_t = sb(st, [heads, 2, P])
            carry = sb(st, [P, 2, heads])
            ps_ends = ps(st, [heads, 4, P])
            ps_carry = ps(st, [P, 2, heads])
            filled = sem("filled")
            loaded = sem("loaded")
            stored = sem("stored")
            step = sem("step")
            pool_step = sem("pool_step")
            ends_ready = sem("ends_ready")
            ends_turned = sem("ends_turned")
            carry_ready = sem("carry_ready")
            carry_turned = sem("carry_turned")
            peak_ready = sem("peak_ready")
            shifted = sem("shifted")
            scanned = sem("scanned")
            total_ready = sem("total_ready")
            inverse_ready = sem("inverse_ready")
            self_ready = sem("self_ready")
            exponent = sem("exponent")
            weights_ready = sem("weights_ready")
            with nc.Block() as block:

                @block.sync
                def _(sp):
                    sp.dma_start(data[:, :, :].rearrange("p t c -> p (t c)"), flat).then_inc(loaded, 16)
                    sp.wait_ge(filled, 1)
                    sp.dma_start(seg_before[1:P, :], in_runs[0:P - 1, RUN - 1, seg:seg + 1],
                                 allow_slow_non_contiguous=True).then_inc(loaded, 16)
                    sp.dma_start(seg_behind[0:P - 1, :], in_runs[1:P, 0, seg:seg + 1],
                                 allow_slow_non_contiguous=True).then_inc(loaded, 16)
                    sp.wait_ge(weights_ready, heads)
                    sp.dma_start(flat, data[:, :, :].rearrange("p t c -> p (t c)")).then_inc(stored, 16)
                    sp.wait_ge(stored, 16)

                @block.gpsimd
                def _(pool):
                    done = [0]

                    def then(instruction):
                        done[0] += 1
                        instruction.then_inc(pool_step, 1)
                        pool.wait_ge(pool_step, done[0])

                    def add_up(h):
                        pool.wait_ge(scanned, h + 1)
                        then(pool.tensor_tensor(bwd[h % 3][:, :], bwd[h % 3][:, :], data[:, :, h], ALU.subtract))
                        pool.tensor_tensor(fwd[h % 2][:, :], fwd[h % 2][:, :], bwd[h % 3][:, :],
                                           ALU.add).then_inc(total_ready, 1)

                    for h in range(heads):
                        pool.wait_ge(peak_ready, h + 1)
                        pool.tensor_tensor(data[:, :, h], data[:, :, h], fwd[h % 2][:, :],
                                           ALU.subtract).then_inc(shifted, 1)
                    add_up(0)
                    if self_minus:
                        pool.wait_ge(self_ready, 1)
                    for h in range(heads):
                        if h + 1 < heads:
                            add_up(h + 1)
                        pool.wait_ge(inverse_ready, h + 1)
                        last = pool.tensor_tensor(data[:, :, h], data[:, :, h], bwd[h % 3][:, :], ALU.mult)
                        if self_minus:
                            then(last)
                            last = pool.tensor_tensor(data[:, :, h], data[:, :, HE + DST], data[:, :, h], ALU.subtract)
                        last.then_inc(weights_ready, 1)

                @block.tensor
                def _(pe):
                    for n in range(2):
                        pe.wait_ge(ends_ready, n + 1)
                        for k in range(4):
                            last = nc.tensor.transpose(ps_ends[:, k, :], ends[:, k, :], ident[:, :])
                        last.then_inc(ends_turned, 1)
                        pe.wait_ge(carry_ready, n + 1)
                        for k in range(2):
                            last = nc.tensor.transpose(ps_carry[:, k, :], carry_t[:, k, :], ident[0:heads, 0:heads])
                        last.then_inc(carry_turned, 1)

                @block.scalar
                def _(act):
                    if beside:
                        beside(act)
                    for h in range(heads):
                        act.wait_ge(shifted, h + 1)
                        nc.scalar.activation(data[:, :, h], data[:, :, h], ACT.Exp).then_inc(exponent, 1)

                @block.vector
                def _(dve):
                    done = [0]

                    def then(instruction):
                        done[0] += 1
                        instruction.then_inc(step, 1)
                        dve.wait_ge(step, done[0])

                    v = nc.vector
                    v.memset(seg_before[:, :], -1.0)
                    v.memset(seg_behind[:, :], -1.0).then_inc(filled, 1)
                    dve.wait_ge(loaded, 3 * 16)
                    segs = data[:, :, seg]
                    v.tensor_tensor(same_f[:, 0:1], segs[:, 0:1], seg_before[:, :], ALU.is_equal)
                    v.tensor_tensor(same_f[:, 1:RUN], segs[:, 1:RUN], segs[:, 0:RUN - 1], ALU.is_equal)
                    v.tensor_tensor(same_b[:, RUN - 1:RUN], segs[:, RUN - 1:RUN], seg_behind[:, :], ALU.is_equal)
                    then(v.tensor_tensor(same_b[:, 0:RUN - 1], segs[:, 0:RUN - 1], segs[:, 1:RUN], ALU.is_equal))
                    v.tensor_scalar(low_f[:, :], same_f[:, :], 1.0, -LOW, ALU.subtract, ALU.mult)
                    v.tensor_scalar(low_b[:, :], same_b[:, :], 1.0, -LOW, ALU.subtract, ALU.mult)
                    v.tensor_reduce(through[:, 2:3], same_f[:, :], AX_X, ALU.min)
                    then(v.tensor_reduce(through[:, 3:4], same_b[:, :], AX_X, ALU.min))
                    then(v.tensor_scalar(through[:, 0:2], through[:, 2:4], 1.0, -LOW, ALU.subtract, ALU.mult))

                    def scans(n, h, flags, start, op, first, second):
                        v.tensor_tensor_scan(fwd[h % 2][:, :], flags[0][:, :], data[:, :, h], first, op[0], op[1])
                        return v.tensor_tensor_scan(bwd[h % 3 * n][:, ::-1], flags[1][:, ::-1], data[:, ::-1, h], second,
                                                    op[0], op[1])

                    def invert(h):
                        dve.wait_ge(total_ready, h + 1)
                        v.reciprocal(bwd[h % 3][:, :], fwd[h % 2][:, :]).then_inc(inverse_ready, 1)

                    for n, (flags, start, op) in enumerate((
                            ((low_f, low_b), LOW, (ALU.add, ALU.max)),
                            ((same_f, same_b), 0.0, (ALU.mult, ALU.add)))):
                        if n == 1:
                            dve.wait_ge(shifted, heads)
                        for h in range(heads):
                            if n == 1:
                                dve.wait_ge(exponent, h + 1)
                            then(scans(n, h, flags, start, op, start, start))
                            v.tensor_copy(ends[:, 0, h:h + 1], fwd[h % 2][:, RUN - 1:RUN])
                            then(v.tensor_copy(ends[:, 1, h:h + 1], bwd[h % 3 * n][:, 0:1]))
                        v.tensor_copy(ends[:, 2, :], through[:, 2 * n:2 * n + 1].to_broadcast([P, heads]))
                        v.tensor_copy(ends[:, 3, :], through[:, 2 * n + 1:2 * n + 2].to_broadcast([P, heads])
                                      ).then_inc(ends_ready, 1)
                        dve.wait_ge(ends_turned, n + 1)
                        then(v.tensor_copy(ends_t[:, :, :], ps_ends[:, :, :]))
                        v.tensor_tensor_scan(chain[:, 0, :], ends_t[:, 2, :], ends_t[:, 0, :], start, op[0], op[1])
                        v.tensor_tensor_scan(chain[:, 1, ::-1], ends_t[:, 3, ::-1], ends_t[:, 1, ::-1], start,
                                             op[0], op[1])
                        then(v.memset(carry_t[:, :, :], start))
                        v.tensor_copy(carry_t[:, 0, 1:P], chain[:, 0, 0:P - 1])
                        v.tensor_copy(carry_t[:, 1, 0:P - 1], chain[:, 1, 1:P]).then_inc(carry_ready, 1)
                        dve.wait_ge(carry_turned, n + 1)
                        then(v.tensor_copy(carry[:, :, :], ps_carry[:, :, :]))
                        if n == 1 and self_minus:
                            v.scalar_tensor_tensor(data[:, :, HE + DST], data[:, :, HE + DST], 1.0,
                                                   data[:, :, HE + SRC1], ALU.add,
                                                   ALU.is_equal).then_inc(self_ready, 1)
                        for h in range(heads):
                            if n == 0:
                                wait(dve, shifted, h - 1)
                                wait(dve, peak_ready, h)
                                then(scans(n, h, flags, start, op, carry[:, 0, h:h + 1], carry[:, 1, h:h + 1]))
                                v.tensor_tensor(fwd[h % 2][:, :], fwd[h % 2][:, :], bwd[0][:, :],
                                                ALU.max).then_inc(peak_ready, 1)
                            else:
                                wait(dve, inverse_ready, h - 1)
                                wait(dve, weights_ready, h - 2)
                                scans(n, h, flags, start, op, carry[:, 0, h:h + 1],
                                      carry[:, 1, h:h + 1]).then_inc(scanned, 1)
                                if h >= 1:
                                    invert(h - 1)
                    invert(heads - 1)

    def weighted_sums(total, value_groups, weight_groups, width, heads, lo, window):
        with ExitStack() as st:
            value = sb(st, [P, WIDE, TILES, D])
            weight = sb(st, [P, WIDE, TILES * width])
            pick = sb(st, [P, SLOTS, TILES, P])
            ps_sum = [ps(st, [P, 512]) for _ in range(BANKS)]
            loaded = [sem(f"loaded{s}") for s in range(WIDE)]
            weights_loaded = [sem(f"weights_loaded{s}") for s in range(WIDE // 2)]
            weighted = sem("weighted")
            pick_ready = sem("pick_ready")
            summed = sem("summed")
            added = sem("added")
            cleared = sem("cleared")
            with nc.Block() as block:

                @block.sync
                def _(sp):
                    def load(i, slot, turn):
                        wait(sp, summed, i - WIDE + 1)
                        sp.dma_start(value[:, slot, :, :], value_groups(i)).then_inc(loaded[slot], 16)

                    pipelined(sp, GROUPS, [load], WIDE)

                @block.scalar
                def _(act):
                    def load_weights(i, slot, turn):
                        if slot % 2 == 0:
                            pair = 1 if isinstance(i, int) and i == GROUPS - 1 else 2
                            wait(act, summed, i - WIDE + 2)
                            act.dma_start(weight[:, slot:slot + pair, :],
                                          weight_groups[bass.ds(i, pair), :, :].rearrange("a p c -> p a c")
                                          ).then_inc(weights_loaded[slot // 2], 16)

                    pipelined(act, GROUPS, [load_weights], WIDE)

                @block.gpsimd
                def _(pool):
                    def weigh(i, slot, turn):
                        pool.wait_ge(loaded[slot], 16 * (turn + 1))
                        pool.wait_ge(weights_loaded[slot // 2], 16 * (turn + 1))
                        by_head = value[:, slot, :, :].rearrange("p j (h d) -> p j h d", h=heads)
                        pool.tensor_tensor(by_head, by_head,
                                           weight[:, slot, :].rearrange("p (j c) -> p j c", j=TILES)[:, :, 0:heads].unsqueeze(3)
                                           .to_broadcast([P, TILES, heads, D // heads]), ALU.mult).then_inc(weighted, 1)

                    pipelined(pool, GROUPS, [weigh], WIDE)

                @block.vector
                def _(dve):
                    v = nc.vector
                    v.memset(total[:, :, :], 0.0).then_inc(cleared, 1)
                    dve.wait_ge(cleared, 1)

                    def choose(i, slot, turn):
                        dve.wait_ge(weights_loaded[slot // 2], 16 * (turn + 1))
                        wait(dve, summed, i - SLOTS + 1)
                        v.tensor_tensor(pick[:, slot % SLOTS, :, :],
                                        weight[:, slot, :].rearrange("p (j c) -> p j c", j=TILES)[:, :, lo:lo + 1]
                                        .to_broadcast([P, TILES, P]),
                                        count1[:, :].unsqueeze(1).to_broadcast([P, TILES, P]),
                                        ALU.is_equal).then_inc(pick_ready, 1)

                    def add(i, slot, turn):
                        w = window_of(dve, window, i)
                        dve.wait_ge(summed, i + 1)
                        wait(dve, added, i)
                        here = total[:, bass.ds(w, 1), :].rearrange("p a d -> p (a d)")
                        v.tensor_tensor(here, here, ps_sum[slot % BANKS][:, 0:D], ALU.add).then_inc(added, 1)

                    pipelined(dve, GROUPS, [choose, None, add], WIDE)

                @block.tensor
                def _(pe):
                    def add_up(i, slot, turn):
                        pe.wait_ge(weighted, i + 1)
                        pe.wait_ge(pick_ready, i + 1)
                        wait(pe, added, i - BANKS + 1)
                        for j in range(TILES):
                            last = nc.tensor.matmul(ps_sum[slot % BANKS][:, 0:D], pick[:, slot % SLOTS, j, :], value[:, slot, j, :],
                                                    start=(j == 0), stop=(j == TILES - 1))
                        last.then_inc(summed, 1)

                    pipelined(pe, GROUPS, [add_up], WIDE)

    fresh_semaphores()
    cleared_dst = sem("cleared_dst")

    def clear_by_dst(act):
        for part in range(2):
            clear_groups(act, by_dst_g, clear2, part, cleared_dst)
        act.wait_ge(cleared_dst, 2 * WINDOWS * 16)

    segment_softmax(scores, SROW, HE, HE + SRC1, True, clear_by_dst)

    tables1 = ExitStack()
    features = sb(tables1, [P, WINDOWS, R, FEAT])
    dst_score = sb(tables1, [P, WINDOWS, R * H1])
    with ExitStack() as sums:
        total = sb(sums, [P, WINDOWS, D])

        def values_of(i):
            return values_g[bass.ds(i, 1), :, :, :].rearrange("a p j c -> (a p) j c")

        weighted_sums(total, values_of, scores_g, SROW, HE, HE + LO1, window1)

        with ExitStack() as st:
            w_out = sb(st, [P, D])
            b_out = sb(st, [1, D])
            rows = sb(st, [P, SLOTS, D])
            rows_t = sb(st, [P, SLOTS, P])
            ps_t = [ps(st, [P, 512]) for _ in range(BANKS)]
            ps_out = [ps(st, [P, 512]) for _ in range(BANKS)]
            weights = sem("weights")
            copied = sem("copied")
            turned = sem("turned")
            turned_copied = sem("turned_copied")
            projected = sem("projected")
            added = sem("added")
            with nc.Block() as block:

                @block.sync
                def _(sp):
                    sp.dma_start(w_out[:, :], Wout).then_inc(weights, 16)
                    sp.dma_start(b_out[:, :], bout.rearrange("(a d) -> a d", a=1)).then_inc(weights, 16)

                @block.scalar
                def _(act):
                    def copy_rows(i, slot, turn):
                        wait(act, turned, i - SLOTS + 1)
                        nc.scalar.activation(rows[:, slot, :], total[:, bass.ds(i, 1), :].rearrange("p a d -> p (a d)"),
                                             ACT.Copy).then_inc(copied, 1)

                    def copy_turned(i, slot, turn):
                        act.wait_ge(turned, i + 1)
                        wait(act, projected, i - SLOTS + 1)
                        nc.scalar.activation(rows_t[:, slot, :], ps_t[slot % BANKS][:, 0:P], ACT.Copy).then_inc(turned_copied, 1)

                    pipelined(act, WINDOWS, [copy_rows, copy_turned])

                @block.tensor
                def _(pe):
                    pe.wait_ge(weights, 32)

                    def turn_rows(i, slot, turn):
                        pe.wait_ge(copied, i + 1)
                        wait(pe, turned_copied, i - BANKS + 1)
                        nc.tensor.transpose(ps_t[slot % BANKS][:, 0:P], rows[:, slot, :], ident[:, :]).then_inc(turned, 1)

                    def project(i, slot, turn):
                        pe.wait_ge(turned_copied, i + 1)
                        wait(pe, added, i - BANKS + 1)
                        nc.tensor.matmul(ps_out[slot % BANKS][:, 0:D], rows_t[:, slot, :], w_out[:, :], start=True, stop=False)
                        nc.tensor.matmul(ps_out[slot % BANKS][:, 0:D], ones[0:1, :], b_out[:, :], start=False,
                                         stop=True).then_inc(projected, 1)

                    pipelined(pe, WINDOWS, [turn_rows, project])

                @block.vector
                def _(dve):
                    def add(i, slot, turn):
                        dve.wait_ge(projected, i + 1)
                        here = x_sb[:, bass.ds(i, 1), :].rearrange("p a d -> p (a d)")
                        nc.vector.tensor_tensor(here, here, ps_out[slot % BANKS][:, 0:D], ALU.add).then_inc(added, 1)

                    pipelined(dve, WINDOWS, [add])

    with ExitStack() as st:
        hn = sb(st, [P, WINDOWS, D])
        layernorm_relu_input(hn)
        w_all = sb(st, [P, R, D])
        attn_all = sb(st, [P, R * H1, 2 * HD1])
        h = sb(st, [P, SLOTS, D])
        h_t = sb(st, [P, SLOTS, P])
        product = sb(st, [P, 2, R * H1, HD1])
        ps_t = [ps(st, [P, 512]) for _ in range(BANKS)]
        ps_feat = [ps(st, [P, R, D]) for _ in range(BANKS)]
        weights = sem("weights")
        relu_done = sem("relu_done")
        turned = sem("turned")
        turned_copied = sem("turned_copied")
        projected = sem("projected")
        product_ready = sem("product_ready")
        scored = sem("scored")
        kept = sem("kept")
        with nc.Block() as block:

            @block.sync
            def _(sp):
                for r in range(R):
                    sp.dma_start(w_all[:, r, :], W_rel[r, :, :]).then_inc(weights, 16)
                sp.dma_start(attn_all[:, :, :].rearrange("p a b -> p (a b)"),
                             attn.rearrange("(o a) b c -> o (a b c)", o=1).to_broadcast([P, R * H1 * 2 * HD1])
                             ).then_inc(weights, 16)

            @block.scalar
            def _(act):
                def rectify(i, slot, turn):
                    wait(act, turned, i - SLOTS + 1)
                    nc.scalar.activation(h[:, slot, :], hn[:, bass.ds(i, 1), :].rearrange("p a d -> p (a d)"),
                                         ACT.Relu).then_inc(relu_done, 1)

                def copy_turned(i, slot, turn):
                    act.wait_ge(turned, i + 1)
                    wait(act, projected, i - SLOTS + 1)
                    nc.scalar.activation(h_t[:, slot, :], ps_t[slot % BANKS][:, 0:P], ACT.Copy).then_inc(turned_copied, 1)

                def keep(i, slot, turn):
                    act.wait_ge(projected, i + 1)
                    nc.scalar.activation(features[:, bass.ds(i, 1), :, 0:D].rearrange("p a r d -> p (a r) d"),
                                         ps_feat[slot % BANKS][:, :, :], ACT.Copy).then_inc(kept, 1)

                pipelined(act, WINDOWS, [rectify, copy_turned, keep])

            @block.tensor
            def _(pe):
                pe.wait_ge(weights, (R + 1) * 16)

                def turn_h(i, slot, turn):
                    pe.wait_ge(relu_done, i + 1)
                    wait(pe, turned_copied, i - BANKS + 1)
                    nc.tensor.transpose(ps_t[slot % BANKS][:, 0:P], h[:, slot, :], ident[:, :]).then_inc(turned, 1)

                def project(i, slot, turn):
                    pe.wait_ge(turned_copied, i + 1)
                    wait(pe, kept, i - BANKS + 1)
                    wait(pe, scored, i - BANKS + 1)
                    nc.tensor.matmul(ps_feat[slot % BANKS][:, :, :].rearrange("p r d -> p (r d)"), h_t[:, slot, :],
                                     w_all[:, :, :].rearrange("p r d -> p (r d)"), start=True,
                                     stop=True).then_inc(projected, 1)

                pipelined(pe, WINDOWS, [turn_h, project])

            @block.vector
            def _(dve):
                v = nc.vector
                dve.wait_ge(weights, (R + 1) * 16)

                def score(i, slot, turn):
                    dve.wait_ge(kept, i + 1)
                    wait(dve, scored, i)
                    feat = ps_feat[slot % BANKS][:, :, :].rearrange("p r (h d) -> p (r h) d", h=H1)
                    v.tensor_tensor(product[:, 0, :, :], feat, attn_all[:, :, 0:HD1], ALU.mult)
                    v.tensor_tensor(product[:, 1, :, :], feat, attn_all[:, :, HD1:2 * HD1],
                                    ALU.mult).then_inc(product_ready, 1)
                    dve.wait_ge(product_ready, i + 1)
                    v.tensor_reduce(features[:, bass.ds(i, 1), :, D:FEAT].rearrange("p a r h -> p (a r) h"),
                                    product[:, 0, :, :].rearrange("p (r h) d -> p r h d", h=H1), AX_X, ALU.add)
                    v.tensor_reduce(dst_score[:, bass.ds(i, 1), :].rearrange("p a c -> p (a c)"),
                                    product[:, 1, :, :], AX_X, ALU.add).then_inc(scored, 1)

                pipelined(dve, WINDOWS, [score])

    fresh_semaphores()

    with ExitStack() as st:
        tag_rows = sb(st, [P, SLOTS, TILES, SROW])
        sources = sb(st, [P, BANKS, GROUP])
        pick = sb(st, [P, 2, R, GROUP])
        rows = sb(st, [P, SLOTS, TILES, YROW])
        nowhere = sb(st, [P, SLOTS, TILES])
        index = sb(st, [P, SLOTS, TILES], I32)
        ps_pick = [ps(st, [P, GROUP]) for _ in range(2)]
        ps_feat = [ps(st, [P, TILES, 256]) for _ in range(2)]
        loaded = [sem(f"loaded{s}") for s in range(SLOTS)]
        scattered = [gpsimd_dma_sem(f"scattered{s}") for s in range(SLOTS)]
        sources_spread = sem("sources_spread")
        sources_copied = sem("sources_copied")
        pick_ready = sem("pick_ready")
        feat_ready = sem("feat_ready")
        tags_kept = sem("tags_kept")
        feat_kept = sem("feat_kept")
        nowhere_ready = sem("nowhere_ready")
        index_ready = sem("index_ready")
        begun = sem("begun")
        with nc.Block() as block:

            @block.sync
            def _(sp):
                def load(i, slot, turn):
                    wait(sp, tags_kept, i - SLOTS + 1)
                    wait(sp, index_ready, i - SLOTS + 1)
                    wait(sp, sources_spread, i - SLOTS + 1)
                    sp.dma_start(tag_rows[:, slot, :, :].rearrange("p j c -> p (j c)"),
                                 scores_g[bass.ds(i, 1), :, :].rearrange("a p c -> (a p) c")).then_inc(loaded[slot], 16)

                pipelined(sp, GROUPS, [load], SLOTS)

            @block.gpsimd
            def _(pool):
                def scatter(i, slot, turn):
                    pool.wait_ge(index_ready, i + 1)
                    pool.wait_ge(feat_kept, i + 1)
                    pool.sem_inc(begun, 1)
                    for j in range(TILES):
                        pool.indirect_dma_start(
                            by_dst[:, :], bass.IndirectOffsetOnAxis(ap=index[:, slot, j:j + 1], axis=0),
                            rows[:, slot, j, :], None, bounds_check=NPOS - 1,
                            oob_is_err=False).then_inc(scattered[slot], 16)

                pipelined(pool, GROUPS, [scatter])
                for s in range(SLOTS):
                    pool.wait_ge(scattered[s], 64 * len(range(s, GROUPS, SLOTS)))

            @block.tensor
            def _(pe):
                def spread(i, slot, turn):
                    pe.wait_ge(loaded[slot], 16 * (turn + 1))
                    wait(pe, sources_copied, i - 1)
                    for j in range(TILES):
                        last = nc.tensor.transpose(
                            ps_pick[slot % 2][:, j * P:(j + 1) * P],
                            tag_rows[:, slot, j, HE + KEY1:HE + KEY1 + 1].to_broadcast([P, P]), ident[:, :])
                    last.then_inc(sources_spread, 1)

                def fetch(i, slot, turn):
                    w = window_of(pe, window1, i)
                    pe.wait_ge(pick_ready, i + 1)
                    wait(pe, feat_kept, i - 1)
                    for j in range(TILES):
                        for t in range(R):
                            last = nc.tensor.matmul(ps_feat[slot % 2][:, j, 0:FEAT],
                                                    pick[:, slot % 2, t, j * P:(j + 1) * P],
                                                    features[:, bass.ds(w, 1), t, :].rearrange("p a c -> p (a c)"),
                                                    start=(t == 0), stop=(t == R - 1))
                    last.then_inc(feat_ready, 1)

                pipelined(pe, GROUPS, [spread, None, fetch])

            @block.scalar
            def _(act):
                def keep_tags(i, slot, turn):
                    act.wait_ge(loaded[slot], 16 * (turn + 1))
                    wait(act, scattered[slot], 64 * turn)
                    nc.scalar.activation(rows[:, slot, :, FEAT:YROW], tag_rows[:, slot, :, SROW - 4:SROW],
                                         ACT.Copy).then_inc(tags_kept, 1)
                    act.wait_ge(sources_spread, i + 1)
                    wait(act, pick_ready, i - BANKS + 1)
                    nc.scalar.activation(sources[:, slot % BANKS, :], ps_pick[slot % 2][:, :],
                                         ACT.Copy).then_inc(sources_copied, 1)

                def keep_features(i, slot, turn):
                    act.wait_ge(feat_ready, i + 1)
                    nc.scalar.activation(rows[:, slot, :, 0:FEAT], ps_feat[slot % 2][:, :, 0:FEAT],
                                         ACT.Copy).then_inc(feat_kept, 1)

                pipelined(act, GROUPS, [keep_tags, None, keep_features])

            @block.vector
            def _(dve):
                v = nc.vector

                def choose(i, slot, turn):
                    dve.wait_ge(sources_copied, i + 1)
                    wait(dve, feat_ready, i - 1)
                    for t in range(R):
                        last = v.tensor_scalar(pick[:, slot % 2, t, :], sources[:, slot % BANKS, :], row1[:, t:t + 1],
                                               None, ALU.is_equal)
                    last.then_inc(pick_ready, 1)
                    spot = tag_rows[:, slot, :, HE + SPOT2]
                    wait(dve, scattered[slot], 64 * turn)
                    v.tensor_scalar(nowhere[:, slot, :], spot, 0.5, NOWHERE, ALU.is_lt, ALU.mult).then_inc(nowhere_ready, 1)
                    dve.wait_ge(nowhere_ready, i + 1)
                    v.scalar_tensor_tensor(index[:, slot, :], spot, -1.0, nowhere[:, slot, :], ALU.add,
                                           ALU.add).then_inc(index_ready, 1)

                pipelined(dve, GROUPS, [choose])

    by_dst_rows = by_dst.rearrange("(g p j) c -> g p j c", p=P, j=TILES)
    alphas_g = alphas.rearrange("(g p j) c -> g p (j c)", p=P, j=TILES)
    Y_DLO1, Y_TYPE, Y_SEG = 1, 2, 3
    with ExitStack() as st:
        rows = sb(st, [P, DEEP, TILES, H1 + 4])
        parts = sb(st, [P, WINDOWS, R, 3, H1], BF16)
        left = [sb(st, [P, WINDOWS, R, H1]) for _ in range(2)]
        target = sb(st, [P, DEEP, TILES], BF16)
        pick = sb(st, [P, DEEP, GROUP], BF16)
        type_hot = sb(st, [P, DEEP, TILES, R])
        chosen = sb(st, [P, DEEP, TILES, R, 3 * H1])
        alpha = sb(st, [P, DEEP, TILES, H1])
        both = sb(st, [P, DEEP, TILES, H1])
        result = sb(st, [P, DEEP, TILES, ZROW])
        ps_pick = [ps(st, [P, GROUP], BF16) for _ in range(BANKS)]
        ps_score = [ps(st, [P, TILES, R * 3 * H1]) for _ in range(BANKS)]
        parted = sem("parted")
        target_ready = sem("target_ready")
        loaded = [sem(f"loaded{s}") for s in range(DEEP)]
        stored = [sem(f"stored{s}") for s in range(DEEP)]
        pick_spread = sem("pick_spread")
        pick_ready = sem("pick_ready")
        dst_ready = sem("dst_ready")
        chosen_ready = sem("chosen_ready")
        alpha_ready = sem("alpha_ready")
        both_ready = sem("both_ready")
        result_ready = sem("result_ready")
        tags_kept = sem("tags_kept")
        with nc.Block() as block:

            @block.sync
            def _(sp):
                def load(i, slot, turn):
                    wait(sp, result_ready, i - DEEP + 1)
                    wait(sp, tags_kept, i - DEEP + 1)
                    sp.dma_start(rows[:, slot, :, :],
                                 by_dst_rows[bass.ds(i, 1), :, :, D:YROW].rearrange("a p j c -> (a p) j c")
                                 ).then_inc(loaded[slot], 16)

                pipelined(sp, GROUPS, [load], DEEP)

            @block.scalar
            def _(act):
                def keep_tags(i, slot, turn):
                    act.wait_ge(loaded[slot], 16 * (turn + 1))
                    wait(act, pick_spread, i - DEEP + 1)
                    nc.scalar.activation(target[:, slot, :], rows[:, slot, :, H1 + Y_DLO1],
                                         ACT.Copy).then_inc(target_ready, 1)
                    wait(act, stored[slot], 16 * turn)
                    nc.scalar.activation(result[:, slot, :, H1:ZROW], rows[:, slot, :, H1:H1 + 4],
                                         ACT.Copy).then_inc(tags_kept, 1)

                def store(i, slot, turn):
                    act.wait_ge(result_ready, i + 1)
                    act.wait_ge(tags_kept, i + 1)
                    act.dma_start(alphas_g[bass.ds(i, 1), :, :].rearrange("a p c -> (a p) c"),
                                 result[:, slot, :, :].rearrange("p j c -> p (j c)")).then_inc(stored[slot], 16)

                pipelined(act, GROUPS, [keep_tags] + [None] * 6 + [store], DEEP)
                for s in range(DEEP):
                    act.wait_ge(stored[s], 16 * len(range(s, GROUPS, DEEP)))

            @block.tensor
            def _(pe):
                pe.wait_ge(parted, 5)

                def spread(i, slot, turn):
                    pe.wait_ge(target_ready, i + 1)
                    wait(pe, pick_ready, i - BANKS + 1)
                    for j in range(TILES):
                        last = nc.tensor.transpose(ps_pick[slot % BANKS][:, j * P:(j + 1) * P],
                                                   target[:, slot, j:j + 1].to_broadcast([P, P]), ident_bf[:, :])
                    last.then_inc(pick_spread, 1)

                def fetch(i, slot, turn):
                    w = window_of(pe, window2, i)
                    pe.wait_ge(pick_ready, i + 1)
                    wait(pe, chosen_ready, i - BANKS + 1)
                    for j in range(TILES):
                        last = nc.tensor.matmul(ps_score[slot % BANKS][:, j, :], pick[:, slot, j * P:(j + 1) * P],
                                                parts[:, bass.ds(w, 1), :, :, :].rearrange("p a r s h -> p (a r s h)"),
                                                start=True, stop=True)
                    last.then_inc(dst_ready, 1)

                pipelined(pe, GROUPS, [spread, None, fetch], DEEP)

            @block.vector
            def _(dve):
                v = nc.vector

                whole_score = dst_score[:, :, :].rearrange("p w (r h) -> p w r h", r=R)
                for s, rest in enumerate((whole_score, left[0][:, :, :, :], left[1][:, :, :, :])):
                    v.tensor_copy(parts[:, :, :, s, :], rest).then_inc(parted, 1)
                    dve.wait_ge(parted, 2 * s + 1)
                    if s < 2:
                        v.tensor_tensor(left[s][:, :, :, :], rest, parts[:, :, :, s, :],
                                        ALU.subtract).then_inc(parted, 1)
                        dve.wait_ge(parted, 2 * s + 2)

                def choose(i, slot, turn):
                    dve.wait_ge(pick_spread, i + 1)
                    wait(dve, dst_ready, i - DEEP + 1)
                    v.tensor_tensor(type_hot[:, slot, :, :],
                                    rows[:, slot, :, H1 + Y_TYPE:H1 + Y_TYPE + 1].to_broadcast([P, TILES, R]),
                                    count0[:, :].unsqueeze(1).to_broadcast([P, TILES, R]), ALU.is_equal)
                    v.tensor_scalar(pick[:, slot, :], ps_pick[slot % BANKS][:, :], row1[:, 0:1], None,
                                    ALU.is_equal).then_inc(pick_ready, 1)

                def of_type(i, slot, turn):
                    dve.wait_ge(dst_ready, i + 1)
                    v.tensor_tensor(chosen[:, slot, :, :, :],
                                    ps_score[slot % BANKS][:, :, :].rearrange("p j (r c) -> p j r c", r=R),
                                    type_hot[:, slot, :, :].unsqueeze(3).to_broadcast([P, TILES, R, 3 * H1]),
                                    ALU.mult).then_inc(chosen_ready, 1)

                def over_types(i, slot, turn):
                    dve.wait_ge(chosen_ready, i + 1)
                    v.tensor_reduce(alpha[:, slot, :, :],
                                    chosen[:, slot, :, :, :].rearrange("p j r (s h) -> p j h (r s)", h=H1),
                                    AX_X, ALU.add).then_inc(alpha_ready, 1)

                def with_source(i, slot, turn):
                    dve.wait_ge(alpha_ready, i + 1)
                    v.tensor_tensor(both[:, slot, :, :], alpha[:, slot, :, :], rows[:, slot, :, 0:H1],
                                    ALU.add).then_inc(both_ready, 1)

                def leaky(i, slot, turn):
                    dve.wait_ge(both_ready, i + 1)
                    wait(dve, stored[slot], 16 * turn)
                    v.scalar_tensor_tensor(result[:, slot, :, 0:H1], both[:, slot, :, :], SLOPE, both[:, slot, :, :],
                                           ALU.mult, ALU.max).then_inc(result_ready, 1)

                pipelined(dve, GROUPS, [choose, None, of_type, over_types, with_source, leaky], DEEP)
    tables1.close()

    fresh_semaphores()
    segment_softmax(alphas, ZROW, H1, H1 + Y_SEG, False)

    with ExitStack() as st:
        total = sb(st, [P, WINDOWS, D])

        def features_of(i):
            return by_dst_rows[bass.ds(i, 1), :, :, 0:D].rearrange("a p j c -> (a p) j c")

        weighted_sums(total, features_of, alphas_g, ZROW, H1, H1 + Y_DLO1, window2)
        added = sem("added")
        stored = sem("stored")
        with nc.Block() as block:

            @block.vector
            def _(dve):
                nc.vector.tensor_tensor(total[:, :, :], total[:, :, :], x_sb[:, :, :], ALU.add).then_inc(added, 1)

            @block.sync
            def _(sp):
                sp.wait_ge(added, 1)
                sp.dma_start(out[0:(WINDOWS - 1) * P, :].rearrange("(w p) d -> p w d", p=P),
                             total[:, 0:WINDOWS - 1, :]).then_inc(stored, 16)
                sp.dma_start(out[(WINDOWS - 1) * P:N, :], total[0:LAST, WINDOWS - 1, :]).then_inc(stored, 16)
                sp.wait_ge(stored, 32)
    whole.close()


_INS = ["x", "src", "dst", "edge_attr_128", "edge_type_4", "L0_gnn_Wq", "L0_gnn_Wk", "L0_gnn_Wv", "L0_gnn_Wek",
        "L0_gnn_Wev", "L0_gnn_Wexp", "L0_gnn_Wout", "L0_gnn_bout", "L1_gnn_W", "L1_gnn_attn"]


def kernel(**inputs):
    import numpy as _np
    import concourse.bacc as _bacc
    from concourse import mybir as _mybir
    from concourse.bass_utils import run_bass_kernel_spmd as _run

    nc = _bacc.Bacc("TRN2", target_bir_lowering=False, num_devices=1)
    arrays, args = {}, []
    for name in _INS:
        a = _np.ascontiguousarray(inputs[name])
        arrays[f"in_{name}"] = a
        args.append(nc.dram_tensor(f"in_{name}", a.shape, _mybir.dt.from_np(a.dtype), kind="ExternalInput").ap())
    shape = inputs["x"].shape
    args.append(nc.dram_tensor("out", shape, _mybir.dt.float32, kind="ExternalOutput").ap())
    gnn_kernel(nc, *args)
    r = _run(nc, [arrays], core_ids=[0])
    return r.results[0]["out"]
```
